# Optimizing a Trainium2 kernel written in Bass

```python
import numpy as np
import jax
import jax.numpy as jnp

def _softmax(x, axis=-1):
    return jax.nn.softmax(x, axis=axis)

def _gelu(x):
    return jax.nn.gelu(x, approximate=True)

def _silu(x):
    return jax.nn.silu(x)

def _sigmoid(x):
    return jax.nn.sigmoid(x)

def _layernorm(x, axis=-1, eps=1e-05):
    m = jnp.mean(x, axis=axis, keepdims=True)
    v = jnp.var(x, axis=axis, keepdims=True)
    return (x - m) / jnp.sqrt(v + eps)

def _scatter_add(tgt, idx, src, axis=0):
    return tgt.at[idx].add(src)

def _segment_sum(src, seg, n):
    return jax.ops.segment_sum(src, seg, n)
kernel_name = 'mk_early_fusion_embed_d1_tok_img1024_r4_daff3d'

def setup_inputs(seed: int=0):
    np.random.seed(seed)
    _w = jnp.asarray

    def _rec_inputs():
        import jax
        import jax.numpy as jnp
        _rk = jax.random.key(seed)
        x = -0.000348323 + 0.999952 * jax.random.normal(jax.random.fold_in(_rk, 1), (16, 3, 96, 96), jnp.float32)
        x_txt = jax.random.randint(jax.random.fold_in(_rk, 51), (16, 128), 0, 8000, jnp.int32)
        return (x, x_txt)
    x, x_txt = _rec_inputs()

    def _L0_tok_setup():
        import jax, jax.numpy as jnp
        import numpy as np
        from jax import lax
        PATCH = 16
        key = jax.random.key(seed)
        k1, k2 = jax.random.split(key)
        B, C, IMG, HID = (32, 3, 96, 256)
        inputs = jax.random.normal(k1, (B, C, IMG, IMG), dtype=jnp.float32)
        flat = C * PATCH * PATCH
        W = jax.random.normal(k2, (flat, HID), dtype=jnp.float32) / np.sqrt(flat)
        return {'inputs': inputs, 'W': W}
    _L0_tok_all = _L0_tok_setup()
    _L0_tok_in = {k: v for k, v in _L0_tok_all.items() if k in ('W',)}
    del _L0_tok_all

    def _L0_txt_setup():
        import jax, jax.numpy as jnp
        import numpy as np
        NUM_VOCAB = 8000
        NUM_HIDDEN = 256
        W_INIT_STDEV = 0.02
        key = jax.random.key(seed)
        k_w, k_x = jax.random.split(key)
        w = jax.random.normal(k_w, (NUM_VOCAB, NUM_HIDDEN), dtype=jnp.float32) * W_INIT_STDEV
        x = jax.random.randint(k_x, (8, 512), 0, NUM_VOCAB, dtype=jnp.int64)
        return {'x': x, 'num_ctx': 0, 'w': w}
    _L0_txt_all = _L0_txt_setup()
    _L0_txt_in = {k: v for k, v in _L0_txt_all.items() if k in ('w',)}
    del _L0_txt_all

    def _L0_attn_setup():
        import jax, jax.numpy as jnp
        import numpy as np
        from math import sqrt
        N_HEAD = 16
        W_SCALE = 0.02

        def _reference_tuple_inner(x, W_dq, W_uq, W_dkv, W_uk, W_uv, W_o):
            B, T, C = x.shape
            nh = N_HEAD
            hs = C // nh
            n_kvl = W_dkv.shape[0]
            k_eff = (W_dq.T @ W_uq.T @ W_uk).reshape(nh, hs, n_kvl)
            v_eff = jnp.transpose((W_uv.T @ W_o.T).reshape(n_kvl, nh, hs), (1, 0, 2))
            c_kv = x @ W_dkv.T
            q = x @ W_dq.T @ W_uq.T
            q = q.reshape(B, T, nh, hs)
            q_lat = jnp.einsum('bqhd,hdl->bhql', q, k_eff)
            attn = jnp.einsum('bhql,bkl->bhqk', q_lat, c_kv) / sqrt(hs)
            causal = jnp.tril(jnp.ones((T, T), dtype=bool))
            attn = jnp.where(causal[None, None], attn, -jnp.inf)
            attn = jax.nn.softmax(attn, axis=-1)
            y_lat = jnp.einsum('bhqk,bkl->bhql', attn, c_kv)
            y = jnp.einsum('bhql,hld->bqhd', y_lat, v_eff).reshape(B, T, C)
            return (y, c_kv)
        key = jax.random.key(seed)
        ks = jax.random.split(key, 7)
        B, T, C = (2, 512, 256)
        QL, KVL = (128, 128)
        return {'x': jax.random.normal(ks[0], (B, T, C), dtype=jnp.float32), 'W_dq': jax.random.normal(ks[1], (QL, C), dtype=jnp.float32) * W_SCALE, 'W_uq': jax.random.normal(ks[2], (C, QL), dtype=jnp.float32) * W_SCALE, 'W_dkv': jax.random.normal(ks[3], (KVL, C), dtype=jnp.float32) * W_SCALE, 'W_uk': jax.random.normal(ks[4], (C, KVL), dtype=jnp.float32) * W_SCALE, 'W_uv': jax.random.normal(ks[5], (C, KVL), dtype=jnp.float32) * W_SCALE, 'W_o': jax.random.normal(ks[6], (C, C), dtype=jnp.float32) * W_SCALE}
    _L0_attn_all = _L0_attn_setup()
    _L0_attn_in = {k: v for k, v in _L0_attn_all.items() if k in ('W_dq', 'W_uq', 'W_dkv', 'W_uk', 'W_uv', 'W_o')}
    del _L0_attn_all

    def _L0_ffn_setup():
        import jax, jax.numpy as jnp
        import numpy as np
        from jax.scipy.linalg import expm
        B, S, D, E, K, NROT = (2, 512, 256, 8, 2, 3)
        EPS = 1e-05

        def _gelu(x):
            return jax.nn.gelu(x, approximate=False)

        def _forward(x, ln_gamma, ln_beta, abel_w, abel_b, moe_gate_w, moe_gate_b, ew1, eb1, ew2, eb2, gens, gc_w, gc_b):
            residual = x
            mu = jnp.mean(x, axis=-1, keepdims=True)
            var = jnp.mean((x - mu) ** 2, axis=-1, keepdims=True)
            xn = (x - mu) * jax.lax.rsqrt(var + EPS) * ln_gamma + ln_beta
            abel_out = _gelu(xn @ abel_w + abel_b)
            logits = xn @ moe_gate_w + moe_gate_b
            topw, topi = jax.lax.top_k(logits, K)
            topw = jax.nn.softmax(topw, axis=-1)
            w_dense = jnp.sum(jax.nn.one_hot(topi, E, dtype=xn.dtype) * topw[..., None], axis=-2)
            h = _gelu(jnp.einsum('bsd,edh->ebsh', xn, ew1) + eb1[:, None, None, :])
            eo = jnp.einsum('ebsh,ehd->ebsd', h, ew2) + eb2[:, None, None, :]
            moe_out = jnp.einsum('ebsd,bse->bsd', eo, w_dense)
            for i in range(NROT):
                moe_out = moe_out @ expm(gens[i])
            combined = jnp.concatenate([abel_out, moe_out], axis=-1)
            gate = jax.nn.sigmoid(combined @ gc_w + gc_b)
            mixed = abel_out * (1.0 - gate) + moe_out * gate
            return residual + mixed
        key = jax.random.key(seed)
        ks = jax.random.split(key, 16)
        sc = 0.02
        x = jax.random.normal(ks[0], (B, S, D), jnp.float32)
        ln_gamma = 1.0 + sc * jax.random.normal(ks[1], (D,), jnp.float32)
        ln_beta = sc * jax.random.normal(ks[2], (D,), jnp.float32)
        abel_w = sc * jax.random.normal(ks[3], (D, D), jnp.float32)
        abel_b = sc * jax.random.normal(ks[4], (D,), jnp.float32)
        moe_gate_w = sc * jax.random.normal(ks[5], (D, E), jnp.float32)
        moe_gate_b = sc * jax.random.normal(ks[6], (E,), jnp.float32)
        ew1 = sc * jax.random.normal(ks[7], (E, D, 2 * D), jnp.float32)
        eb1 = sc * jax.random.normal(ks[8], (E, 2 * D), jnp.float32)
        ew2 = sc * jax.random.normal(ks[9], (E, 2 * D, D), jnp.float32)
        eb2 = sc * jax.random.normal(ks[10], (E, D), jnp.float32)
        g = sc * jax.random.normal(ks[11], (NROT, D, D), jnp.float32)
        gens = 0.5 * (g - jnp.swapaxes(g, -1, -2))
        gc_w = sc * jax.random.normal(ks[12], (2 * D, 1), jnp.float32)
        gc_b = sc * jax.random.normal(ks[13], (1,), jnp.float32)
        return dict(x=x, ln_gamma=ln_gamma, ln_beta=ln_beta, abel_w=abel_w, abel_b=abel_b, moe_gate_w=moe_gate_w, moe_gate_b=moe_gate_b, ew1=ew1, eb1=eb1, ew2=ew2, eb2=eb2, gens=gens, gc_w=gc_w, gc_b=gc_b)
    _L0_ffn_all = _L0_ffn_setup()
    _L0_ffn_in = {k: v for k, v in _L0_ffn_all.items() if k in ('ln_gamma', 'ln_beta', 'abel_w', 'abel_b', 'moe_gate_w', 'moe_gate_b', 'ew1', 'eb1', 'ew2', 'eb2', 'gens', 'gc_w', 'gc_b')}
    del _L0_ffn_all
    return {'x': x, 'x_txt': x_txt, 'L0_tok_W': _L0_tok_in['W'], 'L0_txt_w': _L0_txt_in['w'], 'L0_attn_W_dq': _L0_attn_in['W_dq'], 'L0_attn_W_uq': _L0_attn_in['W_uq'], 'L0_attn_W_dkv': _L0_attn_in['W_dkv'], 'L0_attn_W_uk': _L0_attn_in['W_uk'], 'L0_attn_W_uv': _L0_attn_in['W_uv'], 'L0_attn_W_o': _L0_attn_in['W_o'], 'L0_ffn_ln_gamma': _L0_ffn_in['ln_gamma'], 'L0_ffn_ln_beta': _L0_ffn_in['ln_beta'], 'L0_ffn_abel_w': _L0_ffn_in['abel_w'], 'L0_ffn_abel_b': _L0_ffn_in['abel_b'], 'L0_ffn_moe_gate_w': _L0_ffn_in['moe_gate_w'], 'L0_ffn_moe_gate_b': _L0_ffn_in['moe_gate_b'], 'L0_ffn_ew1': _L0_ffn_in['ew1'], 'L0_ffn_eb1': _L0_ffn_in['eb1'], 'L0_ffn_ew2': _L0_ffn_in['ew2'], 'L0_ffn_eb2': _L0_ffn_in['eb2'], 'L0_ffn_gens': _L0_ffn_in['gens'], 'L0_ffn_gc_w': _L0_ffn_in['gc_w'], 'L0_ffn_gc_b': _L0_ffn_in['gc_b']}

def reference(x, x_txt, L0_tok_W, L0_txt_w, L0_attn_W_dq, L0_attn_W_uq, L0_attn_W_dkv, L0_attn_W_uk, L0_attn_W_uv, L0_attn_W_o, L0_ffn_ln_gamma, L0_ffn_ln_beta, L0_ffn_abel_w, L0_ffn_abel_b, L0_ffn_moe_gate_w, L0_ffn_moe_gate_b, L0_ffn_ew1, L0_ffn_eb1, L0_ffn_ew2, L0_ffn_eb2, L0_ffn_gens, L0_ffn_gc_w, L0_ffn_gc_b):
    import jax
    import jax.numpy as jnp

    def _L0_tok_ref(inputs, W):
        import jax, jax.numpy as jnp
        import numpy as np
        from jax import lax
        PATCH = 16
        B, C, H, Wimg = inputs.shape
        patches = lax.conv_general_dilated_patches(inputs, filter_shape=[PATCH, PATCH], window_strides=[PATCH, PATCH], padding='VALID', dimension_numbers=('NCHW', 'HWIO', 'NCHW'))
        patches = patches.reshape(B, -1, C * PATCH * PATCH)
        return jnp.einsum('bnf,fh->bnh', patches, W)

    def _L0_txt_ref(x, num_ctx, w):
        import jax, jax.numpy as jnp
        import numpy as np
        NUM_VOCAB = 8000
        NUM_HIDDEN = 256
        W_INIT_STDEV = 0.02
        num_vocab, num_hidden = w.shape
        if num_ctx > 0:
            x_flat = jnp.reshape(x, (-1, num_hidden))
            logits = jnp.einsum('th,vh->tv', x_flat, w)
            return jnp.reshape(logits, (-1, num_ctx, num_vocab))
        else:
            bs = x.shape[0]
            x_flat = jnp.reshape(x, (-1,))
            emb = jnp.take(w, x_flat, axis=0)
            return jnp.reshape(emb, (bs, -1, num_hidden))

    def _L0_attn_ref(x, W_dq, W_uq, W_dkv, W_uk, W_uv, W_o):
        import jax, jax.numpy as jnp
        import numpy as np
        from math import sqrt
        N_HEAD = 16
        W_SCALE = 0.02

        def _reference_tuple_inner(x, W_dq, W_uq, W_dkv, W_uk, W_uv, W_o):
            B, T, C = x.shape
            nh = N_HEAD
            hs = C // nh
            n_kvl = W_dkv.shape[0]
            k_eff = (W_dq.T @ W_uq.T @ W_uk).reshape(nh, hs, n_kvl)
            v_eff = jnp.transpose((W_uv.T @ W_o.T).reshape(n_kvl, nh, hs), (1, 0, 2))
            c_kv = x @ W_dkv.T
            q = x @ W_dq.T @ W_uq.T
            q = q.reshape(B, T, nh, hs)
            q_lat = jnp.einsum('bqhd,hdl->bhql', q, k_eff)
            attn = jnp.einsum('bhql,bkl->bhqk', q_lat, c_kv) / sqrt(hs)
            causal = jnp.tril(jnp.ones((T, T), dtype=bool))
            attn = jnp.where(causal[None, None], attn, -jnp.inf)
            attn = jax.nn.softmax(attn, axis=-1)
            y_lat = jnp.einsum('bhqk,bkl->bhql', attn, c_kv)
            y = jnp.einsum('bhql,hld->bqhd', y_lat, v_eff).reshape(B, T, C)
            return (y, c_kv)
        return _reference_tuple_inner(x, W_dq, W_uq, W_dkv, W_uk, W_uv, W_o)[0]

    def _L0_ffn_ref(x, ln_gamma, ln_beta, abel_w, abel_b, moe_gate_w, moe_gate_b, ew1, eb1, ew2, eb2, gens, gc_w, gc_b):
        import jax, jax.numpy as jnp
        import numpy as np
        from jax.scipy.linalg import expm
        B, S, D, E, K, NROT = (2, 512, 256, 8, 2, 3)
        EPS = 1e-05

        def _gelu(x):
            return jax.nn.gelu(x, approximate=False)

        def _forward(x, ln_gamma, ln_beta, abel_w, abel_b, moe_gate_w, moe_gate_b, ew1, eb1, ew2, eb2, gens, gc_w, gc_b):
            residual = x
            mu = jnp.mean(x, axis=-1, keepdims=True)
            var = jnp.mean((x - mu) ** 2, axis=-1, keepdims=True)
            xn = (x - mu) * jax.lax.rsqrt(var + EPS) * ln_gamma + ln_beta
            abel_out = _gelu(xn @ abel_w + abel_b)
            logits = xn @ moe_gate_w + moe_gate_b
            topw, topi = jax.lax.top_k(logits, K)
            topw = jax.nn.softmax(topw, axis=-1)
            w_dense = jnp.sum(jax.nn.one_hot(topi, E, dtype=xn.dtype) * topw[..., None], axis=-2)
            h = _gelu(jnp.einsum('bsd,edh->ebsh', xn, ew1) + eb1[:, None, None, :])
            eo = jnp.einsum('ebsh,ehd->ebsd', h, ew2) + eb2[:, None, None, :]
            moe_out = jnp.einsum('ebsd,bse->bsd', eo, w_dense)
            for i in range(NROT):
                moe_out = moe_out @ expm(gens[i])
            combined = jnp.concatenate([abel_out, moe_out], axis=-1)
            gate = jax.nn.sigmoid(combined @ gc_w + gc_b)
            mixed = abel_out * (1.0 - gate) + moe_out * gate
            return residual + mixed
        return _forward(x, ln_gamma, ln_beta, abel_w, abel_b, moe_gate_w, moe_gate_b, ew1, eb1, ew2, eb2, gens, gc_w, gc_b)
    h = _L0_tok_ref(x, L0_tok_W)
    h = jnp.concatenate([h, _L0_txt_ref(x_txt, 0, L0_txt_w)], axis=1)
    h = h + _L0_attn_ref(_layernorm(h, axis=-1), L0_attn_W_dq, L0_attn_W_uq, L0_attn_W_dkv, L0_attn_W_uk, L0_attn_W_uv, L0_attn_W_o)
    h = h + _L0_ffn_ref(_layernorm(h, axis=-1), L0_ffn_ln_gamma, L0_ffn_ln_beta, L0_ffn_abel_w, L0_ffn_abel_b, L0_ffn_moe_gate_w, L0_ffn_moe_gate_b, L0_ffn_ew1, L0_ffn_eb1, L0_ffn_ew2, L0_ffn_eb2, L0_ffn_gens, L0_ffn_gc_w, L0_ffn_gc_b)
    return h

_drawn_inputs = setup_inputs


def setup_inputs(seed=0):
    import zlib

    import numpy as np

    out = dict(_drawn_inputs(seed))
    spreads = {}
    factors = {'L0_attn_W_dq': 8.0,
     'L0_attn_W_uq': 8.0,
     'L0_attn_W_uk': 8.0,
     'L0_ffn_ln_gamma': 8.0,
     'L0_ffn_ln_beta': 8.0,
     'L0_ffn_abel_b': 8.0,
     'L0_ffn_moe_gate_w': 2.844,
     'L0_ffn_moe_gate_b': 8.0,
     'L0_ffn_eb1': 8.0,
     'L0_ffn_eb2': 8.0,
     'L0_ffn_gens': 6.369,
     'L0_ffn_gc_w': 8.0}
    for name, (base, spread) in spreads.items():
        noise = np.random.default_rng([zlib.crc32(name.encode()), seed]).standard_normal(out[name].shape)
        drawn = base * np.exp(spread * noise) if base else spread * noise
        out[name] = jnp.asarray(drawn.astype(out[name].dtype))
    for name, factor in factors.items():
        out[name] = (out[name] * factor).astype(out[name].dtype)
    return out
```

```python
from contextlib import ExitStack

import concourse.bass as bass
from concourse import mybir

F32 = mybir.dt.float32
BF16 = mybir.dt.bfloat16
I32 = mybir.dt.int32
ACT = mybir.ActivationFunctionType
ALU = mybir.AluOpType
AX = mybir.AxisListType.X
RMAX = bass.bass_isa.ReduceOp.max

NB, NPATCH, NTXT = 16, 36, 128
NQ = NPATCH + NTXT
PAIRS = NB // 2
TP = 2 * NQ
PROWS = 2 * NPATCH
ROWS = (128, 128, PROWS)
TILES = 3 * PAIRS
D = 256
FC = 768 // 128
HEADS, HD = 16, 16
VW = HD + 1
VROW = HEADS * VW + 16
E, HID = 8, 512
SLOT_TILES = (2 * NB * NQ + E * 127) // 128
EPS = 1e-5
TERMS = 6
FACT = [1.0]
for _k in range(1, TERMS + 1):
    FACT.append(FACT[-1] * _k)


class Chain:

    def __init__(self, eng, sem):
        self.eng, self.sem, self.base, self.n = eng, sem, 0, 0

    def __call__(self, ins):
        ins.then_inc(self.sem, 1)
        self.n += 1
        self.eng.wait_ge(self.sem, self.base + self.n)

    def loop(self, base):
        self.base, self.n = base, 0


def early_fusion_program(nc, ins, out):
    ctx = ExitStack()
    with ctx:
        def sb(name, shape, dt=F32):
            return ctx.enter_context(nc.sbuf_tensor(name, shape, dt))

        def sem(name):
            return ctx.enter_context(nc.semaphore(name))

        h_all = sb("h_all", [128, TILES, D])
        pre_all = sb("pre_all", [128, TILES, D + E])
        xn_all = sb("xn_all", [128, TILES, D])
        ident = sb("ident", [128, 128])
        identb = sb("identb", [128, 128], BF16)
        maskb = sb("maskb", [128, 2 * NQ + 2 * NPATCH], BF16)
        gam = sb("gam", [128, D])
        bet = sb("bet", [128, D])
        agb = sb("agb", [128, D + E])
        gcw = sb("gcw", [128, 2 * D])
        gcb = sb("gcb", [128, 1])
        ids = sb("ids", [128, NB], I32)
        R = sb("R", [128, 2, D])

        AW = 29504
        arena = sb("arena", [128, AW])
        top = [0]

        def take(n, rows=128):
            a = top[0]
            top[0] += n
            assert top[0] <= AW, top[0]
            return arena[0:rows, a:a + n]

        wtok = take(FC * D).rearrange("p (c n) -> p c n", c=FC)
        patches = take(FC * NB * NPATCH).rearrange("p (c n) -> p c n", c=FC)
        embT = take(2 * PROWS).rearrange("p (c n) -> p c n", c=2)
        xw = take(3 * D).rearrange("p (u d) -> p u d", u=3)
        xT = take(2 * TP).rearrange("p (c n) -> p c n", c=2)
        lat = take(2 * TP).rearrange("p (c n) -> p c n", c=2)
        qT = [take(4 * TP).rearrange("p (g n) -> p g n", g=4) for _ in range(2)]
        kT = [take(4 * TP).rearrange("p (g n) -> p g n", g=4) for _ in range(2)]
        Vt = [take(2 * VROW).rearrange("p (b n) -> p b n", b=2) for _ in range(2)]
        Vp = [take(2 * VROW).rearrange("p (b n) -> p b n", b=2) for _ in range(2)]
        Pt = [take(8 * NQ).rearrange("p (i g n) -> p i g n", i=4, g=2) for _ in range(2)]
        Pp = [take(8 * NPATCH, NPATCH).rearrange("p (i g n) -> p i g n", i=4, g=2) for _ in range(2)]
        PTt = [take(4 * NTXT).rearrange("p (i n) -> p i n", i=4) for _ in range(2)]
        PTp = [take(4 * NQ, NPATCH).rearrange("p (i n) -> p i n", i=4) for _ in range(2)]
        yTs = [take(4 * TP).rearrange("p (g n) -> p g n", g=4) for _ in range(2)]
        x2w = take(3 * D).rearrange("p (u d) -> p u d", u=3)
        xnw = take(3 * D).rearrange("p (u d) -> p u d", u=3)
        xnT = take(2 * TP).rearrange("p (c n) -> p c n", c=2)
        wdq = take(2 * 128).rearrange("p (c n) -> p c n", c=2)
        wdkv = take(2 * 128).rearrange("p (c n) -> p c n", c=2)
        wuq = take(512)
        ket = take(512)
        ve = take(D)
        wag = take(2 * (D + E)).rearrange("p (c n) -> p c n", c=2)
        p_uq = take(256).rearrange("p (c n) -> p c n", c=2)
        p_uk = take(256).rearrange("p (c n) -> p c n", c=2)
        p_dq = take(512)
        p_uv = take(256).rearrange("p (c n) -> p c n", c=2)
        p_o = take(512).rearrange("p (c n) -> p c n", c=2)
        p_g = take(128)

        top[0] = 0
        w1 = take(E * 2 * HID).rearrange("p (e n) -> p e n", e=E)
        w2 = take(E * 4 * D).rearrange("p (e n) -> p e n", e=E)
        eb1 = take(E * HID).rearrange("p (e n) -> p e n", e=E)
        eb2 = take(E * D).rearrange("p (e n) -> p e n", e=E)
        mark = top[0]
        X = take(3 * 2 * D).rearrange("p (g k n) -> p g k n", g=3, k=2)
        XT = take(3 * 2 * D).rearrange("p (g k n) -> p g k n", g=3, k=2)
        EX = take(3 * 2 * D).rearrange("p (g k n) -> p g k n", g=3, k=2)
        EXT = take(3 * 2 * D).rearrange("p (g k n) -> p g k n", g=3, k=2)
        ident2 = take(2 * D).rearrange("p (k n) -> p k n", k=2)
        top[0] = mark
        tok = [take(D) for _ in range(2)]
        tokT = [take(D).rearrange("p (c n) -> p c n", c=2) for _ in range(2)]
        pre = [take(HID) for _ in range(2)]
        hid = [take(HID) for _ in range(2)]
        hidT = [take(HID).rearrange("p (c n) -> p c n", c=4) for _ in range(2)]
        eo = [take(D) for _ in range(2)]
        top[0] = 0
        G = [take(TILES * D).rearrange("p (t d) -> p t d", t=TILES) for _ in range(2)]
        moe = [take(3 * D).rearrange("p (u d) -> p u d", u=3) for _ in range(2)]
        moeT = [take(2 * TP).rearrange("p (c n) -> p c n", c=2) for _ in range(2)]
        mo = [take(3 * D).rearrange("p (u d) -> p u d", u=3) for _ in range(2)]
        junk = take(D)
        res = [take(3 * D).rearrange("p (u d) -> p u d", u=3) for _ in range(2)]

        stats = sb("stats", [128, 3, 6])
        mv = sb("mv", [128, 3, 2])
        veps = sb("veps", [128, 3])
        lnv = sb("lnv", [128, 3])
        rstd = sb("rstd", [128, 3])
        nt1 = sb("nt1", [128, 3])
        nt2 = sb("nt2", [128, 3])
        carry = sb("carry", [128, 2])
        mx = sb("mx", [128, 4, 2])
        mxp = sb("mxp", [NPATCH, 4, 2])
        rec = sb("rec", [128, HEADS])
        ysum = sb("ysum", [128, D])
        em8 = sb("em8", [128, E])
        valid = sb("valid", [128, TILES])
        slot0 = sb("slot0", [128, SLOT_TILES])
        tri = sb("tri", [128, 128])
        ones = sb("ones", [128, 128])
        TE = [128, TILES, E]
        r1, r2, oh1, oh2, msum = (sb(n, TE) for n in ("r1", "r2", "oh1", "oh2", "msum"))
        m1, m2, e1, e2, wt1, wt2, zab, zmo = (
            sb(n, [128, TILES]) for n in ("m1", "m2", "e1", "e2", "wt1", "wt2", "zab", "zmo"))
        cnt, base, endb = (sb(n, [128, E]) for n in ("cnt", "base", "endb"))
        cnti = sb("cnti", [128, E], I32)
        slots = [sb(f"slots{k}", [128, TILES], I32) for k in range(2)]
        cmp = sb("cmp", [128, SLOT_TILES, E - 1])
        exf = sb("exf", [128, SLOT_TILES])
        exi = sb("exi", [128, SLOT_TILES], I32)
        rows = sb("rows", [128, 8])
        expo = sb("expo", [128, 4], I32)
        zg = sb("zg", [128, 8])

        ps = ctx.enter_context(nc.psum_tensor("ps", [128, 8, 512], F32))
        xg = nc.dram_tensor("xg", (SLOT_TILES * 128, D), F32, kind="Internal").ap()
        eod = nc.dram_tensor("eod", (SLOT_TILES * 128, D), F32, kind="Internal").ap()

        s_ld_attn = sem("ld_attn")
        s_ld_ids = sem("ld_ids")
        s_ld_gens = sem("ld_gens")
        s_ld_ffn = sem("ld_ffn")
        s_ld_exp = sem("ld_exp")
        s_ld_route = sem("ld_route")
        s_gath0 = sem("gath0")
        s_gath = sem("gath")
        s_pads = sem("pads")
        s_prep_mm = sem("prep_mm")
        s_prep_cp = sem("prep_cp")
        s_cleared = sem("cleared")
        s_ones_set = sem("ones_set")
        s_emb_mm = sem("emb_mm")
        s_emb_cp = sem("emb_cp")
        s_emb_tr = sem("emb_tr")
        s_emb_ev = sem("emb_ev")
        s_ln1_var = sem("ln1_var")
        s_ln1_rs = sem("ln1_rs")
        s_x_ready = sem("x_ready")
        s_x_tr = sem("x_tr")
        s_xT_cp = sem("xT_cp")
        s_lat_mm = sem("lat_mm")
        s_lat_cp = sem("lat_cp")
        s_q_mm = sem("q_mm")
        s_q_cp = sem("q_cp")
        s_k_mm = sem("k_mm")
        s_k_cp = sem("k_cp")
        s_v_mm = sem("v_mm")
        s_v_cp = sem("v_cp")
        s_scores = sem("scores")
        s_shifted = sem("shifted")
        s_probs = sem("probs")
        s_p_tr = sem("p_tr")
        s_pt_txt = sem("pt_txt")
        s_pt_patch = sem("pt_patch")
        s_pv = sem("pv")
        s_yt = sem("yt")
        s_y_tr = sem("y_tr")
        s_y_ev = sem("y_ev")
        s_ln2_var = sem("ln2_var")
        s_ln2_rs = sem("ln2_rs")
        s_x2_ready = sem("x2_ready")
        s_ln3_var = sem("ln3_var")
        s_ln3_rs = sem("ln3_rs")
        s_x3_ready = sem("x3_ready")
        s_xn_ready = sem("xn_ready")
        s_xn_tr = sem("xn_tr")
        s_xnT_cp = sem("xnT_cp")
        s_ag_mm = sem("ag_mm")
        s_ag_ev = sem("ag_ev")
        s_h_res = sem("h_res")
        s_xn_kept = sem("xn_kept")
        s_dve_step = sem("dve_step")
        s_act_step = sem("act_step")
        s_pool_step = sem("pool_step")
        s_norm_part = sem("norm_part")
        s_norm_all = sem("norm_all")
        s_x_scaled = sem("x_scaled")
        s_hr_mm = sem("hr_mm")
        s_hr_ev = sem("hr_ev")
        s_sq_mm = sem("sq_mm")
        s_sq_ev = sem("sq_ev")
        s_sqT_mm = sem("sqT_mm")
        s_sqT_cp = sem("sqT_cp")
        s_fin_ready = sem("fin_ready")
        s_rmul = sem("rmul")
        s_rmul_ev = sem("rmul_ev")
        s_rt_m = sem("rt_m")
        s_rt_mm = sem("rt_mm")
        s_slots_ready = sem("slots_ready")
        s_gap_ready = sem("gap_ready")
        s_gates = sem("gates")
        s_sent = sem("sent")
        s_tok_ld0 = sem("tok_ld0")
        s_tok_ld1 = sem("tok_ld1")
        s_tok_tr = sem("tok_tr")
        s_tokT_cp = sem("tokT_cp")
        s_up_mm = sem("up_mm")
        s_up_ev = sem("up_ev")
        s_gelu = sem("gelu")
        s_hid_tr = sem("hid_tr")
        s_hidT_cp = sem("hidT_cp")
        s_down_mm = sem("down_mm")
        s_eo_ready = sem("eo_ready")
        s_eo_st0 = sem("eo_st0")
        s_eo_st1 = sem("eo_st1")
        s_abel_done = sem("abel_done")
        s_back0 = sem("back0")
        s_back1 = sem("back1")
        s_back2 = sem("back2")
        s_mix = sem("mix")
        s_m_tr = sem("m_tr")
        s_mT_cp = sem("mT_cp")
        s_mr_mm = sem("mr_mm")
        s_mr_ev = sem("mr_ev")
        s_z_ready = sem("z_ready")
        s_z_exp = sem("z_exp")
        s_res_ready = sem("res_ready")
        s_out_st0 = sem("out_st0")
        s_out_st1 = sem("out_st1")

        block = ctx.enter_context(nc.Block())

        def after(eng, sem_, count):
            if not (isinstance(count, int) and count <= 0):
                eng.wait_ge(sem_, count)

        def tile3(t3, expr, u):
            return t3[0:ROWS[u], bass.ds(3 * expr + u, 1), :].rearrange("p a d -> p (a d)")

        def pair_loop(eng, body):
            body(0, 0, True, False)
            with eng.Fori(0, (PAIRS - 2) // 2) as i:
                for u in range(2):
                    body(2 * i + (1 + u), (1 + u) % 2, False, False)
            body(PAIRS - 1, (PAIRS - 1) % 2, False, True)

        @block.sync
        def _(sp):
            sp.dma_start(ids[:], ins["ids"]).then_inc(s_ld_ids, 16)
            sp.dma_start(ident[:], ins["ident"]).then_inc(s_ld_attn, 16)
            sp.dma_start(patches, ins["patches"].rearrange("(c p) n -> p c n", p=128)).then_inc(s_ld_attn, 16)
            sp.dma_start(wtok, ins["wtok"].rearrange("(c p) n -> p c n", p=128)).then_inc(s_ld_attn, 16)
            for dst, name in ((p_uq, "uq"), (p_uk, "uk"), (p_uv, "uv"), (p_o, "o_t"), (wdq, "dq_t"),
                              (wdkv, "dkv_t"), (wag, "ag")):
                sp.dma_start(dst, ins[name].rearrange("(c p) n -> p c n", p=128)).then_inc(s_ld_attn, 16)
            for dst, name in ((p_dq, "dq_pad"), (wuq, "uq_pad"), (identb[:], "identb"), (maskb[:], "maskb")):
                sp.dma_start(dst, ins[name]).then_inc(s_ld_attn, 16)
            for dst, name in ((gam, "gamma"), (bet, "beta"), (agb, "ag_b"), (gcw, "gc_w"), (gcb, "gc_b")):
                sp.dma_start(dst[:], ins[name].partition_broadcast(128)).then_inc(s_ld_ffn, 16)
            for dst, name in ((valid, "valid"), (tri, "tri"), (em8, "em8"), (slot0, "slot0")):
                sp.dma_start(dst[:], ins[name]).then_inc(s_ld_route, 16)
            sp.wait_ge(s_cleared, 1)
            zero = xn_all[:, :, :]
            for c in range(SLOT_TILES // TILES):
                sp.dma_start(xg[c * TILES * 128:(c + 1) * TILES * 128, :].rearrange("(t p) d -> p t d", p=128),
                             zero).then_inc(s_pads, 16)
            sp.wait_ge(s_ag_ev, PAIRS)
            sp.wait_ge(s_xn_kept, PAIRS)
            sp.dma_start(X, ins["gens"].rearrange("g (k p) n -> p g k n", p=128)).then_inc(s_ld_gens, 16)
            sp.dma_start(XT, ins["gens_t"].rearrange("g (k p) n -> p g k n", p=128)).then_inc(s_ld_gens, 16)
            for e in range(E):
                sp.dma_start(w1[:, e, :].rearrange("p (k n) -> p k n", k=2),
                             ins["ew1"][e].rearrange("(k p) n -> p k n", p=128)).then_inc(s_ld_exp, 16)
                sp.dma_start(w2[:, e, :].rearrange("p (k n) -> p k n", k=4),
                             ins["ew2"][e].rearrange("(k p) n -> p k n", p=128)).then_inc(s_ld_exp, 16)
            sp.dma_start(eb1.rearrange("p e n -> p (e n)"),
                         ins["eb1"].rearrange("e n -> (e n)").partition_broadcast(128)).then_inc(s_ld_exp, 16)
            sp.dma_start(eb2.rearrange("p e n -> p (e n)"),
                         ins["eb2"].rearrange("e n -> (e n)").partition_broadcast(128)).then_inc(s_ld_exp, 16)
            sp.wait_ge(s_sent, 16 * 2 * TILES)
            sp.wait_ge(s_fin_ready, 2)
            sp.dma_start(tok[0], xg[0:128, :]).then_inc(s_tok_ld0, 16)
            sp.dma_start(tok[1], xg[128:256, :]).then_inc(s_tok_ld1, 16)
            with sp.Fori(0, SLOT_TILES // 2 - 1) as i:
                for p, ld in ((0, s_tok_ld0), (1, s_tok_ld1)):
                    t = 2 * i + (2 + p)
                    sp.wait_ge(s_tok_tr, t - 1)
                    sp.dma_start(tok[p], xg[bass.ds(t * 128, 128), :]).then_inc(ld, 16)
            with sp.Fori(0, PAIRS // 2) as i:
                for p, st in ((0, s_out_st0), (1, s_out_st1)):
                    j = 2 * i + p
                    sp.wait_ge(s_res_ready, j + 1)
                    for u in range(2):
                        b = 2 * j + u
                        sp.dma_start(out[bass.ds(b, 1), NPATCH:NQ, :].rearrange("b n d -> (b n) d"),
                                     res[p][:, u, :]).then_inc(st, 16)
                        sp.dma_start(out[bass.ds(b, 1), 0:NPATCH, :].rearrange("b n d -> (b n) d"),
                                     res[p][NPATCH * u:NPATCH * (u + 1), 2, :]).then_inc(st, 16)
            sp.wait_ge(s_out_st0, 64 * PAIRS // 2)
            sp.wait_ge(s_out_st1, 64 * PAIRS // 2)

        @block.gpsimd
        def _(pool):
            step = Chain(pool, s_pool_step)
            pool.memset(xn_all[:], 0.0).then_inc(s_cleared, 1)
            pool.wait_ge(s_ld_ids, 16)
            for b in range(NB):
                pool.indirect_dma_start(
                    out=h_all[:, 3 * (b // 2) + b % 2, :], out_offset=None, in_=ins["txt_w"],
                    in_offset=bass.IndirectOffsetOnAxis(ap=ids[:, b:b + 1], axis=0),
                ).then_inc(s_gath0 if b < 2 else s_gath, 16)
            pool.memset(pre_all[:], 0.0)
            pool.memset(mv[:], 1.0)
            pool.memset(ones[:], 1.0)
            for p in range(2):
                pool.memset(Vt[p], 1.0)
                pool.memset(Vp[p], 1.0)
            pool.memset(xw, 0.0)
            pool.memset(x2w, 0.0)
            pool.memset(xnw, 0.0).then_inc(s_ones_set, 1)
            pool.wait_ge(s_ld_ffn, 80)
            pool.wait_ge(s_pads, 16 * (SLOT_TILES // TILES))

            def finish_rows(c):
                pool.wait_ge(s_x2_ready, c + 1)
                for u in range(3):
                    ins_ = pool.tensor_tensor(tile3(h_all, c, u), tile3(h_all, c, u), x2w[0:ROWS[u], u, :], ALU.add)
                ins_.then_inc(s_h_res, 1)
                pool.wait_ge(s_x3_ready, c + 1)
                for u in range(3):
                    ins_ = pool.tensor_tensor(xnw[:, u, :], x2w[:, u, :], gam[:], ALU.mult)
                step(ins_)
                for u in range(3):
                    ins_ = pool.tensor_tensor(xnw[:, u, :], xnw[:, u, :], bet[:], ALU.add)
                ins_.then_inc(s_xn_ready, 1)
                pool.wait_ge(s_xn_ready, c + 1)
                for u in range(3):
                    ins_ = pool.tensor_copy(tile3(xn_all, c, u), xnw[0:ROWS[u], u, :])
                ins_.then_inc(s_xn_kept, 1)

            with pool.Fori(0, PAIRS) as c:
                step.loop(c)
                finish_rows(c)
            pool.wait_ge(s_norm_part, 1)
            pool.partition_all_reduce(rows[:, 7:8], rows[:, 6:7], 128, RMAX).then_inc(s_norm_all, 1)
            pool.wait_ge(s_slots_ready, 1)
            for t in range(TILES):
                n = ROWS[t % 3]
                for k in range(2):
                    pool.indirect_dma_start(
                        out=xg, out_offset=bass.IndirectOffsetOnAxis(ap=slots[k][0:n, t:t + 1], axis=0),
                        in_=xn_all[0:n, t, :], in_offset=None).then_inc(s_sent, 16)
            pool.wait_ge(s_eo_st0, 16 * SLOT_TILES // 2)
            pool.wait_ge(s_eo_st1, 16 * SLOT_TILES // 2)
            pool.wait_ge(s_down_mm, SLOT_TILES)
            for t in range(TILES):
                n = ROWS[t % 3]
                part = (s_back0, s_back1, s_back2)[min(t // 6, 2)]
                for k in range(2):
                    pool.indirect_dma_start(
                        out=G[k][0:n, t, :], out_offset=None, in_=eod,
                        in_offset=bass.IndirectOffsetOnAxis(ap=slots[k][0:n, t:t + 1], axis=0)).then_inc(part, 16)

        @block.tensor
        def _(pe):
            def acc(o, pairs):
                for n, (a, b) in enumerate(pairs):
                    last = pe.matmul(o, a, b, start=(n == 0), stop=(n == len(pairs) - 1))
                return last

            pe.wait_ge(s_ld_attn, 16 * 14)
            acc(ps[:, 4, 0:128], [(p_uq[:, c, :], p_uk[:, c, :]) for c in range(2)]).then_inc(s_prep_mm, 1)
            acc(ps[:, 5, 0:D], [(p_uv[:, c, :], p_o[:, c, :]) for c in range(2)]).then_inc(s_prep_mm, 1)
            pe.wait_ge(s_prep_cp, 1)
            pe.matmul(ps[:, 6, :], p_g, p_dq, start=True, stop=True).then_inc(s_prep_mm, 1)
            pe.wait_ge(s_prep_cp, 3)

            def embed(a):
                for m in range(2):
                    last = acc(ps[:, 4, m * PROWS:(m + 1) * PROWS],
                               [(wtok[:, c, m * 128:(m + 1) * 128], patches[:, c, bass.ds(a * PROWS, PROWS)])
                                for c in range(FC)])
                last.then_inc(s_emb_mm, 1)
                pe.wait_ge(s_emb_cp, a + 1)
                for m in range(2):
                    last = pe.transpose(ps[0:PROWS, 5, m * 128:(m + 1) * 128], embT[:, m, :], ident[:])
                last.then_inc(s_emb_tr, 1)

            def turn_x(a):
                pe.wait_ge(s_x_ready, a + 1)
                for c in range(2):
                    for u, at in ((2, 0), (0, PROWS), (1, PROWS + 128)):
                        n = ROWS[u]
                        last = pe.transpose(ps[:, 4 + c, at:at + n], xw[0:n, u, c * 128:(c + 1) * 128],
                                            ident[0:n, 0:n])
                last.then_inc(s_x_tr, 1)

            def latents(a):
                pe.wait_ge(s_xT_cp, a + 1)
                acc(ps[:, 4, 0:TP], [(wdq[:, c, :], xT[:, c, :]) for c in range(2)])
                acc(ps[:, 5, 0:TP], [(wdkv[:, c, :], xT[:, c, :]) for c in range(2)]).then_inc(s_lat_mm, 1)

            def queries_keys_values(a):
                pe.wait_ge(s_lat_cp, a + 1)
                for g in range(4):
                    last = pe.matmul(ps[:, 4 + g, 0:TP], wuq[:, g * 128:(g + 1) * 128], lat[:, 0, :],
                                     start=True, stop=True)
                    if g % 2:
                        last.then_inc(s_q_mm, 1)
                for g in range(4):
                    if g % 2 == 0:
                        pe.wait_ge(s_q_cp, 2 * a + 1 + g // 2)
                    last = pe.matmul(ps[:, 4 + g, 0:TP], ket[:, g * 128:(g + 1) * 128], lat[:, 1, :],
                                     start=True, stop=True)
                    if g % 2:
                        last.then_inc(s_k_mm, 1)
                pe.wait_ge(s_k_cp, 2 * a + 1)
                for b in range(2):
                    at = b * NQ
                    pe.matmul(ps[:, 4, b * D:(b + 1) * D], lat[:, 1, at + NPATCH:at + NQ], ve, start=True, stop=True)
                    last = pe.matmul(ps[0:NPATCH, 5, b * D:(b + 1) * D], lat[:, 1, at:at + NPATCH], ve,
                                     start=True, stop=True)
                last.then_inc(s_v_mm, 1)

            def score(n, p, b, half):
                after(pe, s_shifted, n)
                for i in range(4):
                    pe.matmul(ps[:, i, 0:2 * NQ + 2 * NPATCH], identb[:], maskb[:], start=True, stop=False,
                              skip_group_check=True)
                at = b * NQ
                for gg in range(2):
                    g = 2 * half + gg
                    for i in range(4):
                        r = slice(32 * i, 32 * i + 32)
                        pe.matmul(ps[:, i, gg * NQ:(gg + 1) * NQ], qT[p][r, g, at + NPATCH:at + NQ],
                                  kT[p][r, g, at:at + NQ], start=False, stop=True, skip_group_check=True)
                for gg in range(2):
                    g = 2 * half + gg
                    for i in range(4):
                        r = slice(32 * i, 32 * i + 32)
                        o = 2 * NQ + gg * NPATCH
                        last = pe.matmul(ps[0:NPATCH, i, o:o + NPATCH], qT[p][r, g, at:at + NPATCH],
                                         kT[p][r, g, at:at + NPATCH], start=False, stop=True, skip_group_check=True)
                last.then_inc(s_scores, 1)

            def turn_probs(q, gp, rp):
                for i in range(4):
                    pe.transpose(ps[:, 4, i * NTXT:(i + 1) * NTXT], Pt[rp][:, i, gp, NPATCH:NQ], ident[:])
                for i in range(4):
                    pe.transpose(ps[0:NPATCH, 5, i * NTXT:(i + 1) * NTXT], Pt[rp][:, i, gp, 0:NPATCH], ident[:])
                for i in range(4):
                    last = pe.transpose(ps[0:NPATCH, 6 + gp, i * NPATCH:(i + 1) * NPATCH], Pp[rp][:, i, gp, :],
                                        ident[0:NPATCH, 0:NPATCH])
                last.then_inc(s_p_tr, 1)

            def weigh_values(q, gp, p, b, g):
                pe.wait_ge(s_pt_txt, q + 1)
                pe.wait_ge(s_pt_patch, q + 1)
                for i in range(4):
                    h = 4 * g + i
                    pe.matmul(ps[32 * i:32 * i + 32, 6 + gp, NPATCH:NQ], Vt[p][:, b, VW * h:VW * h + 32],
                              PTt[gp][:, i, :], start=True, stop=False, skip_group_check=True)
                for i in range(4):
                    h = 4 * g + i
                    last = pe.matmul(ps[32 * i:32 * i + 32, 6 + gp, 0:NQ], Vp[p][0:NPATCH, b, VW * h:VW * h + 32],
                                     PTp[gp][:, i, :], start=False, stop=True, skip_group_check=True)
                last.then_inc(s_pv, 1)

            def turn_y(c, p):
                for u, at in ((0, PROWS), (1, PROWS + 128), (2, 0)):
                    for g in range(4):
                        last = pe.transpose(ps[0:ROWS[u], 4 + u, g * 128:(g + 1) * 128],
                                            yTs[p][:, g, at:at + ROWS[u]], ident[:])
                last.then_inc(s_y_tr, 1)

            def turn_xn(c):
                pe.wait_ge(s_xn_ready, c + 1)
                for k in range(2):
                    for u, at in ((2, 0), (0, PROWS), (1, PROWS + 128)):
                        n = ROWS[u]
                        last = pe.transpose(ps[:, 6 + k, at:at + n], xnw[0:n, u, k * 128:(k + 1) * 128],
                                            ident[0:n, 0:n])
                last.then_inc(s_xn_tr, 1)

            def abel_and_gate(c):
                pe.wait_ge(s_xnT_cp, c + 1)
                for u, at, bank in ((0, PROWS, 6), (1, PROWS + 128, 7), (2, 0, 5)):
                    n = ROWS[u]
                    last = acc(ps[0:n, bank, 0:D + E], [(xnT[:, k, at:at + n], wag[:, k, :]) for k in range(2)])
                last.then_inc(s_ag_mm, 1)

            def round_(j, k, par, first, last):
                n = 4 * j + k
                a = j + 1
                c = j - 1
                no_prev = first and k == 0
                q = 2 * n - 2
                prev_par = par if k else 1 - par
                pb, ph = ((k - 1) % 4) // 2, (k - 1) % 2
                rp = (k + 1) % 2
                if not no_prev:
                    pe.wait_ge(s_probs, n)
                    if not (first and k == 1):
                        pe.wait_ge(s_pt_txt, q)
                        pe.wait_ge(s_pt_patch, q)
                        pe.wait_ge(s_yt, q)
                    turn_probs(q, 0, rp)
                    pe.wait_ge(s_pt_txt, q + 1)
                    pe.wait_ge(s_pt_patch, q + 1)
                if k == 0 and not last:
                    embed(a)
                if k == 1 and not first:
                    turn_y(c, 1 - par)
                if k == 2 and not last:
                    turn_x(a)
                if k == 3:
                    if not last:
                        latents(a)
                    if not first:
                        turn_xn(c)
                    if not last:
                        if not first:
                            pe.wait_ge(s_xnT_cp, c + 1)
                        queries_keys_values(a)
                        pe.wait_ge(s_k_cp, 2 * a + 2)
                        pe.wait_ge(s_v_cp, a + 1)
                    if not first:
                        abel_and_gate(c)
                if not no_prev:
                    if k == 0 and not last:
                        pe.wait_ge(s_emb_ev, a + 1)
                    if k == 1 and not first:
                        pe.wait_ge(s_y_ev, c + 1)
                    if k == 2 and not last:
                        pe.wait_ge(s_xT_cp, a + 1)
                    if k == 3 and not first:
                        pe.wait_ge(s_ag_ev, c + 1)
                    turn_probs(q + 1, 1, rp)
                score(n, par, k // 2, k % 2)
                if not no_prev:
                    weigh_values(q, 0, prev_par, pb, 2 * ph)
                    weigh_values(q + 1, 1, prev_par, pb, 2 * ph + 1)

            embed(0)
            turn_x(0)
            latents(0)
            queries_keys_values(0)
            pe.wait_ge(s_k_cp, 2)
            pe.wait_ge(s_v_cp, 1)

            def pair(j, par, first, last):
                for k in range(4):
                    round_(j, k, par, first, last)

            pair_loop(pe, pair)

            n = 4 * PAIRS
            q = 2 * n - 2
            lp = (PAIRS - 1) % 2
            pe.wait_ge(s_probs, n)
            pe.wait_ge(s_yt, q)
            for gp in range(2):
                pe.wait_ge(s_pt_txt, q + gp)
                pe.wait_ge(s_pt_patch, q + gp)
                turn_probs(q + gp, gp, 1)
                weigh_values(q + gp, gp, lp, 1, 2 + gp)
            pe.wait_ge(s_yt, q + 2)
            turn_y(PAIRS - 1, lp)
            turn_xn(PAIRS - 1)
            pe.wait_ge(s_y_ev, PAIRS)
            abel_and_gate(PAIRS - 1)
            pe.wait_ge(s_ag_ev, PAIRS)

            def product(bank, lhsT, rhs):
                for m in range(2):
                    last = acc(ps[:, bank, m * D:(m + 1) * D],
                               [(lhsT[:, k, m * 128:(m + 1) * 128], rhs[:, k, :]) for k in range(2)])
                return last

            def turn(bank, src):
                for a in range(2):
                    for b in range(2):
                        last = pe.transpose(ps[:, bank, a * D + b * 128:a * D + (b + 1) * 128],
                                            src[:, b, a * 128:(a + 1) * 128], ident[:])
                return last

            pe.wait_ge(s_rt_m, 1)
            ms = msum[:, :, :].rearrange("p t e -> p (t e)")
            pe.matmul(ps[:, 6, 0:TILES * E], tri[:], ms, start=True, stop=True)
            pe.matmul(ps[:, 7, 0:TILES * E], ones[:], ms, start=True, stop=True).then_inc(s_rt_mm, 1)

            pe.wait_ge(s_x_scaled, 1)
            for d in range(TERMS - 1):
                for g in range(3):
                    if d:
                        pe.wait_ge(s_hr_ev, 3 * (d - 1) + g + 1)
                    product(g, XT[:, g], EX[:, g]).then_inc(s_hr_mm, 1)
            for g in range(3):
                pe.wait_ge(s_hr_ev, 3 * (TERMS - 2) + g + 1)
                turn(3 + g, EX[:, g]).then_inc(s_sqT_mm, 1)
            squarings = pe.value_load(expo[0:1, 1:2], min_val=1, max_val=126)
            with pe.Fori(0, squarings) as i:
                for g in range(3):
                    pe.wait_ge(s_sqT_cp, 3 * i + 3)
                    product(g, EXT[:, g], EX[:, g]).then_inc(s_sq_mm, 1)
                for g in range(3):
                    pe.wait_ge(s_sq_ev, 3 * i + g + 1)
                    turn(3 + g, EX[:, g]).then_inc(s_sqT_mm, 1)
            pe.wait_ge(s_fin_ready, 1)
            product(0, EXT[:, 1], EX[:, 2]).then_inc(s_rmul, 1)
            pe.wait_ge(s_rmul_ev, 1)
            product(1, EXT[:, 0], EX[:, 1]).then_inc(s_rmul, 1)

            pe.wait_ge(s_ld_exp, 16 * (2 * E + 2))
            pe.wait_ge(s_fin_ready, 2)

            def in_tile(ldcount, t, p):
                pe.wait_ge((s_tok_ld0, s_tok_ld1)[p], ldcount)
                after(pe, s_tokT_cp, t)
                for c in range(2):
                    last = pe.transpose(ps[:, 0, c * 128:(c + 1) * 128], tok[p][:, c * 128:(c + 1) * 128], ident[:])
                last.then_inc(s_tok_tr, 1)

            def up(t, p):
                e = pe.value_load(exi[0:1, bass.ds(t, 1)], min_val=0, max_val=E - 1)
                pe.wait_ge(s_tokT_cp, t + 1)
                if not (isinstance(t, int) and t < 2):
                    pe.wait_ge(s_up_ev, t - 1)
                for k in range(2):
                    w = w1[:, bass.ds(e, 1), k * HID:(k + 1) * HID].rearrange("p a n -> p (a n)")
                    last = pe.matmul(ps[:, 1 + p, :], tokT[p][:, k, :], w, start=(k == 0), stop=(k == 1))
                last.then_inc(s_up_mm, 1)
                return e

            def turn_hid(t, p):
                pe.wait_ge(s_gelu, t + 1)
                after(pe, s_hidT_cp, t)
                for c in range(4):
                    last = pe.transpose(ps[:, 3, c * 128:(c + 1) * 128], hid[p][:, c * 128:(c + 1) * 128], ident[:])
                last.then_inc(s_hid_tr, 1)

            def down(t, p, peeled):
                e = pe.value_load(exi[0:1, bass.ds(t, 1)], min_val=0, max_val=E - 1)
                pe.wait_ge(s_hidT_cp, t + 1)
                if not peeled:
                    pe.wait_ge(s_eo_ready, t - 1)
                for k in range(4):
                    w = w2[:, bass.ds(e, 1), k * D:(k + 1) * D].rearrange("p a n -> p (a n)")
                    last = pe.matmul(ps[:, 4 + p, 0:D], hidT[p][:, k, :], w, start=(k == 0), stop=(k == 3))
                last.then_inc(s_down_mm, 1)

            in_tile(16, 0, 0)
            in_tile(16, 1, 1)
            up(0, 0)
            up(1, 1)
            turn_hid(0, 0)
            in_tile(32, 2, 0)
            down(0, 0, True)
            up(2, 0)
            turn_hid(1, 1)
            in_tile(32, 3, 1)
            down(1, 1, True)
            with pe.Fori(0, SLOT_TILES // 2 - 2) as i:
                for p in range(2):
                    t = 2 * i + (2 + p)
                    up(t + 1, 1 - p)
                    turn_hid(t, p)
                    in_tile(16 * i + 48, t + 2, p)
                    down(t, p, False)
            t = SLOT_TILES - 2
            up(t + 1, 1)
            turn_hid(t, 0)
            down(t, 0, False)
            turn_hid(t + 1, 1)
            down(t + 1, 1, False)

            def rotate(j, p, peeled):
                pe.wait_ge(s_mix, j + 1)
                if not peeled:
                    pe.wait_ge(s_mT_cp, j)
                for c in range(2):
                    for u, at in ((2, 0), (0, PROWS), (1, PROWS + 128)):
                        n = ROWS[u]
                        last = pe.transpose(ps[:, c, at:at + n], moe[p][0:n, u, c * 128:(c + 1) * 128],
                                            ident[0:n, 0:n])
                last.then_inc(s_m_tr, 1)
                pe.wait_ge(s_mT_cp, j + 1)
                if not peeled:
                    pe.wait_ge(s_mr_ev, j)
                for u, at in ((0, PROWS), (1, PROWS + 128), (2, 0)):
                    n = ROWS[u]
                    last = acc(ps[0:n, 2 + u, 0:D], [(moeT[p][:, k, at:at + n], R[:, k, :]) for k in range(2)])
                last.then_inc(s_mr_mm, 1)

            rotate(0, 0, True)
            rotate(1, 1, False)
            with pe.Fori(0, PAIRS // 2 - 1) as i:
                for p in range(2):
                    rotate(2 * i + (2 + p), p, False)

        @block.scalar
        def _(act):
            step = Chain(act, s_act_step)
            act.preload_act_table_set("natural_log_exp_and_others")

            def copy(o, i_):
                return act.activation(o, i_, ACT.Copy)

            def norm_scale(var_ready, rs_ready, a, ch):
                act.wait_ge(var_ready, a + 1)
                ch(act.activation(lnv[:], veps[:], ACT.Ln))
                act.activation(rstd[:], lnv[:], ACT.Exp, scale=-0.5).then_inc(rs_ready, 1)

            def embed(a):
                act.wait_ge(s_emb_mm, a + 1)
                copy(embT, ps[:, 4, 0:2 * PROWS].rearrange("p (c n) -> p c n", c=2)).then_inc(s_emb_cp, 1)

            def x_out(a):
                act.wait_ge(s_x_tr, a + 1)
                dst = xT.rearrange("p c (b n) -> p c b n", b=2)
                copy(dst[:, :, :, 0:NPATCH],
                     ps[:, 4:6, 0:PROWS].rearrange("p c (b n) -> p c b n", b=2))
                copy(dst[:, :, :, NPATCH:NQ],
                     ps[:, 4:6, PROWS:TP].rearrange("p c (b n) -> p c b n", b=2)).then_inc(s_xT_cp, 1)

            def lat_out(a):
                act.wait_ge(s_lat_mm, a + 1)
                copy(lat, ps[:, 4:6, 0:TP]).then_inc(s_lat_cp, 1)

            def q_out(a, p):
                for half in range(2):
                    act.wait_ge(s_q_mm, 2 * a + half + 1)
                    copy(qT[p][:, 2 * half:2 * half + 2, :], ps[:, 4 + 2 * half:6 + 2 * half, 0:TP]).then_inc(s_q_cp, 1)

            def v_out(a, p):
                act.wait_ge(s_v_mm, a + 1)
                copy(Vt[p][:, :, 0:HEADS * VW].rearrange("p b (h d) -> p b h d", d=VW)[:, :, :, 0:HD],
                     ps[:, 4, :].rearrange("p (b h d) -> p b h d", b=2, d=HD))
                copy(Vp[p][0:NPATCH, :, 0:HEADS * VW].rearrange("p b (h d) -> p b h d", d=VW)[:, :, :, 0:HD],
                     ps[0:NPATCH, 5, :].rearrange("p (b h d) -> p b h d", b=2, d=HD)).then_inc(s_v_cp, 1)

            def probs(n, rp):
                act.wait_ge(s_shifted, n + 1)
                act.activation(Pt[rp], Pt[rp], ACT.Exp, scale=0.25)
                act.activation(Pp[rp], Pp[rp], ACT.Exp, scale=0.25).then_inc(s_probs, 1)

            def pt_out(q, gp):
                act.wait_ge(s_p_tr, q + 1)
                copy(PTt[gp], ps[:, 4, :].rearrange("p (i n) -> p i n", i=4)).then_inc(s_pt_txt, 1)

            def y_out(q, gp, p, b, g):
                act.wait_ge(s_pv, q + 1)
                copy(yTs[p][:, g, b * NPATCH:(b + 1) * NPATCH], ps[:, 6 + gp, 0:NPATCH])
                copy(yTs[p][:, g, PROWS + b * 128:PROWS + (b + 1) * 128],
                     ps[:, 6 + gp, NPATCH:NQ]).then_inc(s_yt, 1)

            act.wait_ge(s_ones_set, 1)
            embed(0)
            norm_scale(s_ln1_var, s_ln1_rs, 0, step)
            x_out(0)
            lat_out(0)
            q_out(0, 0)
            v_out(0, 0)

            def round_(j, k, par, first, last):
                n, a, c, q = 4 * j + k, j + 1, j - 1, 8 * j + 2 * k - 2
                no_prev = first and k == 0
                prev_par = par if k else 1 - par
                pb, ph = ((k - 1) % 4) // 2, (k - 1) % 2
                if not no_prev:
                    pt_out(q, 0)
                if k == 0 and not last:
                    embed(a)
                    norm_scale(s_ln1_var, s_ln1_rs, a, step)
                if k == 1 and not first:
                    norm_scale(s_ln2_var, s_ln2_rs, c, step)
                if k == 2:
                    if not last:
                        x_out(a)
                    if not first:
                        norm_scale(s_ln3_var, s_ln3_rs, c, step)
                if k == 3:
                    if not last:
                        lat_out(a)
                    if not first:
                        act.wait_ge(s_xn_tr, c + 1)
                        copy(xnT, ps[:, 6:8, 0:TP]).then_inc(s_xnT_cp, 1)
                    if not last:
                        q_out(a, 1 - par)
                        v_out(a, 1 - par)
                if not no_prev:
                    pt_out(q + 1, 1)
                probs(n, k % 2)
                if not no_prev:
                    y_out(q, 0, prev_par, pb, 2 * ph)
                    y_out(q + 1, 1, prev_par, pb, 2 * ph + 1)

            def pair(j, par, first, last):
                if first:
                    step.loop(1)
                elif last:
                    step.loop(3 * (PAIRS - 1) - 1)
                else:
                    step.loop(3 * j - 1)
                for k in range(4):
                    round_(j, k, par, first, last)
                assert step.n == (1 if first else 2 if last else 3)

            pair_loop(act, pair)
            n = 4 * PAIRS
            q = 2 * n - 2
            for gp in range(2):
                pt_out(q + gp, gp)
                y_out(q + gp, gp, (PAIRS - 1) % 2, 1, 2 + gp)
            c = PAIRS - 1
            norm_scale(s_ln2_var, s_ln2_rs, c, step)
            norm_scale(s_ln3_var, s_ln3_rs, c, step)
            act.wait_ge(s_xn_tr, c + 1)
            copy(xnT, ps[:, 6:8, 0:TP]).then_inc(s_xnT_cp, 1)

            act.wait_ge(s_gap_ready, 1)
            act.activation(wt2[:], m2[:], ACT.Exp).then_inc(s_gates, 1)

            for g in range(3):
                act.wait_ge(s_sqT_mm, g + 1)
                copy(EXT[:, g], ps[:, 3 + g, :].rearrange("p (k n) -> p k n", k=2)).then_inc(s_sqT_cp, 1)
            squarings = act.value_load(expo[0:1, 1:2], min_val=1, max_val=126)
            with act.Fori(0, squarings) as i:
                for g in range(3):
                    act.wait_ge(s_sqT_mm, 3 * i + (g + 4))
                    copy(EXT[:, g], ps[:, 3 + g, :].rearrange("p (k n) -> p k n", k=2)).then_inc(s_sqT_cp, 1)

            act.wait_ge(s_ag_ev, PAIRS)
            act.activation(pre_all[:, :, 0:D], pre_all[:, :, 0:D], ACT.Gelu).then_inc(s_abel_done, 1)

            def tokT_out(t, p, peeled):
                act.wait_ge(s_tok_tr, t + 1)
                if not peeled:
                    act.wait_ge(s_up_mm, t - 1)
                copy(tokT[p], ps[:, 0, 0:D].rearrange("p (c n) -> p c n", c=2)).then_inc(s_tokT_cp, 1)

            def gelu(t, p, peeled):
                act.wait_ge(s_up_ev, t + 1)
                if not peeled:
                    act.wait_ge(s_hid_tr, t - 1)
                act.activation(hid[p], pre[p], ACT.Gelu).then_inc(s_gelu, 1)

            def hidT_out(t, p, peeled):
                act.wait_ge(s_hid_tr, t + 1)
                if not peeled:
                    act.wait_ge(s_down_mm, t - 1)
                copy(hidT[p], ps[:, 3, :].rearrange("p (c n) -> p c n", c=4)).then_inc(s_hidT_cp, 1)

            def store(t, p):
                act.wait_ge(s_eo_ready, t + 1)
                act.dma_start(eod[bass.ds(t * 128, 128), :], eo[p]).then_inc((s_eo_st0, s_eo_st1)[p], 16)

            tokT_out(0, 0, True)
            tokT_out(1, 1, True)
            gelu(0, 0, True)
            gelu(1, 1, True)
            hidT_out(0, 0, True)
            tokT_out(2, 0, False)
            gelu(2, 0, False)
            hidT_out(1, 1, True)
            tokT_out(3, 1, False)
            store(0, 0)
            store(1, 1)
            with act.Fori(0, SLOT_TILES // 2 - 2) as i:
                for p in range(2):
                    t = 2 * i + (2 + p)
                    gelu(t + 1, 1 - p, False)
                    hidT_out(t, p, False)
                    tokT_out(t + 2, p, False)
                    store(t, p)
            t = SLOT_TILES - 2
            gelu(t + 1, 1, False)
            hidT_out(t, 0, False)
            store(t, 0)
            hidT_out(t + 1, 1, False)
            store(t + 1, 1)

            def rotated(j, p):
                act.wait_ge(s_m_tr, j + 1)
                copy(moeT[p], ps[:, 0:2, 0:TP]).then_inc(s_mT_cp, 1)
                act.wait_ge(s_z_ready, j + 1)
                act.activation(zg[:, 3 * p:3 * p + 3], zg[:, 3 * p:3 * p + 3], ACT.Exp, scale=-1.0).then_inc(s_z_exp, 1)

            with act.Fori(0, PAIRS // 2) as i:
                for p in range(2):
                    rotated(2 * i + p, p)

        @block.vector
        def _(dve):
            step = Chain(dve, s_dve_step)
            dve.wait_ge(s_prep_mm, 1)
            dve.tensor_copy(p_g, ps[:, 4, 0:128]).then_inc(s_prep_cp, 1)
            dve.wait_ge(s_prep_mm, 2)
            dve.tensor_copy(ve, ps[:, 5, 0:D]).then_inc(s_prep_cp, 1)
            dve.wait_ge(s_prep_mm, 3)
            dve.tensor_copy(ket, ps[:, 6, :]).then_inc(s_prep_cp, 1)
            dve.wait_ge(s_ones_set, 1)

            def spread(src, var_ready):
                dve.memset(carry[:, 0:1], 0.0)
                for u in range(3):
                    last = dve.bn_stats(stats[0:ROWS[u], u, :], src(u))
                step(last)
                dve.memset(carry[:, 1:2], 0.0)
                for u in range(3):
                    last = dve.bn_aggr(mv[0:ROWS[u], u, :], stats[0:ROWS[u], u, :])
                step(last)
                dve.tensor_scalar(veps[:], mv[:, :, 1], EPS, None, ALU.add).then_inc(var_ready, 1)

            def refine(rs_ready, a):
                dve.wait_ge(rs_ready, a + 1)
                step(dve.scalar_tensor_tensor(out=nt1[:], in0=rstd[:], scalar=-0.5, in1=rstd[:], op0=ALU.mult, op1=ALU.mult))
                step(dve.tensor_tensor(nt2[:], nt1[:], veps[:], ALU.mult))
                step(dve.scalar_tensor_tensor(out=rstd[:], in0=nt2[:], scalar=1.5, in1=rstd[:], op0=ALU.add, op1=ALU.mult))

            def normalise(dst, src):
                for u in range(3):
                    n = ROWS[u]
                    last = dve.tensor_scalar(dst[0:n, u, :], src(u), mv[0:n, u, 0:1], rstd[0:n, u:u + 1],
                                             ALU.subtract, ALU.mult)
                return last

            def embed(a):
                dve.wait_ge(s_emb_tr, a + 1)
                dve.tensor_copy(tile3(h_all, a, 2), ps[0:PROWS, 5, 0:D]).then_inc(s_emb_ev, 1)
                dve.wait_ge(s_emb_ev, a + 1)
                spread(lambda u: tile3(h_all, a, u), s_ln1_var)
                refine(s_ln1_rs, a)
                normalise(xw, lambda u: tile3(h_all, a, u)).then_inc(s_x_ready, 1)

            def k_out(a, p):
                for half in range(2):
                    dve.wait_ge(s_k_mm, 2 * a + half + 1)
                    dve.tensor_copy(kT[p][:, 2 * half:2 * half + 2, :], ps[:, 4 + 2 * half:6 + 2 * half, 0:TP]).then_inc(s_k_cp, 1)

            def shift(n, rp):
                dve.wait_ge(s_scores, n + 1)
                st = ps[:, 0:4, 0:2 * NQ].rearrange("p i (g n) -> p i g n", g=2)
                sp_ = ps[0:NPATCH, 0:4, 2 * NQ:2 * NQ + 2 * NPATCH].rearrange("p i (g n) -> p i g n", g=2)
                dve.tensor_reduce(mx[:], st, AX, ALU.max)
                step(dve.tensor_reduce(mxp[:], sp_, AX, ALU.max))
                dve.tensor_tensor(Pt[rp], st, mx[:].unsqueeze(3).to_broadcast([128, 4, 2, NQ]), ALU.subtract)
                dve.tensor_tensor(Pp[rp], sp_, mxp[:].unsqueeze(3).to_broadcast([NPATCH, 4, 2, NPATCH]),
                                  ALU.subtract).then_inc(s_shifted, 1)

            def pt_out(q, gp):
                dve.wait_ge(s_p_tr, q + 1)
                dve.tensor_copy(PTp[gp][:, :, NPATCH:NQ], ps[0:NPATCH, 5, :].rearrange("p (i n) -> p i n", i=4))
                dve.tensor_copy(PTp[gp][:, :, 0:NPATCH],
                                ps[0:NPATCH, 6 + gp, 0:4 * NPATCH].rearrange("p (i n) -> p i n", i=4)).then_inc(s_pt_patch, 1)

            def add_attention(c):
                dve.wait_ge(s_y_tr, c + 1)
                for u in range(3):
                    n = ROWS[u]
                    y = ps[0:n, 4 + u, :].rearrange("p (h d) -> p h d", d=32)
                    step(dve.reciprocal(rec[0:n, :], y[:, :, HD]))
                    o = ysum[0:n, :].rearrange("p (h d) -> p h d", d=HD)
                    last = dve.tensor_tensor(o, y[:, :, 0:HD], rec[0:n, :].unsqueeze(2).to_broadcast([n, HEADS, HD]), ALU.mult)
                    if u < 2:
                        step(last)
                    else:
                        last.then_inc(s_y_ev, 1)
                        dve.wait_ge(s_y_ev, c + 1)
                    step(dve.tensor_tensor(tile3(h_all, c, u), tile3(h_all, c, u), ysum[0:n, :], ALU.add))
                spread(lambda u: tile3(h_all, c, u), s_ln2_var)
                refine(s_ln2_rs, c)
                normalise(x2w, lambda u: tile3(h_all, c, u)).then_inc(s_x2_ready, 1)

            def second_norm(c):
                dve.wait_ge(s_x2_ready, c + 1)
                spread(lambda u: x2w[0:ROWS[u], u, :], s_ln3_var)
                refine(s_ln3_rs, c)
                dve.wait_ge(s_h_res, c + 1)
                normalise(x2w, lambda u: x2w[0:ROWS[u], u, :]).then_inc(s_x3_ready, 1)

            def ag_out(c):
                dve.wait_ge(s_ag_mm, c + 1)
                for u, bank in ((0, 6), (1, 7), (2, 5)):
                    n = ROWS[u]
                    last = dve.tensor_tensor(tile3(pre_all, c, u), ps[0:n, bank, 0:D + E], agb[0:n, :], ALU.add)
                last.then_inc(s_ag_ev, 1)

            dve.wait_ge(s_gath0, 32)
            embed(0)
            k_out(0, 0)

            def round_(j, k, par, first, last):
                n, a, c, q = 4 * j + k, j + 1, j - 1, 8 * j + 2 * k - 2
                no_prev = first and k == 0
                if not no_prev:
                    pt_out(q, 0)
                if k == 0 and not last:
                    if first:
                        dve.wait_ge(s_gath, 16 * (NB - 2))
                        dve.wait_ge(s_ld_ffn, 80)
                    embed(a)
                if k == 1 and not first:
                    add_attention(c)
                if k == 2 and not first:
                    second_norm(c)
                if k == 3:
                    if not last:
                        k_out(a, 1 - par)
                    if not first:
                        ag_out(c)
                if not no_prev:
                    pt_out(q + 1, 1)
                shift(n, k % 2)

            A_STEPS, C_STEPS = 5, 8 + 5 + 5
            PER = A_STEPS + C_STEPS + 4

            def pair(j, par, first, last):
                if first:
                    step.loop(A_STEPS)
                elif last:
                    step.loop(A_STEPS + (A_STEPS + 4) + PER * (PAIRS - 2))
                else:
                    step.loop(PER * j + (A_STEPS + (A_STEPS + 4) - PER))
                for k in range(4):
                    round_(j, k, par, first, last)
                assert step.n == (A_STEPS + 4 if first else C_STEPS + 4 if last else PER), step.n

            pair_loop(dve, pair)
            n = 4 * PAIRS
            q = 2 * n - 2
            for gp in range(2):
                pt_out(q + gp, gp)
            c = PAIRS - 1
            add_attention(c)
            second_norm(c)
            ag_out(c)

            dve.wait_ge(s_ld_route, 64)
            dve.wait_ge(s_ag_ev, PAIRS)
            logits = pre_all[:, :, D:D + E]
            def bt(x):
                return x[:].unsqueeze(2).to_broadcast(TE)
            def be(x):
                return x[:].unsqueeze(1).to_broadcast(TE)

            def first_best(src, m, e, oh):
                step(dve.tensor_reduce(m[:], src, AX, ALU.max))
                step(dve.tensor_tensor(r2[:], src, bt(m), ALU.is_equal))
                step(dve.tensor_tensor(r2[:], r2[:], be(em8), ALU.mult))
                step(dve.tensor_reduce(e[:], r2[:], AX, ALU.min))
                step(dve.tensor_tensor(oh[:], bt(e), be(em8), ALU.is_equal))

            first_best(logits, m1, e1, oh1)
            step(dve.scalar_tensor_tensor(out=r1[:].rearrange("p t e -> p (t e)"),
                                          in0=oh1[:].rearrange("p t e -> p (t e)"), scalar=-3.0e38,
                                          in1=oh1[:].rearrange("p t e -> p (t e)"), op0=ALU.mult, op1=ALU.mult))
            step(dve.tensor_tensor(r1[:], r1[:], logits, ALU.add))
            first_best(r1[:], m2, e2, oh2)
            step(dve.tensor_tensor(msum[:], oh1[:], oh2[:], ALU.add))
            dve.tensor_tensor(msum[:], msum[:], bt(valid), ALU.mult).then_inc(s_rt_m, 1)
            dve.tensor_tensor(m2[:], m2[:], m1[:], ALU.subtract).then_inc(s_gap_ready, 1)
            dve.wait_ge(s_rt_mm, 1)
            dve.wait_ge(s_rt_m, 1)
            ps7 = ps[:, 7, 0:TILES * E].rearrange("p (t e) -> p t e", e=E)
            ps6 = ps[:, 6, 0:TILES * E].rearrange("p (t e) -> p t e", e=E)
            step(dve.tensor_copy(r1[:], ps7))
            src, dst = r1, r2
            sh = 1
            while sh < TILES:
                dve.tensor_copy(dst[:, 0:sh, :], src[:, 0:sh, :])
                step(dve.tensor_tensor(dst[:, sh:, :], src[:, sh:, :], src[:, 0:TILES - sh, :], ALU.add))
                src, dst = dst, src
                sh *= 2
            step(dve.tensor_copy(cnti[:], src[:, TILES - 1, :]))
            step(dve.tensor_scalar(cnti[:], cnti[:], 127, None, ALU.add))
            step(dve.tensor_scalar(cnti[:], cnti[:], 7, 7, ALU.arith_shift_right, ALU.logical_shift_left))
            step(dve.tensor_copy(cnt[:], cnti[:]))
            step(dve.tensor_tensor_scan(endb[:], ones[:, 0:E], cnt[:], 0.0, ALU.mult, ALU.add))
            step(dve.tensor_tensor(base[:], endb[:], cnt[:], ALU.subtract))
            step(dve.tensor_tensor(src[:], src[:], ps7, ALU.subtract))
            step(dve.tensor_tensor(src[:], src[:], ps6, ALU.add))
            step(dve.tensor_tensor(src[:], src[:], be(base), ALU.add))
            for k, oh in ((0, oh1), (1, oh2)):
                step(dve.tensor_tensor(dst[:], src[:], oh[:], ALU.mult))
                step(dve.tensor_reduce((e1, e2)[k][:], dst[:], AX, ALU.add))
                step(dve.tensor_copy(slots[k][:], (e1, e2)[k][:]))
            CE = [128, SLOT_TILES, E - 1]
            step(dve.tensor_tensor(cmp[:], slot0[:].unsqueeze(2).to_broadcast(CE),
                                   endb[:, 0:E - 1].unsqueeze(1).to_broadcast(CE), ALU.is_ge))
            step(dve.tensor_reduce(exf[:], cmp[:], AX, ALU.add))
            dve.tensor_copy(exi[:], exf[:]).then_inc(s_slots_ready, 1)
            dve.wait_ge(s_gates, 1)
            step(dve.tensor_scalar(m1[:], wt2[:], 1.0, None, ALU.add))
            step(dve.reciprocal(wt1[:], m1[:]))
            step(dve.tensor_tensor(wt2[:], wt2[:], wt1[:], ALU.mult))

            dve.wait_ge(s_ld_gens, 32)
            step(dve.tensor_reduce(rows[:, 0:6].rearrange("p (g k) -> p g k", g=3), X, AX, ALU.add,
                                   apply_absolute_value=True))
            dve.tensor_reduce(rows[:, 6:7], rows[:, 0:6], AX, ALU.max).then_inc(s_norm_part, 1)
            dve.wait_ge(s_norm_all, 1)
            step(dve.tensor_scalar(expo[:, 0:1], rows[:, 7:8].bitcast(I32), 23, None, ALU.logical_shift_right))
            step(dve.tensor_scalar(expo[:, 1:2], expo[:, 0:1], -124, 1, ALU.add, ALU.max))
            step(dve.tensor_scalar(expo[:, 2:3], expo[:, 1:2], -1, 127, ALU.mult, ALU.add))
            step(dve.tensor_scalar(rows[:, 6:7].bitcast(I32), expo[:, 2:3], 23, None, ALU.logical_shift_left))
            fl = lambda t: t.rearrange("p g k n -> p (g k n)")
            dve.tensor_scalar(fl(X), fl(X), rows[:, 6:7], None, ALU.mult)
            dve.memset(ident2, 0.0)
            step(dve.tensor_scalar(fl(XT), fl(XT), rows[:, 6:7], None, ALU.mult))
            for k in range(2):
                last = dve.tensor_copy(ident2[:, k, k * 128:(k + 1) * 128], ident[:])
            step(last)
            step(dve.tensor_scalar(fl(EX), fl(X), 1.0 / FACT[TERMS], None, ALU.mult))
            for g in range(3):
                last = dve.scalar_tensor_tensor(out=EX[:, g], in0=ident2, scalar=1.0 / FACT[TERMS - 1], in1=EX[:, g],
                                                op0=ALU.mult, op1=ALU.add)
            last.then_inc(s_x_scaled, 1)
            for d in range(TERMS - 1):
                for g in range(3):
                    dve.wait_ge(s_hr_mm, 3 * d + g + 1)
                    src_ = ps[:, g, :].rearrange("p (k n) -> p k n", k=2)
                    if d < TERMS - 2:
                        ins_ = dve.scalar_tensor_tensor(out=EX[:, g], in0=ident2, scalar=1.0 / FACT[TERMS - 2 - d],
                                                        in1=src_, op0=ALU.mult, op1=ALU.add)
                    else:
                        ins_ = dve.tensor_copy(EX[:, g], src_)
                    ins_.then_inc(s_hr_ev, 1)
            squarings = dve.value_load(expo[0:1, 1:2], min_val=1, max_val=126)
            dve.wait_ge(s_hr_ev, 3 * (TERMS - 1))
            with dve.Fori(0, squarings) as i:
                for g in range(3):
                    dve.wait_ge(s_sq_mm, 3 * i + g + 1)
                    dve.wait_ge(s_sqT_mm, 3 * i + 3)
                    dve.scalar_tensor_tensor(out=EX[:, g], in0=EX[:, g], scalar=2.0,
                                             in1=ps[:, g, :].rearrange("p (k n) -> p k n", k=2),
                                             op0=ALU.mult, op1=ALU.add).then_inc(s_sq_ev, 1)
                dve.wait_ge(s_sq_ev, 3 * i + 3)
            dve.wait_ge(s_sqT_cp, 3 * squarings + 3)
            for g in range(3):
                dve.tensor_tensor(EX[:, g], EX[:, g], ident2, ALU.add)
                last = dve.tensor_tensor(EXT[:, g], EXT[:, g], ident2, ALU.add)
            last.then_inc(s_fin_ready, 1)
            dve.wait_ge(s_rmul, 1)
            dve.tensor_copy(EX[:, 1], ps[:, 0, :].rearrange("p (k n) -> p k n", k=2)).then_inc(s_rmul_ev, 1)
            dve.wait_ge(s_rmul, 2)
            dve.tensor_copy(R[:], ps[:, 1, :].rearrange("p (k n) -> p k n", k=2)).then_inc(s_fin_ready, 1)

            dve.wait_ge(s_abel_done, 1)
            dve.wait_ge(s_fin_ready, 2)
            for t in range(TILES):
                step(dve.tensor_tensor_reduce(ysum[:], pre_all[:, t, 0:D], gcw[:, 0:D], 1.0, 0.0, ALU.mult, ALU.add,
                                              zab[:, t:t + 1]))

            def up_out(t, p, peeled):
                e = dve.value_load(exi[0:1, bass.ds(t, 1)], min_val=0, max_val=E - 1)
                dve.wait_ge(s_up_mm, t + 1)
                if not peeled:
                    dve.wait_ge(s_gelu, t - 1)
                dve.tensor_tensor(pre[p], ps[:, 1 + p, :], eb1[:, bass.ds(e, 1), :].rearrange("p a n -> p (a n)"),
                                  ALU.add).then_inc(s_up_ev, 1)

            def down_out(t, p, stored):
                e = dve.value_load(exi[0:1, bass.ds(t, 1)], min_val=0, max_val=E - 1)
                dve.wait_ge(s_down_mm, t + 1)
                if stored is not None:
                    dve.wait_ge((s_eo_st0, s_eo_st1)[p], stored)
                dve.tensor_tensor(eo[p], ps[:, 4 + p, 0:D], eb2[:, bass.ds(e, 1), :].rearrange("p a n -> p (a n)"),
                                  ALU.add).then_inc(s_eo_ready, 1)

            dve.wait_ge(s_ld_exp, 16 * (2 * E + 2))
            up_out(0, 0, True)
            up_out(1, 1, True)
            down_out(0, 0, None)
            up_out(2, 0, False)
            down_out(1, 1, None)
            with dve.Fori(0, SLOT_TILES // 2 - 2) as i:
                for p in range(2):
                    t = 2 * i + (2 + p)
                    up_out(t + 1, 1 - p, False)
                    down_out(t, p, 16 * i + 16)
            t = SLOT_TILES - 2
            up_out(t + 1, 1, False)
            down_out(t, 0, 16 * (t // 2))
            down_out(t + 1, 1, 16 * (t // 2))

            mixbase = step.n + step.base if isinstance(step.base, int) else None
            sel = lambda x, j, u: x[0:ROWS[u], bass.ds(3 * j + u, 1)]

            def mix(j, p, b0):
                step.loop(b0)
                for u in range(3):
                    n = ROWS[u]
                    last = dve.tensor_scalar(moe[p][0:n, u, :], tile3(G[0], j, u), sel(wt1, j, u), None, ALU.mult)
                step(last)
                for u in range(3):
                    n = ROWS[u]
                    last = dve.scalar_tensor_tensor(out=moe[p][0:n, u, :], in0=tile3(G[1], j, u), scalar=sel(wt2, j, u),
                                                    in1=moe[p][0:n, u, :], op0=ALU.mult, op1=ALU.add)
                last.then_inc(s_mix, 1)
                dve.wait_ge(s_mr_mm, j + 1)
                z3 = zg[:, 3 * p:3 * p + 3]
                for u in range(3):
                    n = ROWS[u]
                    last = dve.tensor_copy(mo[p][0:n, u, :], ps[0:n, 2 + u, 0:D])
                last.then_inc(s_mr_ev, 1)
                dve.wait_ge(s_mr_ev, j + 1)
                for u in range(3):
                    n = ROWS[u]
                    last = dve.tensor_tensor_reduce(junk[0:n, :], mo[p][0:n, u, :], gcw[0:n, D:2 * D], 1.0, 0.0,
                                                    ALU.mult, ALU.add, zmo[0:n, u:u + 1])
                    step(last)
                step(dve.tensor_tensor(z3, zmo[:, 0:3], zab[:, bass.ds(3 * j, 3)], ALU.add))
                dve.tensor_scalar(z3, z3, gcb[:, 0:1], None, ALU.add).then_inc(s_z_ready, 1)
                for u in range(3):
                    n = ROWS[u]
                    ab = pre_all[0:n, bass.ds(3 * j + u, 1), 0:D].rearrange("p a d -> p (a d)")
                    dve.tensor_tensor(mo[p][0:n, u, :], mo[p][0:n, u, :], ab, ALU.subtract)
                    last = dve.tensor_tensor(res[p][0:n, u, :], tile3(h_all, j, u), ab, ALU.add)
                step(last)
                dve.wait_ge(s_z_exp, j + 1)
                step(dve.tensor_scalar(z3, z3, 1.0, None, ALU.add))
                step(dve.reciprocal(z3, z3))
                for u in range(3):
                    n = ROWS[u]
                    last = dve.scalar_tensor_tensor(out=res[p][0:n, u, :], in0=mo[p][0:n, u, :],
                                                    scalar=zg[0:n, 3 * p + u:3 * p + u + 1], in1=res[p][0:n, u, :],
                                                    op0=ALU.mult, op1=ALU.add)
                last.then_inc(s_res_ready, 1)

            MIX_STEPS = 8
            dve.memset(zmo[:, 0:3], 0.0)
            dve.wait_ge(s_back0, 16 * 12)
            mix(0, 0, mixbase)
            mix(1, 1, mixbase + MIX_STEPS)
            dve.wait_ge(s_back1, 16 * 12)
            dve.wait_ge(s_back2, 16 * 24)
            with dve.Fori(0, PAIRS // 2 - 1) as i:
                for p in range(2):
                    dve.wait_ge((s_out_st0, s_out_st1)[p], 64 * i + 64)
                    mix(2 * i + (2 + p), p, MIX_STEPS * 2 * i + (mixbase + MIX_STEPS * (2 + p)))
                    assert step.n == MIX_STEPS, step.n


def kernel(**inputs):
    import numpy as np
    import ml_dtypes
    import concourse.bacc as bacc
    from concourse.bass_utils import run_bass_kernel_spmd as run

    f = {k: np.asarray(v) for k, v in inputs.items()}
    c = np.ascontiguousarray

    def head_columns(w):
        o = np.zeros((w.shape[0], HEADS, 32), w.dtype)
        o[:, :, 0:HD] = w.reshape(w.shape[0], HEADS, HD)
        return o.reshape(w.shape[0], HEADS * 32)

    pat = f["x"].reshape(NB, 3, 6, 16, 6, 16).transpose(0, 1, 3, 5, 2, 4).reshape(NB, NPATCH, 768)
    pat = pat.transpose(2, 0, 1).reshape(768, NB * NPATCH)
    order = np.arange(128)
    mask = np.zeros((128, 2 * NQ + 2 * NPATCH), np.float32)
    low = np.float32(-1e30)
    later = order[None, :] > order[:, None]
    for g in range(2):
        mask[:, g * NQ + NPATCH:(g + 1) * NQ][later] = low
        mask[0:NPATCH, 2 * NQ + g * NPATCH:2 * NQ + (g + 1) * NPATCH][later[0:NPATCH, 0:NPATCH]] = low
    arrays = {
        "patches": c(pat), "ids": c(f["x_txt"].T), "wtok": f["L0_tok_W"], "txt_w": f["L0_txt_w"],
        "uq": f["L0_attn_W_uq"], "uk": f["L0_attn_W_uk"], "uv": f["L0_attn_W_uv"], "o_t": c(f["L0_attn_W_o"].T),
        "dq_t": c(f["L0_attn_W_dq"].T), "dkv_t": c(f["L0_attn_W_dkv"].T),
        "dq_pad": head_columns(f["L0_attn_W_dq"]), "uq_pad": head_columns(f["L0_attn_W_uq"].T),
        "ag": np.concatenate([f["L0_ffn_abel_w"], f["L0_ffn_moe_gate_w"]], axis=1),
        "ag_b": np.concatenate([f["L0_ffn_abel_b"], f["L0_ffn_moe_gate_b"]]),
        "gamma": f["L0_ffn_ln_gamma"], "beta": f["L0_ffn_ln_beta"],
        "gc_w": c(f["L0_ffn_gc_w"].reshape(-1)), "gc_b": f["L0_ffn_gc_b"],
        "ew1": f["L0_ffn_ew1"], "ew2": f["L0_ffn_ew2"], "eb1": f["L0_ffn_eb1"], "eb2": f["L0_ffn_eb2"],
        "gens": f["L0_ffn_gens"], "gens_t": c(f["L0_ffn_gens"].transpose(0, 2, 1)),
        "ident": np.eye(128, dtype=np.float32), "identb": np.eye(128).astype(ml_dtypes.bfloat16),
        "maskb": mask.astype(ml_dtypes.bfloat16),
        "valid": np.stack([(order < ROWS[t % 3]) for t in range(TILES)], 1).astype(np.float32),
        "tri": (order[:, None] < order[None, :]).astype(np.float32),
        "em8": np.tile(np.arange(E, dtype=np.float32) - 8, (128, 1)),
        "slot0": np.tile(128 * np.arange(SLOT_TILES, dtype=np.float32), (128, 1)),
    }
    nc = bacc.Bacc("TRN2", target_bir_lowering=False, num_devices=1)
    ins = {k: nc.dram_tensor("in_" + k, a.shape, mybir.dt.from_np(a.dtype), kind="ExternalInput").ap()
           for k, a in arrays.items()}
    out = nc.dram_tensor("out", (NB, NQ, D), F32, kind="ExternalOutput").ap()
    early_fusion_program(nc, ins, out)
    r = run(nc, [{"in_" + k: a for k, a in arrays.items()}], core_ids=[0])
    return r.results[0]["out"]
```

```python
from contextlib import ExitStack

import concourse.bass as bass
from concourse import mybir

F32 = mybir.dt.float32
BF16 = mybir.dt.bfloat16
I32 = mybir.dt.int32
ACT = mybir.ActivationFunctionType
ALU = mybir.AluOpType
AX = mybir.AxisListType.X
RMAX = bass.bass_isa.ReduceOp.max

NB, NPATCH, NTXT = 16, 36, 128
NQ = NPATCH + NTXT
PAIRS = NB // 2
TP = 2 * NQ
PROWS = 2 * NPATCH
ROWS = (128, 128, PROWS)
TILES = 3 * PAIRS
D = 256
FC = 768 // 128
HEADS, HD = 16, 16
VW = HD + 1
VROW = HEADS * VW + 16
E, HID = 8, 512
SLOT_TILES = (2 * NB * NQ + E * 127) // 128
EPS = 1e-5
SPARE = 2 * NQ + 2 * NPATCH
TERMS = 6
FACT = [1.0]
for _k in range(1, TERMS + 1):
    FACT.append(FACT[-1] * _k)


class Chain:

    def __init__(self, eng, sem):
        self.eng, self.sem, self.base, self.n = eng, sem, 0, 0

    def __call__(self, ins):
        ins.then_inc(self.sem, 1)
        self.n += 1
        self.eng.wait_ge(self.sem, self.base + self.n)

    def loop(self, base):
        self.base, self.n = base, 0


def early_fusion_program(nc, ins, out):
    ctx = ExitStack()
    with ctx:
        def sb(name, shape, dt=F32):
            return ctx.enter_context(nc.sbuf_tensor(name, shape, dt))

        def sem(name):
            return ctx.enter_context(nc.semaphore(name))

        h_all = sb("h_all", [128, TILES, D])
        pre_all = sb("pre_all", [128, TILES, D + E])
        xn_all = sb("xn_all", [128, TILES, D])
        ident = sb("ident", [128, 128])
        identb = sb("identb", [128, 128], BF16)
        maskb = sb("maskb", [128, 2 * NQ + 2 * NPATCH], BF16)
        gam = sb("gam", [128, D])
        bet = sb("bet", [128, D])
        agb = sb("agb", [128, D + E])
        gcw = sb("gcw", [128, 2 * D])
        gcb = sb("gcb", [128, 1])
        ids = sb("ids", [128, NB], I32)
        RG = D + 1
        R = sb("R", [128, 2, RG])

        AW = 29504
        arena = sb("arena", [128, AW])
        top = [0]

        def take(n, rows=128):
            a = top[0]
            top[0] += n
            assert top[0] <= AW, top[0]
            return arena[0:rows, a:a + n]

        wtok = take(FC * D).rearrange("p (c n) -> p c n", c=FC)
        patches = take(FC * NB * NPATCH).rearrange("p (c n) -> p c n", c=FC)
        xw = take(3 * D).rearrange("p (u d) -> p u d", u=3)
        xT = take(2 * TP).rearrange("p (c n) -> p c n", c=2)
        lat = take(2 * TP).rearrange("p (c n) -> p c n", c=2)
        qT = [take(4 * TP).rearrange("p (g n) -> p g n", g=4) for _ in range(2)]
        kT = [take(4 * TP).rearrange("p (g n) -> p g n", g=4) for _ in range(2)]
        Vt = [take(2 * VROW).rearrange("p (b n) -> p b n", b=2) for _ in range(2)]
        Vp = [take(2 * VROW).rearrange("p (b n) -> p b n", b=2) for _ in range(2)]
        Pt = [take(8 * NQ).rearrange("p (i g n) -> p i g n", i=4, g=2) for _ in range(2)]
        Pp = [take(8 * NPATCH, NPATCH).rearrange("p (i g n) -> p i g n", i=4, g=2) for _ in range(2)]
        PTt = [take(4 * NTXT).rearrange("p (i n) -> p i n", i=4) for _ in range(2)]
        PTp = [take(4 * NQ, NPATCH).rearrange("p (i n) -> p i n", i=4) for _ in range(2)]
        y_at = top[0]
        yTs = [take(4 * TP).rearrange("p (g n) -> p g n", g=4) for _ in range(2)]
        x2w = take(3 * D).rearrange("p (u d) -> p u d", u=3)
        x3w = take(3 * D).rearrange("p (u d) -> p u d", u=3)
        xnw = take(3 * D).rearrange("p (u d) -> p u d", u=3)
        xnT = take(2 * TP).rearrange("p (c n) -> p c n", c=2)
        wdq = take(2 * 128).rearrange("p (c n) -> p c n", c=2)
        wdkv = take(2 * 128).rearrange("p (c n) -> p c n", c=2)
        wuq = take(512)
        ket = take(512)
        ve = take(D)
        wag = take(2 * (D + E)).rearrange("p (c n) -> p c n", c=2)
        attn_end, top[0] = top[0], y_at
        p_uq = take(256).rearrange("p (c n) -> p c n", c=2)
        p_uk = take(256).rearrange("p (c n) -> p c n", c=2)
        p_dq = take(512)
        p_uv = take(256).rearrange("p (c n) -> p c n", c=2)
        p_o = take(512).rearrange("p (c n) -> p c n", c=2)
        p_g = take(128)
        assert top[0] <= y_at + 8 * TP

        top[0] = 0
        w1 = take(E * 2 * HID).rearrange("p (e n) -> p e n", e=E)
        w2 = take(E * 4 * D).rearrange("p (e n) -> p e n", e=E)
        eb1 = take(E * HID).rearrange("p (e n) -> p e n", e=E)
        eb2 = take(E * D).rearrange("p (e n) -> p e n", e=E)
        mark = top[0]
        X = take(3 * 2 * D).rearrange("p (g k n) -> p g k n", g=3, k=2)
        XT = take(3 * 2 * D).rearrange("p (g k n) -> p g k n", g=3, k=2)
        EX = take(3 * 2 * D).rearrange("p (g k n) -> p g k n", g=3, k=2)
        EXT = take(3 * 2 * D).rearrange("p (g k n) -> p g k n", g=3, k=2)
        ident2 = take(2 * D).rearrange("p (k n) -> p k n", k=2)
        top[0] = mark
        tok = [take(D) for _ in range(2)]
        tokT = [take(D).rearrange("p (c n) -> p c n", c=2) for _ in range(2)]
        pre = [take(HID) for _ in range(2)]
        hid = [take(HID) for _ in range(2)]
        hidT = [take(HID).rearrange("p (c n) -> p c n", c=4) for _ in range(2)]
        eo = [take(D) for _ in range(2)]
        top[0] = 0
        G = [take(TILES * D).rearrange("p (t d) -> p t d", t=TILES) for _ in range(2)]
        moe = [take(3 * D).rearrange("p (u d) -> p u d", u=3) for _ in range(2)]
        moeT = [take(2 * TP).rearrange("p (c n) -> p c n", c=2) for _ in range(2)]
        mo = [take(3 * D).rearrange("p (u d) -> p u d", u=3) for _ in range(2)]
        junk = take(D)
        res = [take(3 * D).rearrange("p (u d) -> p u d", u=3) for _ in range(2)]

        stats = sb("stats", [128, 3, 6])
        mv = sb("mv", [128, 3, 2])
        mv1 = sb("mv1", [128, TILES, 2])
        veps = sb("veps", [128, TILES])
        lnv = sb("lnv", [128, TILES])
        rstd1 = sb("rstd1", [128, TILES])
        rstd = sb("rstd", [128, 6])
        nt1 = sb("nt1", [128, TILES])
        nt2 = sb("nt2", [128, TILES])
        carry = sb("carry", [128, 2])
        mx = sb("mx", [128, 4, 2])
        mxp = sb("mxp", [NPATCH, 4, 2])
        rec = sb("rec", [128, 3, HEADS])
        ysum = sb("ysum", [128, 3, D])
        em8 = sb("em8", [128, E])
        valid = sb("valid", [128, TILES])
        slot0 = sb("slot0", [128, SLOT_TILES])
        tri = sb("tri", [128, 128])
        ones = sb("ones", [128, 128])
        TE = [128, TILES, E]
        r1, r2, oh1, oh2, msum = (sb(n, TE) for n in ("r1", "r2", "oh1", "oh2", "msum"))
        m1, m2, e1, e2, wt1, wt2, zab, zmo = (
            sb(n, [128, TILES]) for n in ("m1", "m2", "e1", "e2", "wt1", "wt2", "zab", "zmo"))
        cnt, base, endb = (sb(n, [128, E]) for n in ("cnt", "base", "endb"))
        cnti = sb("cnti", [128, E], I32)
        slots = [sb(f"slots{k}", [128, TILES], I32) for k in range(2)]
        cmp = ysum[:].rearrange("p u d -> p (u d)")[:, 0:SLOT_TILES * (E - 1)].rearrange("p (s e) -> p s e", e=E - 1)
        exf = sb("exf", [128, SLOT_TILES])
        exi = sb("exi", [128, SLOT_TILES], I32)
        rows = sb("rows", [128, 8])
        expo = sb("expo", [128, 4], I32)
        zg = sb("zg", [128, 8])

        ps = ctx.enter_context(nc.psum_tensor("ps", [128, 8, 512], F32))
        xg = nc.dram_tensor("xg", (SLOT_TILES * 128, D), F32, kind="Internal").ap()
        eod = nc.dram_tensor("eod", (SLOT_TILES * 128, D), F32, kind="Internal").ap()

        s_ld_attn = sem("ld_attn")
        s_ld_ids = sem("ld_ids")
        s_ld_gens = sem("ld_gens")
        s_ld_ffn = sem("ld_ffn")
        s_ld_exp = sem("ld_exp")
        s_ld_route = sem("ld_route")
        s_gath = sem("gath")
        s_pads = sem("pads")
        s_prep_mm = sem("prep_mm")
        s_prep_cp = sem("prep_cp")
        s_cleared = sem("cleared")
        s_ones_set = sem("ones_set")
        s_emb_mm = sem("emb_mm")
        s_emb_ev = sem("emb_ev")
        s_ln1_var = sem("ln1_var")
        s_ln1_rs = sem("ln1_rs")
        s_x_ready = sem("x_ready")
        s_x_tr = sem("x_tr")
        s_xT_cp = sem("xT_cp")
        s_lat_mm = sem("lat_mm")
        s_lat_cp = sem("lat_cp")
        s_q_mm = sem("q_mm")
        s_q_cp = sem("q_cp")
        s_k_mm = sem("k_mm")
        s_k_cp = sem("k_cp")
        s_v_mm = sem("v_mm")
        s_v_cp = sem("v_cp")
        s_scores = sem("scores")
        s_shifted = sem("shifted")
        s_probs = sem("probs")
        s_p_tr = sem("p_tr")
        s_pt_txt = sem("pt_txt")
        s_pt_patch = sem("pt_patch")
        s_pv = sem("pv")
        s_yt = sem("yt")
        s_y_tr = sem("y_tr")
        s_y_ev = sem("y_ev")
        s_ln2_var = sem("ln2_var")
        s_ln2_rs = sem("ln2_rs")
        s_x2_ready = sem("x2_ready")
        s_x3_ready = sem("x3_ready")
        s_xn_ready = sem("xn_ready")
        s_xn_tr = sem("xn_tr")
        s_xnT_cp = sem("xnT_cp")
        s_ag_mm = sem("ag_mm")
        s_ag_ev = sem("ag_ev")
        s_h_res = sem("h_res")
        s_xn_kept = sem("xn_kept")
        s_dve_step = sem("dve_step")
        s_act_step = sem("act_step")
        s_pool_step = sem("pool_step")
        s_norm_part = sem("norm_part")
        s_norm_all = sem("norm_all")
        s_x_scaled = sem("x_scaled")
        s_hr_mm = sem("hr_mm")
        s_hr_ev = sem("hr_ev")
        s_sq_mm = sem("sq_mm")
        s_sq_ev = sem("sq_ev")
        s_sqT_mm = sem("sqT_mm")
        s_sqT_cp = sem("sqT_cp")
        s_fin_ready = sem("fin_ready")
        s_rmul = sem("rmul")
        s_rmul_ev = sem("rmul_ev")
        s_rt_m = sem("rt_m")
        s_rt_mm = sem("rt_mm")
        s_slots_ready = sem("slots_ready")
        s_gap_ready = sem("gap_ready")
        s_gates = sem("gates")
        s_sent = sem("sent")
        s_tok_ld0 = sem("tok_ld0")
        s_tok_ld1 = sem("tok_ld1")
        s_tok_tr = sem("tok_tr")
        s_tokT_cp = sem("tokT_cp")
        s_up_mm = sem("up_mm")
        s_up_ev = sem("up_ev")
        s_gelu = sem("gelu")
        s_hid_tr = sem("hid_tr")
        s_hidT_cp = sem("hidT_cp")
        s_down_mm = sem("down_mm")
        s_eo_ready = sem("eo_ready")
        s_eo_st0 = sem("eo_st0")
        s_eo_st1 = sem("eo_st1")
        s_abel_done = sem("abel_done")
        s_back0 = sem("back0")
        s_back1 = sem("back1")
        s_r_wide = sem("r_wide")
        s_mix = sem("mix")
        s_m_tr = sem("m_tr")
        s_mT_cp = sem("mT_cp")
        s_mr_mm = sem("mr_mm")
        s_mr_ev = sem("mr_ev")
        s_z_ready = sem("z_ready")
        s_z_exp = sem("z_exp")
        s_res_ready = sem("res_ready")
        s_out_st0 = sem("out_st0")
        s_out_st1 = sem("out_st1")

        block = ctx.enter_context(nc.Block())

        def after(eng, sem_, count):
            if not (isinstance(count, int) and count <= 0):
                eng.wait_ge(sem_, count)

        def tile3(t3, expr, u):
            return t3[0:ROWS[u], bass.ds(3 * expr + u, 1), :].rearrange("p a d -> p (a d)")

        def texts(t3, expr):
            return t3[:, bass.ds(3 * expr, 2), :]

        def pair_loop(eng, body):
            body(0, 0, True, False)
            with eng.Fori(0, (PAIRS - 2) // 2) as i:
                for u in range(2):
                    body(2 * i + (1 + u), (1 + u) % 2, False, False)
            body(PAIRS - 1, (PAIRS - 1) % 2, False, True)

        @block.sync
        def _(sp):
            sp.dma_start(ids[:], ins["ids"]).then_inc(s_ld_ids, 16)
            sp.dma_start(ident[:], ins["ident"]).then_inc(s_ld_attn, 16)
            sp.dma_start(patches, ins["patches"].rearrange("(c p) n -> p c n", p=128)).then_inc(s_ld_attn, 16)
            sp.dma_start(wtok, ins["wtok"].rearrange("(c p) n -> p c n", p=128)).then_inc(s_ld_attn, 16)
            for dst, name in ((p_uq, "uq"), (p_uk, "uk"), (p_uv, "uv"), (p_o, "o_t"), (wdq, "dq_t"),
                              (wdkv, "dkv_t"), (wag, "ag")):
                sp.dma_start(dst, ins[name].rearrange("(c p) n -> p c n", p=128)).then_inc(s_ld_attn, 16)
            for dst, name in ((p_dq, "dq_pad"), (wuq, "uq_pad"), (identb[:], "identb"), (maskb[:], "maskb")):
                sp.dma_start(dst, ins[name]).then_inc(s_ld_attn, 16)
            for dst, name in ((gam, "gamma"), (bet, "beta"), (agb, "ag_b"), (gcw, "gc_w"), (gcb, "gc_b")):
                sp.dma_start(dst[:], ins[name].partition_broadcast(128)).then_inc(s_ld_ffn, 16)
            for dst, name in ((valid, "valid"), (tri, "tri"), (em8, "em8"), (slot0, "slot0")):
                sp.dma_start(dst[:], ins[name]).then_inc(s_ld_route, 16)
            sp.wait_ge(s_cleared, 1)
            zero = xn_all[:, :, :]
            for c in range(SLOT_TILES // TILES):
                sp.dma_start(xg[c * TILES * 128:(c + 1) * TILES * 128, :].rearrange("(t p) d -> p t d", p=128),
                             zero).then_inc(s_pads, 16)
            sp.wait_ge(s_ag_ev, PAIRS + 1)
            sp.wait_ge(s_xn_kept, PAIRS)
            sp.dma_start(X, ins["gens"].rearrange("g (k p) n -> p g k n", p=128)).then_inc(s_ld_gens, 16)
            sp.dma_start(XT, ins["gens_t"].rearrange("g (k p) n -> p g k n", p=128)).then_inc(s_ld_gens, 16)
            for e in range(E):
                sp.dma_start(w1[:, e, :].rearrange("p (k n) -> p k n", k=2),
                             ins["ew1"][e].rearrange("(k p) n -> p k n", p=128)).then_inc(s_ld_exp, 16)
                sp.dma_start(w2[:, e, :].rearrange("p (k n) -> p k n", k=4),
                             ins["ew2"][e].rearrange("(k p) n -> p k n", p=128)).then_inc(s_ld_exp, 16)
            sp.dma_start(eb1.rearrange("p e n -> p (e n)"),
                         ins["eb1"].rearrange("e n -> (e n)").partition_broadcast(128)).then_inc(s_ld_exp, 16)
            sp.dma_start(eb2.rearrange("p e n -> p (e n)"),
                         ins["eb2"].rearrange("e n -> (e n)").partition_broadcast(128)).then_inc(s_ld_exp, 16)
            sp.wait_ge(s_sent, 16 * 2 * TILES)
            sp.wait_ge(s_fin_ready, 2)
            sp.dma_start(tok[0], xg[0:128, :]).then_inc(s_tok_ld0, 16)
            sp.dma_start(tok[1], xg[128:256, :]).then_inc(s_tok_ld1, 16)
            with sp.Fori(0, SLOT_TILES // 2 - 1) as i:
                for p, ld in ((0, s_tok_ld0), (1, s_tok_ld1)):
                    t = 2 * i + (2 + p)
                    sp.wait_ge(s_tok_tr, t - 1)
                    sp.dma_start(tok[p], xg[bass.ds(t * 128, 128), :]).then_inc(ld, 16)
            with sp.Fori(0, PAIRS // 2) as i:
                for p, st in ((0, s_out_st0), (1, s_out_st1)):
                    j = 2 * i + p
                    sp.wait_ge(s_res_ready, j + 1)
                    for u in range(2):
                        b = 2 * j + u
                        sp.dma_start(out[bass.ds(b, 1), NPATCH:NQ, :].rearrange("b n d -> (b n) d"),
                                     res[p][:, u, :]).then_inc(st, 16)
                        sp.dma_start(out[bass.ds(b, 1), 0:NPATCH, :].rearrange("b n d -> (b n) d"),
                                     res[p][NPATCH * u:NPATCH * (u + 1), 2, :]).then_inc(st, 16)
            sp.wait_ge(s_out_st0, 64 * PAIRS // 2)
            sp.wait_ge(s_out_st1, 64 * PAIRS // 2)

        @block.gpsimd
        def _(pool):
            step = Chain(pool, s_pool_step)
            pool.memset(xn_all[:], 0.0).then_inc(s_cleared, 1)
            pool.wait_ge(s_ld_ids, 16)
            for b in range(NB):
                pool.indirect_dma_start(
                    out=h_all[:, 3 * (b // 2) + b % 2, :], out_offset=None, in_=ins["txt_w"],
                    in_offset=bass.IndirectOffsetOnAxis(ap=ids[:, b:b + 1], axis=0),
                ).then_inc(s_gath, 16)
            pool.memset(pre_all[:], 0.0).then_inc(s_ag_ev, 1)
            pool.memset(mv[:], 1.0)
            pool.memset(mv1[:], 1.0)
            pool.memset(ysum[:], 0.0)
            pool.memset(ones[:], 1.0)
            for p in range(2):
                pool.memset(Vt[p], 1.0)
                pool.memset(Vp[p], 1.0)
            pool.memset(xw, 0.0)
            pool.memset(x2w, 0.0).then_inc(s_h_res, 1)
            pool.memset(x3w, 0.0)
            pool.memset(xnw, 0.0).then_inc(s_ones_set, 1)
            pool.wait_ge(s_ld_ffn, 80)
            pool.wait_ge(s_pads, 16 * (SLOT_TILES // TILES))

            def finish_rows(c):
                pool.wait_ge(s_x2_ready, c + 1)
                wide = [128, 3, D]
                step(pool.tensor_tensor(xnw, x3w, gam[:].unsqueeze(1).to_broadcast(wide), ALU.mult))
                pool.tensor_tensor(xnw, xnw, bet[:].unsqueeze(1).to_broadcast(wide), ALU.add).then_inc(s_xn_ready, 1)
                pool.tensor_tensor(texts(h_all, c), texts(h_all, c), x2w[:, 0:2, :], ALU.add)
                pool.tensor_tensor(tile3(h_all, c, 2), tile3(h_all, c, 2), x2w[0:PROWS, 2, :],
                                   ALU.add).then_inc(s_h_res, 1)
                pool.wait_ge(s_xn_ready, c + 1)
                pool.tensor_copy(texts(xn_all, c), xnw[:, 0:2, :])
                pool.tensor_copy(tile3(xn_all, c, 2), xnw[0:PROWS, 2, :]).then_inc(s_xn_kept, 1)
                pool.wait_ge(s_xn_kept, c + 1)
                pool.wait_ge(s_xn_tr, c + 1)

            with pool.Fori(0, PAIRS) as c:
                step.loop(c)
                finish_rows(c)
            pool.wait_ge(s_norm_part, 1)
            pool.partition_all_reduce(rows[:, 7:8], rows[:, 6:7], 128, RMAX).then_inc(s_norm_all, 1)
            pool.wait_ge(s_slots_ready, 1)
            for t in range(TILES):
                n = ROWS[t % 3]
                for k in range(2):
                    pool.indirect_dma_start(
                        out=xg, out_offset=bass.IndirectOffsetOnAxis(ap=slots[k][0:n, t:t + 1], axis=0),
                        in_=xn_all[0:n, t, :], in_offset=None).then_inc(s_sent, 16)
            pool.wait_ge(s_eo_st0, 16 * SLOT_TILES // 2)
            pool.wait_ge(s_eo_st1, 16 * SLOT_TILES // 2)
            pool.wait_ge(s_down_mm, SLOT_TILES)
            for t in range(TILES):
                n = ROWS[t % 3]
                back = (s_back0, s_back1)[t // 3 % 2]
                if t >= 6 and t % 3 == 0:
                    pool.wait_ge(back, 96 * (t // 6))
                for k in range(2):
                    pool.indirect_dma_start(
                        out=G[k][0:n, t, :], out_offset=None, in_=eod,
                        in_offset=bass.IndirectOffsetOnAxis(ap=slots[k][0:n, t:t + 1], axis=0)).then_inc(back, 16)

        @block.tensor
        def _(pe):
            def acc(o, pairs):
                for n, (a, b) in enumerate(pairs):
                    last = pe.matmul(o, a, b, start=(n == 0), stop=(n == len(pairs) - 1))
                return last

            pe.wait_ge(s_ld_attn, 16 * 14)
            acc(ps[:, 4, 0:128], [(p_uq[:, c, :], p_uk[:, c, :]) for c in range(2)]).then_inc(s_prep_mm, 1)
            acc(ps[:, 5, 0:D], [(p_uv[:, c, :], p_o[:, c, :]) for c in range(2)]).then_inc(s_prep_mm, 1)
            pe.wait_ge(s_prep_cp, 1)
            pe.matmul(ps[:, 6, :], p_g, p_dq, start=True, stop=True).then_inc(s_prep_mm, 1)
            pe.wait_ge(s_prep_cp, 3)

            for j in range(PAIRS):
                after(pe, s_emb_ev, j - 3)
                acc(ps[0:PROWS, 4 + j % 4, 0:D],
                    [(patches[:, c, j * PROWS:(j + 1) * PROWS], wtok[:, c, :]) for c in range(FC)]).then_inc(s_emb_mm, 1)

            def turn_x(a):
                pe.wait_ge(s_x_ready, a + 1)
                for c in range(2):
                    for u, at in ((2, 0), (0, PROWS), (1, PROWS + 128)):
                        n = ROWS[u]
                        last = pe.transpose(ps[:, 6 + c, at:at + n], xw[0:n, u, c * 128:(c + 1) * 128],
                                            ident[0:n, 0:n])
                last.then_inc(s_x_tr, 1)

            def latents(a):
                pe.wait_ge(s_xT_cp, a + 1)
                acc(ps[:, 6, 0:TP], [(wdq[:, c, :], xT[:, c, :]) for c in range(2)])
                acc(ps[:, 7, 0:TP], [(wdkv[:, c, :], xT[:, c, :]) for c in range(2)]).then_inc(s_lat_mm, 1)

            def heads_t(w, src, half, bank, mm):
                for m in range(2):
                    g = 2 * half + m
                    last = pe.matmul(ps[:, bank + m, 0:TP], w[:, g * 128:(g + 1) * 128], src,
                                     start=True, stop=True)
                last.then_inc(mm, 1)

            def values(a):
                for b in range(2):
                    at = b * NQ
                    pe.matmul(ps[:, 4, b * D:(b + 1) * D], lat[:, 1, at + NPATCH:at + NQ], ve, start=True, stop=True)
                    last = pe.matmul(ps[0:NPATCH, 5, b * D:(b + 1) * D], lat[:, 1, at:at + NPATCH], ve,
                                     start=True, stop=True)
                last.then_inc(s_v_mm, 1)

            def score(n, p, b, half, gg):
                if gg == 0:
                    after(pe, s_shifted, n)
                    for i in range(4):
                        pe.matmul(ps[:, i, 0:2 * NQ + 2 * NPATCH], identb[:], maskb[:], start=True, stop=False,
                                  skip_group_check=True)
                at = b * NQ
                g = 2 * half + gg
                for i in range(4):
                    r = slice(32 * i, 32 * i + 32)
                    pe.matmul(ps[:, i, gg * NQ:(gg + 1) * NQ], qT[p][r, g, at + NPATCH:at + NQ],
                              kT[p][r, g, at:at + NQ], start=False, stop=True, skip_group_check=True)
                for i in range(4):
                    r = slice(32 * i, 32 * i + 32)
                    o = 2 * NQ + gg * NPATCH
                    last = pe.matmul(ps[0:NPATCH, i, o:o + NPATCH], qT[p][r, g, at:at + NPATCH],
                                     kT[p][r, g, at:at + NPATCH], start=False, stop=True, skip_group_check=True)
                if gg == 1:
                    last.then_inc(s_scores, 1)

            def turn_probs(gp, rp):
                for i in range(4):
                    pe.transpose(ps[:, 4 + gp, i * NTXT:(i + 1) * NTXT], Pt[rp][:, i, gp, NPATCH:NQ], ident[:])
                for i in range(4):
                    pe.transpose(ps[0:NPATCH, 6 + gp, i * NTXT:(i + 1) * NTXT], Pt[rp][:, i, gp, 0:NPATCH],
                                 ident[:])
                for i in range(4):
                    o = SPARE + NPATCH * (i % 2)
                    last = pe.transpose(ps[0:NPATCH, 2 * gp + i // 2, o:o + NPATCH], Pp[rp][:, i, gp, :],
                                        ident[0:NPATCH, 0:NPATCH])
                last.then_inc(s_p_tr, 1)

            def weigh_values(q, gp, p, b, g):
                pe.wait_ge(s_pt_txt, q + 1)
                pe.wait_ge(s_pt_patch, q + 1)
                bank = 4 + gp
                for i in range(4):
                    h = 4 * g + i
                    pe.matmul(ps[32 * i:32 * i + 32, bank, NPATCH:NQ], Vt[p][:, b, VW * h:VW * h + 32],
                              PTt[gp][:, i, :], start=True, stop=False, skip_group_check=True)
                for i in range(4):
                    h = 4 * g + i
                    last = pe.matmul(ps[32 * i:32 * i + 32, bank, 0:NQ], Vp[p][0:NPATCH, b, VW * h:VW * h + 32],
                                     PTp[gp][:, i, :], start=False, stop=True, skip_group_check=True)
                last.then_inc(s_pv, 1)

            def turn_y(p, tiles):
                for u, at, bank in tiles:
                    for g in range(4):
                        last = pe.transpose(ps[0:ROWS[u], bank, g * 128:(g + 1) * 128],
                                            yTs[p][:, g, at:at + ROWS[u]], ident[:])
                last.then_inc(s_y_tr, 1)

            def turn_xn(c):
                pe.wait_ge(s_xn_ready, c + 1)
                for k in range(2):
                    for u, at in ((2, 0), (0, PROWS), (1, PROWS + 128)):
                        n = ROWS[u]
                        last = pe.transpose(ps[:, 6 + k, at:at + n], xnw[0:n, u, k * 128:(k + 1) * 128],
                                            ident[0:n, 0:n])
                last.then_inc(s_xn_tr, 1)

            def abel_and_gate(c):
                for u, at, bank in ((0, PROWS, 6), (1, PROWS + 128, 7), (2, 0, 4)):
                    n = ROWS[u]
                    last = acc(ps[0:n, bank, 0:D + E], [(xnT[:, k, at:at + n], wag[:, k, :]) for k in range(2)])
                last.then_inc(s_ag_mm, 1)

            TEXTS_45 = ((0, PROWS, 4), (1, PROWS + 128, 5))
            PATCHES_4 = ((2, 0, 4),)

            def round_(j, k, par, first, last):
                n = 4 * j + k
                a = j + 1
                c = j - 1
                no_prev = first and k == 0
                q = 2 * n - 2
                prev_par = par if k else 1 - par
                pb, ph = (k - 1) % 2, ((k - 1) % 4) // 2
                rp = (k + 1) % 2
                if k % 2 == 0:
                    pe.wait_ge(s_q_cp, 2 * j + (1 + k // 2))
                    pe.wait_ge(s_k_cp, 2 * j + (1 + k // 2))
                score(n, par, k % 2, k // 2, 0)
                if k == 0:
                    if not first:
                        pe.wait_ge(s_yt, q)
                        pe.wait_ge(s_q_cp, 2 * j + 2)
                        pe.wait_ge(s_ag_ev, c + 1)
                    heads_t(ket, lat[:, 1, :], 1, 4, s_k_mm)
                if k == 1 and not first:
                    pe.wait_ge(s_yt, q)
                    pe.wait_ge(s_v_cp, j + 1)
                    turn_y(1 - par, TEXTS_45)
                score(n, par, k % 2, k // 2, 1)
                if not no_prev:
                    pe.wait_ge(s_probs, n)
                    after(pe, s_yt, q)
                    if k == 0:
                        pe.wait_ge(s_k_cp, 2 * j + 2)
                        pe.wait_ge(s_ag_ev, c + 1)
                    if k == 1:
                        pe.wait_ge(s_v_cp, j + 1)
                        if not last:
                            pe.wait_ge(s_xT_cp, a + 1)
                        if not first:
                            pe.wait_ge(s_y_ev, 2 * c + 1)
                    if k == 2:
                        if not last:
                            pe.wait_ge(s_lat_cp, a + 1)
                        if not first:
                            pe.wait_ge(s_y_ev, 2 * c + 2)
                    if k == 3 and not last:
                        pe.wait_ge(s_q_cp, 2 * a + 1)
                        pe.wait_ge(s_k_cp, 2 * a + 1)
                    turn_probs(0, rp)
                    turn_probs(1, rp)
                    weigh_values(q, 0, prev_par, pb, 2 * ph)
                    weigh_values(q + 1, 1, prev_par, pb, 2 * ph + 1)
                if k == 0:
                    if not last:
                        turn_x(a)
                    after(pe, s_yt, q + 2)
                    if first:
                        pe.wait_ge(s_k_cp, 2)
                    values(j)
                if k == 1:
                    if not last:
                        pe.wait_ge(s_k_cp, 2 * j + 2)
                        latents(a)
                    if not first:
                        pe.wait_ge(s_yt, q + 1)
                        turn_y(1 - par, PATCHES_4)
                if k == 2 and not last:
                    heads_t(wuq, lat[:, 0, :], 0, 6, s_q_mm)
                    pe.wait_ge(s_yt, q + 2)
                    heads_t(ket, lat[:, 1, :], 0, 4, s_k_mm)
                if k == 3:
                    if not first:
                        turn_xn(c)
                    pe.wait_ge(s_yt, q + 2)
                    if not last:
                        heads_t(wuq, lat[:, 0, :], 1, 4, s_q_mm)
                    if not first:
                        pe.wait_ge(s_xnT_cp, c + 1)
                        if not last:
                            pe.wait_ge(s_q_cp, 2 * a + 2)
                        abel_and_gate(c)

            pe.wait_ge(s_emb_ev, PAIRS)
            turn_x(0)
            latents(0)
            pe.wait_ge(s_lat_cp, 1)
            for half in range(2):
                heads_t(wuq, lat[:, 0, :], half, 4 + 2 * half, s_q_mm)
            pe.wait_ge(s_q_cp, 1)
            heads_t(ket, lat[:, 1, :], 0, 4, s_k_mm)

            def pair(j, par, first, last):
                for k in range(4):
                    round_(j, k, par, first, last)

            pair_loop(pe, pair)

            n = 4 * PAIRS
            q = 2 * n - 2
            lp = (PAIRS - 1) % 2
            pe.wait_ge(s_probs, n)
            pe.wait_ge(s_yt, q)
            pe.wait_ge(s_ag_ev, PAIRS)
            for gp in range(2):
                turn_probs(gp, 1)
            for gp in range(2):
                weigh_values(q + gp, gp, lp, 1, 2 + gp)
            pe.wait_ge(s_yt, q + 2)
            turn_y(lp, TEXTS_45)
            turn_y(lp, ((2, 0, 6),))
            pe.wait_ge(s_y_ev, 2 * PAIRS)
            turn_xn(PAIRS - 1)
            pe.wait_ge(s_xnT_cp, PAIRS)
            abel_and_gate(PAIRS - 1)
            pe.wait_ge(s_ag_ev, PAIRS + 1)

            def product(bank, lhsT, rhs):
                for m in range(2):
                    last = acc(ps[:, bank, m * D:(m + 1) * D],
                               [(lhsT[:, k, m * 128:(m + 1) * 128], rhs[:, k, :]) for k in range(2)])
                return last

            def turn(bank, src):
                for a in range(2):
                    for b in range(2):
                        last = pe.transpose(ps[:, bank, a * D + b * 128:a * D + (b + 1) * 128],
                                            src[:, b, a * 128:(a + 1) * 128], ident[:])
                return last

            pe.wait_ge(s_rt_m, 1)
            ms = msum[:, :, :].rearrange("p t e -> p (t e)")
            pe.matmul(ps[:, 6, 0:TILES * E], tri[:], ms, start=True, stop=True)
            pe.matmul(ps[:, 7, 0:TILES * E], ones[:], ms, start=True, stop=True).then_inc(s_rt_mm, 1)

            pe.wait_ge(s_x_scaled, 1)
            for d in range(TERMS - 1):
                for g in range(3):
                    if d:
                        pe.wait_ge(s_hr_ev, 3 * (d - 1) + g + 1)
                    product(g, XT[:, g], EX[:, g]).then_inc(s_hr_mm, 1)
            for g in range(3):
                pe.wait_ge(s_hr_ev, 3 * (TERMS - 2) + g + 1)
                turn(3 + g, EX[:, g]).then_inc(s_sqT_mm, 1)
            squarings = pe.value_load(expo[0:1, 1:2], min_val=1, max_val=126)
            with pe.Fori(0, squarings) as i:
                for g in range(3):
                    pe.wait_ge(s_sqT_cp, 3 * i + 3)
                    product(g, EXT[:, g], EX[:, g]).then_inc(s_sq_mm, 1)
                for g in range(3):
                    pe.wait_ge(s_sq_ev, 3 * i + g + 1)
                    turn(3 + g, EX[:, g]).then_inc(s_sqT_mm, 1)
            pe.wait_ge(s_fin_ready, 1)
            product(0, EXT[:, 1], EX[:, 2]).then_inc(s_rmul, 1)
            pe.wait_ge(s_rmul_ev, 1)
            product(1, EXT[:, 0], EX[:, 1]).then_inc(s_rmul, 1)

            pe.wait_ge(s_ld_exp, 16 * (2 * E + 2))
            pe.wait_ge(s_fin_ready, 2)

            def in_tile(ldcount, t, p):
                pe.wait_ge((s_tok_ld0, s_tok_ld1)[p], ldcount)
                after(pe, s_tokT_cp, t)
                for c in range(2):
                    last = pe.transpose(ps[:, 0, c * 128:(c + 1) * 128], tok[p][:, c * 128:(c + 1) * 128], ident[:])
                last.then_inc(s_tok_tr, 1)

            def up(t, p):
                e = pe.value_load(exi[0:1, bass.ds(t, 1)], min_val=0, max_val=E - 1)
                pe.wait_ge(s_tokT_cp, t + 1)
                if not (isinstance(t, int) and t < 2):
                    pe.wait_ge(s_up_ev, t - 1)
                for k in range(2):
                    w = w1[:, bass.ds(e, 1), k * HID:(k + 1) * HID].rearrange("p a n -> p (a n)")
                    last = pe.matmul(ps[:, 1 + p, :], tokT[p][:, k, :], w, start=(k == 0), stop=(k == 1))
                last.then_inc(s_up_mm, 1)
                return e

            def turn_hid(t, p):
                pe.wait_ge(s_gelu, t + 1)
                after(pe, s_hidT_cp, t)
                for c in range(4):
                    last = pe.transpose(ps[:, 3, c * 128:(c + 1) * 128], hid[p][:, c * 128:(c + 1) * 128], ident[:])
                last.then_inc(s_hid_tr, 1)

            def down(t, p, peeled):
                e = pe.value_load(exi[0:1, bass.ds(t, 1)], min_val=0, max_val=E - 1)
                pe.wait_ge(s_hidT_cp, t + 1)
                if not peeled:
                    pe.wait_ge(s_eo_ready, t - 1)
                for k in range(4):
                    w = w2[:, bass.ds(e, 1), k * D:(k + 1) * D].rearrange("p a n -> p (a n)")
                    last = pe.matmul(ps[:, 4 + p, 0:D], hidT[p][:, k, :], w, start=(k == 0), stop=(k == 3))
                last.then_inc(s_down_mm, 1)

            in_tile(16, 0, 0)
            in_tile(16, 1, 1)
            up(0, 0)
            turn_hid(0, 0)
            in_tile(32, 2, 0)
            up(1, 1)
            down(0, 0, True)
            turn_hid(1, 1)
            in_tile(32, 3, 1)
            up(2, 0)
            down(1, 1, True)
            with pe.Fori(0, SLOT_TILES // 2 - 2) as i:
                for p in range(2):
                    t = 2 * i + (2 + p)
                    turn_hid(t, p)
                    in_tile(16 * i + 48, t + 2, p)
                    up(t + 1, 1 - p)
                    down(t, p, False)
            t = SLOT_TILES - 2
            turn_hid(t, 0)
            up(t + 1, 1)
            down(t, 0, False)
            turn_hid(t + 1, 1)
            down(t + 1, 1, False)

            def rotate(j, p, peeled):
                mb = 2 + 3 * p
                pe.wait_ge(s_mix, j + 1)
                if not peeled:
                    pe.wait_ge(s_mT_cp, j)
                for c in range(2):
                    for u, at in ((2, 0), (0, PROWS), (1, PROWS + 128)):
                        n = ROWS[u]
                        last = pe.transpose(ps[:, c, at:at + n], moe[p][0:n, u, c * 128:(c + 1) * 128],
                                            ident[0:n, 0:n])
                last.then_inc(s_m_tr, 1)
                pe.wait_ge(s_mT_cp, j + 1)
                if isinstance(j, int):
                    after(pe, s_mr_ev, j - 1)
                else:
                    pe.wait_ge(s_mr_ev, j - 1)
                for u, at in ((0, PROWS), (1, PROWS + 128), (2, 0)):
                    n = ROWS[u]
                    last = acc(ps[0:n, mb + u, 0:RG], [(moeT[p][:, k, at:at + n], R[:, k, :]) for k in range(2)])
                last.then_inc(s_mr_mm, 1)

            pe.wait_ge(s_r_wide, 1)
            rotate(0, 0, True)
            rotate(1, 1, False)
            with pe.Fori(0, PAIRS // 2 - 1) as i:
                for p in range(2):
                    rotate(2 * i + (2 + p), p, False)

        @block.scalar
        def _(act):
            step = Chain(act, s_act_step)
            act.preload_act_table_set("natural_log_exp_and_others")

            def copy(o, i_):
                return act.activation(o, i_, ACT.Copy)

            def norm_scale(var_ready, rs_ready, a, ch, dst, w):
                act.wait_ge(var_ready, a + 1)
                ch(act.activation(lnv[:, 0:w], veps[:, 0:w], ACT.Ln))
                act.activation(dst[:, 0:w], lnv[:, 0:w], ACT.Exp, scale=-0.5).then_inc(rs_ready, 1)

            def x_out(a):
                act.wait_ge(s_x_tr, a + 1)
                dst = xT.rearrange("p c (b n) -> p c b n", b=2)
                copy(dst[:, :, :, 0:NPATCH],
                     ps[:, 6:8, 0:PROWS].rearrange("p c (b n) -> p c b n", b=2))
                copy(dst[:, :, :, NPATCH:NQ],
                     ps[:, 6:8, PROWS:TP].rearrange("p c (b n) -> p c b n", b=2)).then_inc(s_xT_cp, 1)

            def lat_out(a):
                act.wait_ge(s_lat_mm, a + 1)
                copy(lat, ps[:, 6:8, 0:TP]).then_inc(s_lat_cp, 1)

            def q_out(a, p, half, bank):
                act.wait_ge(s_q_mm, 2 * a + half + 1)
                copy(qT[p][:, 2 * half:2 * half + 2, :], ps[:, bank:bank + 2, 0:TP]).then_inc(s_q_cp, 1)

            def k_out(a, p, half, bank):
                act.wait_ge(s_k_mm, 2 * a + half + 1)
                copy(kT[p][:, 2 * half:2 * half + 2, :], ps[:, bank:bank + 2, 0:TP]).then_inc(s_k_cp, 1)

            def v_out(a, p):
                act.wait_ge(s_v_mm, a + 1)
                copy(Vt[p][:, :, 0:HEADS * VW].rearrange("p b (h d) -> p b h d", d=VW)[:, :, :, 0:HD],
                     ps[:, 4, :].rearrange("p (b h d) -> p b h d", b=2, d=HD))
                copy(Vp[p][0:NPATCH, :, 0:HEADS * VW].rearrange("p b (h d) -> p b h d", d=VW)[:, :, :, 0:HD],
                     ps[0:NPATCH, 5, :].rearrange("p (b h d) -> p b h d", b=2, d=HD)).then_inc(s_v_cp, 1)

            def xn_out(c):
                act.wait_ge(s_xn_tr, c + 1)
                copy(xnT, ps[:, 6:8, 0:TP]).then_inc(s_xnT_cp, 1)

            def probs(n, rp):
                act.wait_ge(s_shifted, n + 1)
                act.activation(Pt[rp], Pt[rp], ACT.Exp, scale=0.25)
                act.activation(Pp[rp], Pp[rp], ACT.Exp, scale=0.25).then_inc(s_probs, 1)

            def pt_out(q, gp):
                act.wait_ge(s_p_tr, q + 1)
                copy(PTt[gp], ps[:, 4 + gp, :].rearrange("p (i n) -> p i n", i=4)).then_inc(s_pt_txt, 1)

            def y_out(q, gp, p, b, g):
                act.wait_ge(s_pv, q + 1)
                copy(yTs[p][:, g, b * NPATCH:(b + 1) * NPATCH], ps[:, 4 + gp, 0:NPATCH])
                copy(yTs[p][:, g, PROWS + b * 128:PROWS + (b + 1) * 128],
                     ps[:, 4 + gp, NPATCH:NQ]).then_inc(s_yt, 1)

            act.wait_ge(s_ones_set, 1)
            norm_scale(s_ln1_var, s_ln1_rs, 0, step, rstd1, TILES)
            x_out(0)
            lat_out(0)
            for half in range(2):
                q_out(0, 0, half, 4 + 2 * half)
            k_out(0, 0, 0, 4)

            def round_(j, k, par, first, last):
                n, a, c, q = 4 * j + k, j + 1, j - 1, 8 * j + 2 * k - 2
                no_prev = first and k == 0
                prev_par = par if k else 1 - par
                pb, ph = (k - 1) % 2, ((k - 1) % 4) // 2
                if k == 0:
                    k_out(j, par, 1, 4)
                if not no_prev:
                    pt_out(q, 0)
                    pt_out(q + 1, 1)
                    y_out(q, 0, prev_par, pb, 2 * ph)
                    y_out(q + 1, 1, prev_par, pb, 2 * ph + 1)
                if k == 2 and not first:
                    norm_scale(s_ln2_var, s_ln2_rs, c, step, rstd, 6)
                if k == 0:
                    if not last:
                        x_out(a)
                    v_out(j, par)
                if k == 1 and not last:
                    lat_out(a)
                if k == 2 and not last:
                    q_out(a, 1 - par, 0, 6)
                if k == 3:
                    if not first:
                        xn_out(c)
                    if not last:
                        q_out(a, 1 - par, 1, 4)
                probs(n, k % 2)

            def pair(j, par, first, last):
                step.loop(1 if first else j)
                for k in range(4):
                    round_(j, k, par, first, last)
                assert step.n == (0 if first else 1)

            pair_loop(act, pair)
            n = 4 * PAIRS
            q = 2 * n - 2
            for gp in range(2):
                pt_out(q + gp, gp)
            for gp in range(2):
                y_out(q + gp, gp, (PAIRS - 1) % 2, 1, 2 + gp)
            c = PAIRS - 1
            norm_scale(s_ln2_var, s_ln2_rs, c, step, rstd, 6)
            xn_out(c)

            act.wait_ge(s_gap_ready, 1)
            act.activation(wt2[:], m2[:], ACT.Exp).then_inc(s_gates, 1)

            for g in range(3):
                act.wait_ge(s_sqT_mm, g + 1)
                copy(EXT[:, g], ps[:, 3 + g, :].rearrange("p (k n) -> p k n", k=2)).then_inc(s_sqT_cp, 1)
            squarings = act.value_load(expo[0:1, 1:2], min_val=1, max_val=126)
            with act.Fori(0, squarings) as i:
                for g in range(3):
                    act.wait_ge(s_sqT_mm, 3 * i + (g + 4))
                    copy(EXT[:, g], ps[:, 3 + g, :].rearrange("p (k n) -> p k n", k=2)).then_inc(s_sqT_cp, 1)

            act.wait_ge(s_ag_ev, PAIRS + 1)
            act.activation(pre_all[:, :, 0:D], pre_all[:, :, 0:D], ACT.Gelu).then_inc(s_abel_done, 1)

            def tokT_out(t, p, peeled):
                act.wait_ge(s_tok_tr, t + 1)
                if not peeled:
                    act.wait_ge(s_up_mm, t - 1)
                copy(tokT[p], ps[:, 0, 0:D].rearrange("p (c n) -> p c n", c=2)).then_inc(s_tokT_cp, 1)

            def gelu(t, p, peeled):
                act.wait_ge(s_up_ev, t + 1)
                if not peeled:
                    act.wait_ge(s_hid_tr, t - 1)
                act.activation(hid[p], pre[p], ACT.Gelu).then_inc(s_gelu, 1)

            def hidT_out(t, p, peeled):
                act.wait_ge(s_hid_tr, t + 1)
                if not peeled:
                    act.wait_ge(s_down_mm, t - 1)
                copy(hidT[p], ps[:, 3, :].rearrange("p (c n) -> p c n", c=4)).then_inc(s_hidT_cp, 1)

            def store(t, p):
                act.wait_ge(s_eo_ready, t + 1)
                act.dma_start(eod[bass.ds(t * 128, 128), :], eo[p]).then_inc((s_eo_st0, s_eo_st1)[p], 16)

            tokT_out(0, 0, True)
            tokT_out(1, 1, True)
            gelu(0, 0, True)
            hidT_out(0, 0, True)
            tokT_out(2, 0, False)
            gelu(1, 1, True)
            store(0, 0)
            hidT_out(1, 1, True)
            tokT_out(3, 1, False)
            gelu(2, 0, False)
            store(1, 1)
            with act.Fori(0, SLOT_TILES // 2 - 2) as i:
                for p in range(2):
                    t = 2 * i + (2 + p)
                    hidT_out(t, p, False)
                    tokT_out(t + 2, p, False)
                    gelu(t + 1, 1 - p, False)
                    store(t, p)
            t = SLOT_TILES - 2
            hidT_out(t, 0, False)
            gelu(t + 1, 1, False)
            store(t, 0)
            hidT_out(t + 1, 1, False)
            store(t + 1, 1)

            def turned(j, p):
                act.wait_ge(s_m_tr, j + 1)
                copy(moeT[p], ps[:, 0:2, 0:TP]).then_inc(s_mT_cp, 1)

            def gate(j, p):
                act.wait_ge(s_z_ready, j + 1)
                act.activation(zg[:, 3 * p:3 * p + 3], zg[:, 3 * p:3 * p + 3], ACT.Exp, scale=-1.0).then_inc(s_z_exp, 1)

            turned(0, 0)
            with act.Fori(0, PAIRS // 2 - 1) as i:
                for p in range(2):
                    turned(2 * i + (1 + p), 1 - p)
                    gate(2 * i + p, p)
            turned(PAIRS - 1, 1)
            gate(PAIRS - 2, 0)
            gate(PAIRS - 1, 1)

        @block.vector
        def _(dve):
            step = Chain(dve, s_dve_step)
            dve.wait_ge(s_prep_mm, 1)
            dve.tensor_copy(p_g, ps[:, 4, 0:128]).then_inc(s_prep_cp, 1)
            dve.wait_ge(s_prep_mm, 2)
            dve.tensor_copy(ve, ps[:, 5, 0:D]).then_inc(s_prep_cp, 1)
            dve.wait_ge(s_prep_mm, 3)
            dve.tensor_copy(ket, ps[:, 6, :]).then_inc(s_prep_cp, 1)
            dve.wait_ge(s_ones_set, 1)

            def statistics(src, out_, tiles, var, eps_var):
                for t0 in range(0, tiles, 3):
                    for u in range(3):
                        last = dve.bn_stats(stats[0:ROWS[u], u, :], src(t0 + u))
                    step(last)
                    if tiles == 3:
                        dve.memset(carry[:, 1:2], 0.0)
                    for u in range(3):
                        last = dve.bn_aggr(out_[0:ROWS[u], t0 + u, :], stats[0:ROWS[u], u, :])
                    step(last)
                return dve.tensor_scalar(eps_var, var, EPS, None, ALU.add)

            def refine(rs_ready, a, y, w):
                dve.wait_ge(rs_ready, a + 1)
                step(dve.scalar_tensor_tensor(out=nt1[:, 0:w], in0=y[:, 0:w], scalar=-0.5, in1=y[:, 0:w],
                                              op0=ALU.mult, op1=ALU.mult))
                step(dve.tensor_tensor(nt2[:, 0:w], nt1[:, 0:w], veps[:, 0:w], ALU.mult))
                step(dve.scalar_tensor_tensor(out=y[:, 0:w], in0=nt2[:, 0:w], scalar=1.5, in1=y[:, 0:w],
                                              op0=ALU.add, op1=ALU.mult))

            def first_norm(a):
                for u in range(3):
                    n = ROWS[u]
                    t = bass.ds(3 * a + u, 1)
                    last = dve.tensor_scalar(xw[0:n, u, :], tile3(h_all, a, u),
                                             mv1[0:n, t, 0:1].rearrange("p a b -> p (a b)"), rstd1[0:n, t],
                                             ALU.subtract, ALU.mult)
                last.then_inc(s_x_ready, 1)

            def k_out(a, p, half):
                dve.wait_ge(s_k_mm, 2 * a + half + 1)
                dve.tensor_copy(kT[p][:, 2 * half:2 * half + 2, :], ps[:, 4:6, 0:TP]).then_inc(s_k_cp, 1)

            def shift(n, rp):
                dve.wait_ge(s_scores, n + 1)
                st = ps[:, 0:4, 0:2 * NQ].rearrange("p i (g n) -> p i g n", g=2)
                sp_ = ps[0:NPATCH, 0:4, 2 * NQ:2 * NQ + 2 * NPATCH].rearrange("p i (g n) -> p i g n", g=2)
                dve.tensor_reduce(mx[:], st, AX, ALU.max)
                step(dve.tensor_reduce(mxp[:], sp_, AX, ALU.max))
                dve.tensor_tensor(Pt[rp], st, mx[:].unsqueeze(3).to_broadcast([128, 4, 2, NQ]), ALU.subtract)
                dve.tensor_tensor(Pp[rp], sp_, mxp[:].unsqueeze(3).to_broadcast([NPATCH, 4, 2, NPATCH]),
                                  ALU.subtract).then_inc(s_shifted, 1)

            def pt_out(q, gp):
                dve.wait_ge(s_p_tr, q + 1)
                dve.tensor_copy(PTp[gp][:, :, NPATCH:NQ],
                                ps[0:NPATCH, 6 + gp, :].rearrange("p (i n) -> p i n", i=4))
                dve.tensor_copy(PTp[gp].rearrange("p (b i) n -> p b i n", b=2)[:, :, :, 0:NPATCH],
                                ps[0:NPATCH, 2 * gp:2 * gp + 2, SPARE:SPARE + 2 * NPATCH].rearrange(
                                    "p b (i n) -> p b i n", i=2)).then_inc(s_pt_patch, 1)

            def y_over_sum(c, at, y, n, u0, u1):
                dve.wait_ge(s_y_tr, 2 * c + at + 1)
                w = u1 - u0
                step(dve.reciprocal(rec[0:n, u0:u1, :], y[:, :, :, HD]))
                o = ysum[0:n, u0:u1, :].rearrange("p u (h d) -> p u h d", d=HD)
                dve.tensor_tensor(o, y[:, :, :, 0:HD], rec[0:n, u0:u1, :].unsqueeze(3).to_broadcast([n, w, HEADS, HD]),
                                  ALU.mult).then_inc(s_y_ev, 1)

            def text_rows(c):
                y_over_sum(c, 0, ps[:, 4:6, :].rearrange("p u (h d) -> p u h d", d=32), 128, 0, 2)

            def patch_rows(c, bank):
                y_over_sum(c, 1, ps[0:PROWS, bank:bank + 1, :].rearrange("p u (h d) -> p u h d", d=32), PROWS, 2, 3)

            def add_attention(c):
                dve.wait_ge(s_y_ev, 2 * c + 2)
                dve.tensor_tensor(texts(h_all, c), texts(h_all, c), ysum[:, 0:2, :], ALU.add)
                step(dve.tensor_tensor(tile3(h_all, c, 2), tile3(h_all, c, 2), ysum[0:PROWS, 2, :], ALU.add))
                dve.memset(carry[:, 0:1], 0.0)
                step(statistics(lambda u: tile3(h_all, c, u), mv, 3, mv[:, :, 1], veps[:, 0:3]))
                dve.scalar_tensor_tensor(out=veps[:, 3:6], in0=veps[:, 0:3], scalar=EPS, in1=mv[:, :, 1],
                                         op0=ALU.mult, op1=ALU.add).then_inc(s_ln2_var, 1)

            def both_norms(c):
                refine(s_ln2_rs, c, rstd, 6)
                dve.wait_ge(s_h_res, c + 1)
                for u in range(3):
                    n = ROWS[u]
                    for x, r in ((x3w, 3 + u), (x2w, u)):
                        last = dve.tensor_scalar(x[0:n, u, :], tile3(h_all, c, u), mv[0:n, u, 0:1], rstd[0:n, r:r + 1],
                                                 ALU.subtract, ALU.mult)
                last.then_inc(s_x2_ready, 1)

            def ag_out(c):
                dve.wait_ge(s_ag_mm, c + 1)
                for u, bank in ((0, 6), (1, 7), (2, 4)):
                    n = ROWS[u]
                    last = dve.tensor_tensor(tile3(pre_all, c, u), ps[0:n, bank, 0:D + E], agb[0:n, :], ALU.add)
                last.then_inc(s_ag_ev, 1)

            for j in range(PAIRS):
                dve.wait_ge(s_emb_mm, j + 1)
                dve.tensor_copy(h_all[0:PROWS, 3 * j + 2, :], ps[0:PROWS, 4 + j % 4, 0:D]).then_inc(s_emb_ev, 1)
            dve.wait_ge(s_gath, 16 * NB)
            dve.wait_ge(s_emb_ev, PAIRS)
            statistics(lambda t: h_all[0:ROWS[t % 3], t, :], mv1, TILES, mv1[:, :, 1], veps[:]).then_inc(s_ln1_var, 1)
            refine(s_ln1_rs, 0, rstd1, TILES)
            first_norm(0)

            def round_(j, k, par, first, last):
                n, a, c, q = 4 * j + k, j + 1, j - 1, 8 * j + 2 * k - 2
                no_prev = first and k == 0
                if k == 0 and not last:
                    dve.wait_ge(s_x_tr, a)
                    first_norm(a)
                if k == 1 and not first:
                    text_rows(c)
                if not no_prev:
                    pt_out(q, 0)
                    pt_out(q + 1, 1)
                shift(n, k % 2)
                if k == 1 and not first:
                    patch_rows(c, 4)
                    add_attention(c)
                if k == 2:
                    if not last:
                        k_out(a, 1 - par, 0)
                    if not first:
                        both_norms(c)
                if k == 3 and not first:
                    ag_out(c)

            A_STEPS, C_STEPS = 16 + 3, 2 + 1 + 3 + 3

            def pair(j, par, first, last):
                if first:
                    step.loop(A_STEPS)
                else:
                    step.loop((C_STEPS + 4) * j + (A_STEPS + 4 - C_STEPS - 4))
                for k in range(4):
                    round_(j, k, par, first, last)
                assert step.n == (4 if first else C_STEPS + 4), step.n

            pair_loop(dve, pair)
            n = 4 * PAIRS
            q = 2 * n - 2
            for gp in range(2):
                pt_out(q + gp, gp)
            c = PAIRS - 1
            text_rows(c)
            patch_rows(c, 6)
            add_attention(c)
            both_norms(c)
            ag_out(c)
            dve.wait_ge(s_ag_ev, PAIRS + 1)

            dve.wait_ge(s_ld_route, 64)
            dve.wait_ge(s_ag_ev, PAIRS + 1)
            logits = pre_all[:, :, D:D + E]
            def bt(x):
                return x[:].unsqueeze(2).to_broadcast(TE)
            def be(x):
                return x[:].unsqueeze(1).to_broadcast(TE)

            def first_best(src, m, e, oh):
                step(dve.tensor_reduce(m[:], src, AX, ALU.max))
                step(dve.tensor_tensor(r2[:], src, bt(m), ALU.is_equal))
                step(dve.tensor_tensor(r2[:], r2[:], be(em8), ALU.mult))
                step(dve.tensor_reduce(e[:], r2[:], AX, ALU.min))
                step(dve.tensor_tensor(oh[:], bt(e), be(em8), ALU.is_equal))

            first_best(logits, m1, e1, oh1)
            step(dve.scalar_tensor_tensor(out=r1[:].rearrange("p t e -> p (t e)"),
                                          in0=oh1[:].rearrange("p t e -> p (t e)"), scalar=-3.0e38,
                                          in1=oh1[:].rearrange("p t e -> p (t e)"), op0=ALU.mult, op1=ALU.mult))
            step(dve.tensor_tensor(r1[:], r1[:], logits, ALU.add))
            first_best(r1[:], m2, e2, oh2)
            step(dve.tensor_tensor(msum[:], oh1[:], oh2[:], ALU.add))
            dve.tensor_tensor(msum[:], msum[:], bt(valid), ALU.mult).then_inc(s_rt_m, 1)
            dve.tensor_tensor(m2[:], m2[:], m1[:], ALU.subtract).then_inc(s_gap_ready, 1)
            dve.wait_ge(s_rt_mm, 1)
            dve.wait_ge(s_rt_m, 1)
            ps7 = ps[:, 7, 0:TILES * E].rearrange("p (t e) -> p t e", e=E)
            ps6 = ps[:, 6, 0:TILES * E].rearrange("p (t e) -> p t e", e=E)
            step(dve.tensor_copy(r1[:], ps7))
            src, dst = r1, r2
            sh = 1
            while sh < TILES:
                dve.tensor_copy(dst[:, 0:sh, :], src[:, 0:sh, :])
                step(dve.tensor_tensor(dst[:, sh:, :], src[:, sh:, :], src[:, 0:TILES - sh, :], ALU.add))
                src, dst = dst, src
                sh *= 2
            step(dve.tensor_copy(cnti[:], src[:, TILES - 1, :]))
            step(dve.tensor_scalar(cnti[:], cnti[:], 127, None, ALU.add))
            step(dve.tensor_scalar(cnti[:], cnti[:], 7, 7, ALU.arith_shift_right, ALU.logical_shift_left))
            step(dve.tensor_copy(cnt[:], cnti[:]))
            step(dve.tensor_tensor_scan(endb[:], ones[:, 0:E], cnt[:], 0.0, ALU.mult, ALU.add))
            step(dve.tensor_tensor(base[:], endb[:], cnt[:], ALU.subtract))
            step(dve.tensor_tensor(src[:], src[:], ps7, ALU.subtract))
            step(dve.tensor_tensor(src[:], src[:], ps6, ALU.add))
            step(dve.tensor_tensor(src[:], src[:], be(base), ALU.add))
            for k, oh in ((0, oh1), (1, oh2)):
                step(dve.tensor_tensor(dst[:], src[:], oh[:], ALU.mult))
                step(dve.tensor_reduce((e1, e2)[k][:], dst[:], AX, ALU.add))
                step(dve.tensor_copy(slots[k][:], (e1, e2)[k][:]))
            CE = [128, SLOT_TILES, E - 1]
            step(dve.tensor_tensor(cmp, slot0[:].unsqueeze(2).to_broadcast(CE),
                                   endb[:, 0:E - 1].unsqueeze(1).to_broadcast(CE), ALU.is_ge))
            step(dve.tensor_reduce(exf[:], cmp, AX, ALU.add))
            dve.tensor_copy(exi[:], exf[:]).then_inc(s_slots_ready, 1)
            dve.wait_ge(s_gates, 1)
            step(dve.tensor_scalar(m1[:], wt2[:], 1.0, None, ALU.add))
            step(dve.reciprocal(wt1[:], m1[:]))
            step(dve.tensor_tensor(wt2[:], wt2[:], wt1[:], ALU.mult))

            dve.wait_ge(s_ld_gens, 32)
            step(dve.tensor_reduce(rows[:, 0:6].rearrange("p (g k) -> p g k", g=3), X, AX, ALU.add,
                                   apply_absolute_value=True))
            dve.tensor_reduce(rows[:, 6:7], rows[:, 0:6], AX, ALU.max).then_inc(s_norm_part, 1)
            dve.wait_ge(s_norm_all, 1)
            step(dve.tensor_scalar(expo[:, 0:1], rows[:, 7:8].bitcast(I32), 23, None, ALU.logical_shift_right))
            step(dve.tensor_scalar(expo[:, 1:2], expo[:, 0:1], -124, 1, ALU.add, ALU.max))
            step(dve.tensor_scalar(expo[:, 2:3], expo[:, 1:2], -1, 127, ALU.mult, ALU.add))
            step(dve.tensor_scalar(rows[:, 6:7].bitcast(I32), expo[:, 2:3], 23, None, ALU.logical_shift_left))
            fl = lambda t: t.rearrange("p g k n -> p (g k n)")
            dve.tensor_scalar(fl(X), fl(X), rows[:, 6:7], None, ALU.mult)
            dve.memset(ident2, 0.0)
            step(dve.tensor_scalar(fl(XT), fl(XT), rows[:, 6:7], None, ALU.mult))
            for k in range(2):
                last = dve.tensor_copy(ident2[:, k, k * 128:(k + 1) * 128], ident[:])
            step(last)
            step(dve.tensor_scalar(fl(EX), fl(X), 1.0 / FACT[TERMS], None, ALU.mult))
            for g in range(3):
                last = dve.scalar_tensor_tensor(out=EX[:, g], in0=ident2, scalar=1.0 / FACT[TERMS - 1], in1=EX[:, g],
                                                op0=ALU.mult, op1=ALU.add)
            last.then_inc(s_x_scaled, 1)
            for d in range(TERMS - 1):
                for g in range(3):
                    dve.wait_ge(s_hr_mm, 3 * d + g + 1)
                    src_ = ps[:, g, :].rearrange("p (k n) -> p k n", k=2)
                    if d < TERMS - 2:
                        ins_ = dve.scalar_tensor_tensor(out=EX[:, g], in0=ident2, scalar=1.0 / FACT[TERMS - 2 - d],
                                                        in1=src_, op0=ALU.mult, op1=ALU.add)
                    else:
                        ins_ = dve.tensor_copy(EX[:, g], src_)
                    ins_.then_inc(s_hr_ev, 1)
            squarings = dve.value_load(expo[0:1, 1:2], min_val=1, max_val=126)
            dve.wait_ge(s_hr_ev, 3 * (TERMS - 1))
            with dve.Fori(0, squarings) as i:
                for g in range(3):
                    dve.wait_ge(s_sq_mm, 3 * i + g + 1)
                    dve.wait_ge(s_sqT_mm, 3 * i + 3)
                    dve.scalar_tensor_tensor(out=EX[:, g], in0=EX[:, g], scalar=2.0,
                                             in1=ps[:, g, :].rearrange("p (k n) -> p k n", k=2),
                                             op0=ALU.mult, op1=ALU.add).then_inc(s_sq_ev, 1)
                dve.wait_ge(s_sq_ev, 3 * i + 3)
            dve.wait_ge(s_sqT_cp, 3 * squarings + 3)
            for g in range(3):
                dve.tensor_tensor(EX[:, g], EX[:, g], ident2, ALU.add)
                last = dve.tensor_tensor(EXT[:, g], EXT[:, g], ident2, ALU.add)
            last.then_inc(s_fin_ready, 1)
            dve.wait_ge(s_rmul, 1)
            dve.tensor_copy(EX[:, 1], ps[:, 0, :].rearrange("p (k n) -> p k n", k=2)).then_inc(s_rmul_ev, 1)
            dve.wait_ge(s_rmul, 2)
            dve.tensor_copy(R[:, :, 0:D], ps[:, 1, :].rearrange("p (k n) -> p k n", k=2)).then_inc(s_fin_ready, 1)

            dve.wait_ge(s_abel_done, 1)
            dve.wait_ge(s_fin_ready, 2)
            for t in range(TILES):
                step(dve.tensor_tensor_reduce(ysum[:, 0, :], pre_all[:, t, 0:D], gcw[:, 0:D], 1.0, 0.0, ALU.mult, ALU.add,
                                              zab[:, t:t + 1]))
            step(dve.tensor_scalar(zab[:], zab[:], gcb[:, 0:1], None, ALU.add))
            for k in range(2):
                step(dve.tensor_tensor_reduce(ysum[:, 0, :], R[:, k, 0:D], gcw[:, D:2 * D], 1.0, 0.0, ALU.mult, ALU.add,
                                              zmo[:, k:k + 1]))
            dve.tensor_copy(R[:, :, D], zmo[:, 0:2]).then_inc(s_r_wide, 1)

            def up_out(t, p, peeled):
                e = dve.value_load(exi[0:1, bass.ds(t, 1)], min_val=0, max_val=E - 1)
                dve.wait_ge(s_up_mm, t + 1)
                if not peeled:
                    dve.wait_ge(s_gelu, t - 1)
                dve.tensor_tensor(pre[p], ps[:, 1 + p, :], eb1[:, bass.ds(e, 1), :].rearrange("p a n -> p (a n)"),
                                  ALU.add).then_inc(s_up_ev, 1)

            def down_out(t, p, stored):
                e = dve.value_load(exi[0:1, bass.ds(t, 1)], min_val=0, max_val=E - 1)
                dve.wait_ge(s_down_mm, t + 1)
                if stored is not None:
                    dve.wait_ge((s_eo_st0, s_eo_st1)[p], stored)
                dve.tensor_tensor(eo[p], ps[:, 4 + p, 0:D], eb2[:, bass.ds(e, 1), :].rearrange("p a n -> p (a n)"),
                                  ALU.add).then_inc(s_eo_ready, 1)

            dve.wait_ge(s_ld_exp, 16 * (2 * E + 2))
            up_out(0, 0, True)
            up_out(1, 1, True)
            down_out(0, 0, None)
            up_out(2, 0, False)
            down_out(1, 1, None)
            with dve.Fori(0, SLOT_TILES // 2 - 2) as i:
                for p in range(2):
                    t = 2 * i + (2 + p)
                    up_out(t + 1, 1 - p, False)
                    down_out(t, p, 16 * i + 16)
            t = SLOT_TILES - 2
            up_out(t + 1, 1, False)
            down_out(t, 0, 16 * (t // 2))
            down_out(t + 1, 1, 16 * (t // 2))

            mixbase = step.n + step.base if isinstance(step.base, int) else None
            sel = lambda x, j, u: x[0:ROWS[u], bass.ds(3 * j + u, 1)]

            def mix(j, p):
                for u in range(3):
                    n = ROWS[u]
                    last = dve.tensor_scalar(moe[p][0:n, u, :], tile3(G[0], j, u), sel(wt1, j, u), None, ALU.mult)
                step(last)
                for u in range(3):
                    n = ROWS[u]
                    last = dve.scalar_tensor_tensor(out=moe[p][0:n, u, :], in0=tile3(G[1], j, u), scalar=sel(wt2, j, u),
                                                    in1=moe[p][0:n, u, :], op0=ALU.mult, op1=ALU.add)
                last.then_inc(s_mix, 1)

            def gate(j, p):
                mb = 2 + 3 * p
                z3 = zg[:, 3 * p:3 * p + 3]
                t3 = bass.ds(3 * j, 2)
                dve.wait_ge(s_mr_mm, j + 1)
                dve.tensor_tensor(zg[:, 3 * p:3 * p + 2], ps[:, mb:mb + 2, D], zab[:, t3], ALU.add)
                dve.tensor_tensor(zg[0:PROWS, 3 * p + 2:3 * p + 3], ps[0:PROWS, mb + 2, D:D + 1],
                                  zab[0:PROWS, bass.ds(3 * j + 2, 1)], ALU.add).then_inc(s_z_ready, 1)
                ab = pre_all[:, t3, 0:D]
                ab2 = pre_all[0:PROWS, bass.ds(3 * j + 2, 1), 0:D].rearrange("p a d -> p (a d)")
                dve.tensor_tensor(mo[p][:, 0:2, :], ps[:, mb:mb + 2, 0:D], ab, ALU.subtract)
                dve.tensor_tensor(mo[p][0:PROWS, 2, :], ps[0:PROWS, mb + 2, 0:D], ab2, ALU.subtract).then_inc(s_mr_ev, 1)
                dve.tensor_tensor(res[p][:, 0:2, :], texts(h_all, j), ab, ALU.add)
                step(dve.tensor_tensor(res[p][0:PROWS, 2, :], tile3(h_all, j, 2), ab2, ALU.add))

            def finish(j, p):
                z3 = zg[:, 3 * p:3 * p + 3]
                dve.wait_ge(s_z_exp, j + 1)
                step(dve.tensor_scalar(z3, z3, 1.0, None, ALU.add))
                step(dve.reciprocal(z3, z3))
                dve.wait_ge(s_mr_ev, j + 1)
                for u in range(3):
                    n = ROWS[u]
                    last = dve.scalar_tensor_tensor(out=res[p][0:n, u, :], in0=mo[p][0:n, u, :],
                                                    scalar=zg[0:n, 3 * p + u:3 * p + u + 1], in1=res[p][0:n, u, :],
                                                    op0=ALU.mult, op1=ALU.add)
                last.then_inc(s_res_ready, 1)

            MIX_STEPS, OUT_STEPS = 1, 3
            dve.memset(zg[:], 0.0)
            step.loop(mixbase)
            dve.wait_ge(s_back0, 96)
            mix(0, 0)
            for j in range(2):
                dve.wait_ge(s_back1 if j == 0 else s_back0, 96 if j == 0 else 192)
                if j == 1:
                    dve.wait_ge(s_m_tr, 1)
                mix(j + 1, 1 - j)
                gate(j, j)
                finish(j, j)
            with dve.Fori(0, PAIRS // 2 - 2) as i:
                step.loop((MIX_STEPS + OUT_STEPS) * 2 * i + (mixbase + 3 * MIX_STEPS + 2 * OUT_STEPS))
                for p in range(2):
                    j = 2 * i + (2 + p)
                    dve.wait_ge((s_back1, s_back0)[p], 96 * i + 96 * (2 + p))
                    dve.wait_ge(s_m_tr, j)
                    mix(j + 1, 1 - p)
                    dve.wait_ge((s_out_st0, s_out_st1)[p], 64 * i + 64)
                    gate(j, p)
                    finish(j, p)
            step.loop(mixbase + (PAIRS - 1) * MIX_STEPS + (PAIRS - 2) * OUT_STEPS)
            j = PAIRS - 2
            dve.wait_ge(s_back1, 96 * PAIRS // 2)
            dve.wait_ge(s_m_tr, j)
            mix(j + 1, 1)
            for p in range(2):
                dve.wait_ge((s_out_st0, s_out_st1)[p], 64 * (PAIRS // 2 - 1))
                gate(j + p, p)
                finish(j + p, p)


def kernel(**inputs):
    import numpy as np
    import ml_dtypes
    import concourse.bacc as bacc
    from concourse.bass_utils import run_bass_kernel_spmd as run

    f = {k: np.asarray(v) for k, v in inputs.items()}
    c = np.ascontiguousarray

    def head_columns(w):
        o = np.zeros((w.shape[0], HEADS, 32), w.dtype)
        o[:, :, 0:HD] = w.reshape(w.shape[0], HEADS, HD)
        return o.reshape(w.shape[0], HEADS * 32)

    pat = f["x"].reshape(NB, 3, 6, 16, 6, 16).transpose(0, 1, 3, 5, 2, 4).reshape(NB, NPATCH, 768)
    pat = pat.transpose(2, 0, 1).reshape(768, NB * NPATCH)
    order = np.arange(128)
    mask = np.zeros((128, 2 * NQ + 2 * NPATCH), np.float32)
    low = np.float32(-1e30)
    later = order[None, :] > order[:, None]
    for g in range(2):
        mask[:, g * NQ + NPATCH:(g + 1) * NQ][later] = low
        mask[0:NPATCH, 2 * NQ + g * NPATCH:2 * NQ + (g + 1) * NPATCH][later[0:NPATCH, 0:NPATCH]] = low
    arrays = {
        "patches": c(pat), "ids": c(f["x_txt"].T), "wtok": f["L0_tok_W"], "txt_w": f["L0_txt_w"],
        "uq": f["L0_attn_W_uq"], "uk": f["L0_attn_W_uk"], "uv": f["L0_attn_W_uv"], "o_t": c(f["L0_attn_W_o"].T),
        "dq_t": c(f["L0_attn_W_dq"].T), "dkv_t": c(f["L0_attn_W_dkv"].T),
        "dq_pad": head_columns(f["L0_attn_W_dq"]), "uq_pad": head_columns(f["L0_attn_W_uq"].T),
        "ag": np.concatenate([f["L0_ffn_abel_w"], f["L0_ffn_moe_gate_w"]], axis=1),
        "ag_b": np.concatenate([f["L0_ffn_abel_b"], f["L0_ffn_moe_gate_b"]]),
        "gamma": f["L0_ffn_ln_gamma"], "beta": f["L0_ffn_ln_beta"],
        "gc_w": c(f["L0_ffn_gc_w"].reshape(-1)), "gc_b": f["L0_ffn_gc_b"],
        "ew1": f["L0_ffn_ew1"], "ew2": f["L0_ffn_ew2"], "eb1": f["L0_ffn_eb1"], "eb2": f["L0_ffn_eb2"],
        "gens": f["L0_ffn_gens"], "gens_t": c(f["L0_ffn_gens"].transpose(0, 2, 1)),
        "ident": np.eye(128, dtype=np.float32), "identb": np.eye(128).astype(ml_dtypes.bfloat16),
        "maskb": mask.astype(ml_dtypes.bfloat16),
        "valid": np.stack([(order < ROWS[t % 3]) for t in range(TILES)], 1).astype(np.float32),
        "tri": (order[:, None] < order[None, :]).astype(np.float32),
        "em8": np.tile(np.arange(E, dtype=np.float32) - 8, (128, 1)),
        "slot0": np.tile(128 * np.arange(SLOT_TILES, dtype=np.float32), (128, 1)),
    }
    nc = bacc.Bacc("TRN2", target_bir_lowering=False, num_devices=1)
    ins = {k: nc.dram_tensor("in_" + k, a.shape, mybir.dt.from_np(a.dtype), kind="ExternalInput").ap()
           for k, a in arrays.items()}
    out = nc.dram_tensor("out", (NB, NQ, D), F32, kind="ExternalOutput").ap()
    early_fusion_program(nc, ins, out)
    r = run(nc, [{"in_" + k: a for k, a in arrays.items()}], core_ids=[0])
    return r.results[0]["out"]
```

```python
from contextlib import ExitStack

import concourse.bass as bass
from concourse import mybir

F32 = mybir.dt.float32
BF16 = mybir.dt.bfloat16
I32 = mybir.dt.int32
ACT = mybir.ActivationFunctionType
ALU = mybir.AluOpType
AX = mybir.AxisListType.X
RMAX = bass.bass_isa.ReduceOp.max

NB, NPATCH, NTXT = 16, 36, 128
NQ = NPATCH + NTXT
PAIRS = NB // 2
TP = 2 * NQ
PROWS = 2 * NPATCH
ROWS = (128, 128, PROWS)
TILES = 3 * PAIRS
D = 256
FC = 768 // 128
HEADS, HD = 16, 16
VW = HD + 1
VROW = HEADS * VW + 16
E, HID = 8, 512
SLOT_TILES = (2 * NB * NQ + E * 127) // 128
EPS = 1e-5
SPARE = 2 * NQ + 2 * NPATCH
TERMS = 6
FACT = [1.0]
for _k in range(1, TERMS + 1):
    FACT.append(FACT[-1] * _k)


class Chain:

    def __init__(self, eng, sem):
        self.eng, self.sem, self.base, self.n = eng, sem, 0, 0

    def __call__(self, ins):
        ins.then_inc(self.sem, 1)
        self.n += 1
        self.eng.wait_ge(self.sem, self.base + self.n)

    def loop(self, base):
        self.base, self.n = base, 0


def early_fusion_program(nc, ins, out):
    ctx = ExitStack()
    with ctx:
        def sb(name, shape, dt=F32):
            return ctx.enter_context(nc.sbuf_tensor(name, shape, dt))

        def sem(name):
            return ctx.enter_context(nc.semaphore(name))

        h_all = sb("h_all", [128, TILES, D])
        pre_all = sb("pre_all", [128, TILES, D + E])
        xn_all = sb("xn_all", [128, TILES, D])
        ident = sb("ident", [128, 128])
        identb = sb("identb", [128, 128], BF16)
        maskb = sb("maskb", [128, 2 * NQ + 2 * NPATCH], BF16)
        gam = sb("gam", [128, D])
        bet = sb("bet", [128, D])
        agb = sb("agb", [128, D + E])
        gcw = sb("gcw", [128, 2 * D])
        gcb = sb("gcb", [128, 1])
        ids = sb("ids", [128, NB], I32)
        RG = D + 1
        R = sb("R", [128, 2, RG])

        AW = 29184
        arena = sb("arena", [128, AW])
        top = [0]

        def take(n, rows=128):
            a = top[0]
            top[0] += n
            assert top[0] <= AW, top[0]
            return arena[0:rows, a:a + n]

        wtok = take(FC * D).rearrange("p (c n) -> p c n", c=FC)
        patches = take(FC * NB * NPATCH).rearrange("p (c n) -> p c n", c=FC)
        xw = take(3 * D).rearrange("p (u d) -> p u d", u=3)
        xT = take(2 * TP).rearrange("p (c n) -> p c n", c=2)
        lat = take(2 * TP).rearrange("p (c n) -> p c n", c=2)
        qT = [take(4 * TP).rearrange("p (g n) -> p g n", g=4) for _ in range(2)]
        kT = [take(4 * TP).rearrange("p (g n) -> p g n", g=4) for _ in range(2)]
        Vt = [take(2 * VROW).rearrange("p (b n) -> p b n", b=2) for _ in range(2)]
        Vp = [take(2 * VROW).rearrange("p (b n) -> p b n", b=2) for _ in range(2)]
        Pt = [take(8 * NQ).rearrange("p (i g n) -> p i g n", i=4, g=2) for _ in range(2)]
        Pp = [take(8 * NPATCH, NPATCH).rearrange("p (i g n) -> p i g n", i=4, g=2) for _ in range(2)]
        PTt = [take(4 * NTXT).rearrange("p (i n) -> p i n", i=4) for _ in range(2)]
        PTp = [take(4 * NQ, NPATCH).rearrange("p (i n) -> p i n", i=4) for _ in range(2)]
        y_at = top[0]
        yTs = [take(4 * TP).rearrange("p (g n) -> p g n", g=4) for _ in range(2)]
        x2w = take(3 * D).rearrange("p (u d) -> p u d", u=3)
        x3w = take(3 * D).rearrange("p (u d) -> p u d", u=3)
        xnw = take(3 * D).rearrange("p (u d) -> p u d", u=3)
        xnT = take(2 * TP).rearrange("p (c n) -> p c n", c=2)
        wdq = take(2 * 128).rearrange("p (c n) -> p c n", c=2)
        wdkv = take(2 * 128).rearrange("p (c n) -> p c n", c=2)
        wuq = take(512)
        ket = take(512)
        ve = take(D)
        wag = take(2 * (D + E)).rearrange("p (c n) -> p c n", c=2)
        attn_end, top[0] = top[0], y_at
        p_uq = take(256).rearrange("p (c n) -> p c n", c=2)
        p_uk = take(256).rearrange("p (c n) -> p c n", c=2)
        p_dq = take(512)
        p_uv = take(256).rearrange("p (c n) -> p c n", c=2)
        p_o = take(512).rearrange("p (c n) -> p c n", c=2)
        p_g = take(128)
        assert top[0] <= y_at + 8 * TP

        top[0] = 0
        X = take(3 * 2 * D).rearrange("p (g k n) -> p g k n", g=3, k=2)
        XT = take(3 * 2 * D).rearrange("p (g k n) -> p g k n", g=3, k=2)
        EX = take(3 * 2 * D).rearrange("p (g k n) -> p g k n", g=3, k=2)
        assert top[0] <= FC * (D + NB * NPATCH)
        EXT = take(3 * 2 * D).rearrange("p (g k n) -> p g k n", g=3, k=2)
        free = take(2 * D)
        w1 = take(E * 2 * HID).rearrange("p (e n) -> p e n", e=E)
        w2 = take(E * 4 * D).rearrange("p (e n) -> p e n", e=E)
        eb1 = take(E * HID).rearrange("p (e n) -> p e n", e=E)
        eb2 = take(E * D).rearrange("p (e n) -> p e n", e=E)
        top[0] = 0
        tok = [take(D) for _ in range(2)]
        tokT = [take(D).rearrange("p (c n) -> p c n", c=2) for _ in range(2)]
        pre = [take(HID) for _ in range(2)]
        hid = [take(HID) for _ in range(2)]
        assert top[0] <= 2 * 3 * 2 * D
        eo = [EX[:, 0, k, :] for k in range(2)]
        hidT = [EXT[:, 2].rearrange("p k n -> p (k n)").rearrange("p (c n) -> p c n", c=4),
                free.rearrange("p (c n) -> p c n", c=4)]
        top[0] = 0
        G = [take(TILES * D).rearrange("p (t d) -> p t d", t=TILES) for _ in range(2)]
        moe = [take(3 * D).rearrange("p (u d) -> p u d", u=3) for _ in range(2)]
        moeT = [take(2 * TP).rearrange("p (c n) -> p c n", c=2) for _ in range(2)]
        mo = [take(3 * D).rearrange("p (u d) -> p u d", u=3) for _ in range(2)]
        junk = take(D)
        res = [take(3 * D).rearrange("p (u d) -> p u d", u=3) for _ in range(2)]

        stats = sb("stats", [128, 3, 6])
        mv = sb("mv", [128, 3, 2])
        mv1 = sb("mv1", [128, TILES, 2])
        veps = sb("veps", [128, TILES])
        lnv = sb("lnv", [128, TILES])
        rstd1 = sb("rstd1", [128, TILES])
        rstd = sb("rstd", [128, 6])
        nt1 = sb("nt1", [128, TILES])
        nt2 = sb("nt2", [128, TILES])
        carry = sb("carry", [128, 2])
        mx = sb("mx", [128, 4, 2])
        mxp = sb("mxp", [NPATCH, 4, 2])
        rec = sb("rec", [128, 3, HEADS])
        ysum = sb("ysum", [128, 3, D])
        em8 = sb("em8", [128, E])
        valid = sb("valid", [128, TILES])
        slot0 = sb("slot0", [128, SLOT_TILES])
        tri = sb("tri", [128, 128])
        ones = sb("ones", [128, 128])
        TE = [128, TILES, E]
        oh1, oh2, msum = (sb(n, TE) for n in ("oh1", "oh2", "msum"))
        spare = ysum[:].rearrange("p u d -> p (u d)")
        r1, r2 = (spare[:, k * TILES * E:(k + 1) * TILES * E].rearrange("p (t e) -> p t e", e=E) for k in range(2))
        m1, m2, e1, e2, wt1, wt2, zab, zmo = (
            sb(n, [128, TILES]) for n in ("m1", "m2", "e1", "e2", "wt1", "wt2", "zab", "zmo"))
        cnt, base, endb = (sb(n, [128, E]) for n in ("cnt", "base", "endb"))
        cnti = sb("cnti", [128, E], I32)
        slots = [sb(f"slots{k}", [128, TILES], I32) for k in range(2)]
        cmp = spare[:, 2 * TILES * E:2 * TILES * E + SLOT_TILES * (E - 1)].rearrange("p (s e) -> p s e", e=E - 1)
        exf = sb("exf", [128, SLOT_TILES])
        exi = sb("exi", [128, SLOT_TILES], I32)
        rows = sb("rows", [128, 8])
        expo = sb("expo", [128, 4], I32)
        kident = sb("kident", [128, TERMS - 2, 128], BF16)
        ident2b = sb("ident2b", [128, 2, D], BF16)
        zg = sb("zg", [128, 8])

        ps = ctx.enter_context(nc.psum_tensor("ps", [128, 8, 512], F32))
        xg = nc.dram_tensor("xg", (SLOT_TILES * 128, D), F32, kind="Internal").ap()
        eod = nc.dram_tensor("eod", (SLOT_TILES * 128, D), F32, kind="Internal").ap()

        s_ld_attn = sem("ld_attn")
        s_ld_embed = sem("ld_embed")
        s_ld_ids = sem("ld_ids")
        s_ld_gens = sem("ld_gens")
        s_ld_ffn = sem("ld_ffn")
        s_ld_exp = sem("ld_exp")
        s_ld_route = sem("ld_route")
        s_gath0 = sem("gath0")
        s_gath = sem("gath")
        s_pads = sem("pads")
        s_prep_mm = sem("prep_mm")
        s_prep_cp = sem("prep_cp")
        s_cleared = sem("cleared")
        s_ones_set = sem("ones_set")
        s_emb_mm = sem("emb_mm")
        s_emb_ev = sem("emb_ev")
        s_ln1_var = sem("ln1_var")
        s_ln1_rs = sem("ln1_rs")
        s_x_ready = sem("x_ready")
        s_x_tr = sem("x_tr")
        s_xT_cp = sem("xT_cp")
        s_lat_mm = sem("lat_mm")
        s_lat_cp = sem("lat_cp")
        s_q_mm = sem("q_mm")
        s_q_cp = sem("q_cp")
        s_k_mm = sem("k_mm")
        s_k_cp = sem("k_cp")
        s_v_mm = sem("v_mm")
        s_v_cp = sem("v_cp")
        s_scores = sem("scores")
        s_shifted = sem("shifted")
        s_probs = sem("probs")
        s_p_tr = sem("p_tr")
        s_pt_txt = sem("pt_txt")
        s_pt_patch = sem("pt_patch")
        s_pv = sem("pv")
        s_yt = sem("yt")
        s_y_tr = sem("y_tr")
        s_y_ev = sem("y_ev")
        s_ln2_var = sem("ln2_var")
        s_ln2_rs = sem("ln2_rs")
        s_x2_ready = sem("x2_ready")
        s_x3_ready = sem("x3_ready")
        s_xn_ready = sem("xn_ready")
        s_xn_tr = sem("xn_tr")
        s_xnT_cp = sem("xnT_cp")
        s_ag_mm = sem("ag_mm")
        s_ag_ev = sem("ag_ev")
        s_h_res = sem("h_res")
        s_xn_kept = sem("xn_kept")
        s_dve_step = sem("dve_step")
        s_act_step = sem("act_step")
        s_pool_step = sem("pool_step")
        s_norm_part = sem("norm_part")
        s_norm_all = sem("norm_all")
        s_x_scaled = sem("x_scaled")
        s_ident2_clear = sem("ident2_clear")
        s_hr_mm = sem("hr_mm")
        s_hr_ev = sem("hr_ev")
        s_sq_mm = sem("sq_mm")
        s_sq_ev = sem("sq_ev")
        s_sqT_mm = sem("sqT_mm")
        s_sqT_cp = sem("sqT_cp")
        s_fin_ready = sem("fin_ready")
        s_rmul = sem("rmul")
        s_rmul_ev = sem("rmul_ev")
        s_rt_m = sem("rt_m")
        s_rt_mm = sem("rt_mm")
        s_slots_ready = sem("slots_ready")
        s_experts_ready = sem("experts_ready")
        s_gap_ready = sem("gap_ready")
        s_gates = sem("gates")
        s_sent = sem("sent")
        s_tok_ld0 = sem("tok_ld0")
        s_tok_ld1 = sem("tok_ld1")
        s_tok_tr = sem("tok_tr")
        s_tokT_cp = sem("tokT_cp")
        s_up_mm = sem("up_mm")
        s_up_ev = sem("up_ev")
        s_gelu = sem("gelu")
        s_hid_tr = sem("hid_tr")
        s_hidT_cp = sem("hidT_cp")
        s_down_mm = sem("down_mm")
        s_eo_ready = sem("eo_ready")
        s_eo_st0 = sem("eo_st0")
        s_eo_st1 = sem("eo_st1")
        s_abel_done = sem("abel_done")
        s_back0 = sem("back0")
        s_back1 = sem("back1")
        s_r_wide = sem("r_wide")
        s_weights_ready = sem("weights_ready")
        s_weighted = sem("weighted")
        s_mix = sem("mix")
        s_m_tr = sem("m_tr")
        s_mT_cp = sem("mT_cp")
        s_mr_mm = sem("mr_mm")
        s_mr_ev = sem("mr_ev")
        s_z_ready = sem("z_ready")
        s_z_exp = sem("z_exp")
        s_res_ready = sem("res_ready")
        s_out_st0 = sem("out_st0")
        s_out_st1 = sem("out_st1")

        block = ctx.enter_context(nc.Block())

        def after(eng, sem_, count):
            if not (isinstance(count, int) and count <= 0):
                eng.wait_ge(sem_, count)

        def tile3(t3, expr, u):
            return t3[0:ROWS[u], bass.ds(3 * expr + u, 1), :].rearrange("p a d -> p (a d)")

        def texts(t3, expr):
            return t3[:, bass.ds(3 * expr, 2), :]

        def pair_loop(eng, body):
            body(0, 0, True, False)
            with eng.Fori(0, (PAIRS - 2) // 2) as i:
                for u in range(2):
                    body(2 * i + (1 + u), (1 + u) % 2, False, False)
            body(PAIRS - 1, (PAIRS - 1) % 2, False, True)

        @block.sync
        def _(sp):
            sp.dma_start(ids[:], ins["ids"]).then_inc(s_ld_ids, 16)
            sp.dma_start(ident[:], ins["ident"]).then_inc(s_ld_attn, 16)
            sp.dma_start(wtok, ins["wtok"].rearrange("(c p) n -> p c n", p=128)).then_inc(s_ld_embed, 16)
            cut = 2 * PROWS
            src = ins["patches"].rearrange("(c p) n -> p c n", p=128)
            sp.dma_start(patches[:, :, 0:cut], src[:, :, 0:cut]).then_inc(s_ld_embed, 16)
            for dst, name in ((p_uq, "uq"), (p_uk, "uk"), (p_uv, "uv"), (p_o, "o_t"), (wdq, "dq_t"),
                              (wdkv, "dkv_t"), (wag, "ag")):
                sp.dma_start(dst, ins[name].rearrange("(c p) n -> p c n", p=128)).then_inc(s_ld_attn, 16)
            for dst, name in ((p_dq, "dq_pad"), (wuq, "uq_pad"), (identb[:], "identb"), (maskb[:], "maskb")):
                sp.dma_start(dst, ins[name]).then_inc(s_ld_attn, 16)
            sp.dma_start(patches[:, :, cut:], src[:, :, cut:]).then_inc(s_ld_attn, 16)
            for dst, name in ((gam, "gamma"), (bet, "beta"), (agb, "ag_b"), (gcw, "gc_w"), (gcb, "gc_b")):
                sp.dma_start(dst[:], ins[name].partition_broadcast(128)).then_inc(s_ld_ffn, 16)
            for dst, name in ((valid, "valid"), (tri, "tri"), (em8, "em8"), (slot0, "slot0")):
                sp.dma_start(dst[:], ins[name]).then_inc(s_ld_route, 16)
            sp.wait_ge(s_cleared, 1)
            sp.wait_ge(s_gath, 16 * (NB - 2))
            zero = xn_all[:, :, :]
            for c in range(SLOT_TILES // TILES):
                sp.dma_start(xg[c * TILES * 128:(c + 1) * TILES * 128, :].rearrange("(t p) d -> p t d", p=128),
                             zero).then_inc(s_pads, 16)
            sp.wait_ge(s_emb_mm, PAIRS)
            sp.dma_start(X, ins["gens"].rearrange("g (k p) n -> p g k n", p=128)).then_inc(s_ld_gens, 16)
            sp.dma_start(XT, ins["gens_t"].rearrange("g (k p) n -> p g k n", p=128)).then_inc(s_ld_gens, 16)
            sp.wait_ge(s_ag_ev, PAIRS + 1)
            sp.wait_ge(s_xn_kept, PAIRS)
            for e in range(E):
                sp.dma_start(w1[:, e, :].rearrange("p (k n) -> p k n", k=2),
                             ins["ew1"][e].rearrange("(k p) n -> p k n", p=128)).then_inc(s_ld_exp, 16)
                sp.dma_start(w2[:, e, :].rearrange("p (k n) -> p k n", k=4),
                             ins["ew2"][e].rearrange("(k p) n -> p k n", p=128)).then_inc(s_ld_exp, 16)
            sp.dma_start(eb1.rearrange("p e n -> p (e n)"),
                         ins["eb1"].rearrange("e n -> (e n)").partition_broadcast(128)).then_inc(s_ld_exp, 16)
            sp.dma_start(eb2.rearrange("p e n -> p (e n)"),
                         ins["eb2"].rearrange("e n -> (e n)").partition_broadcast(128)).then_inc(s_ld_exp, 16)
            sp.wait_ge(s_sent, 16 * 2 * TILES)
            sp.wait_ge(s_hr_mm, 3 * (TERMS - 1))
            sp.dma_start(tok[0], xg[0:128, :]).then_inc(s_tok_ld0, 16)
            sp.dma_start(tok[1], xg[128:256, :]).then_inc(s_tok_ld1, 16)
            def store(t, p):
                sp.wait_ge(s_eo_ready, t + 1)
                sp.dma_start(eod[bass.ds(t * 128, 128), :], eo[p]).then_inc((s_eo_st0, s_eo_st1)[p], 16)

            def load(t, p):
                sp.wait_ge(s_tok_tr, t - 1)
                sp.dma_start(tok[p], xg[bass.ds(t * 128, 128), :]).then_inc((s_tok_ld0, s_tok_ld1)[p], 16)

            load(2, 0)
            with sp.Fori(0, SLOT_TILES // 2 - 2) as i:
                for p in range(2):
                    load(2 * i + (3 + p), 1 - p)
                    store(2 * i + p, p)
            load(SLOT_TILES - 1, 1)
            for t in range(SLOT_TILES - 4, SLOT_TILES):
                store(t, t % 2)
            with sp.Fori(0, PAIRS // 2) as i:
                for p, st in ((0, s_out_st0), (1, s_out_st1)):
                    j = 2 * i + p
                    sp.wait_ge(s_res_ready, j + 1)
                    for u in range(2):
                        b = 2 * j + u
                        sp.dma_start(out[bass.ds(b, 1), NPATCH:NQ, :].rearrange("b n d -> (b n) d"),
                                     res[p][:, u, :]).then_inc(st, 16)
                        sp.dma_start(out[bass.ds(b, 1), 0:NPATCH, :].rearrange("b n d -> (b n) d"),
                                     res[p][NPATCH * u:NPATCH * (u + 1), 2, :]).then_inc(st, 16)
            sp.wait_ge(s_out_st0, 64 * PAIRS // 2)
            sp.wait_ge(s_out_st1, 64 * PAIRS // 2)

        @block.gpsimd
        def _(pool):
            step = Chain(pool, s_pool_step)
            pool.memset(xn_all[:], 0.0).then_inc(s_cleared, 1)
            pool.wait_ge(s_ld_ids, 16)
            for b in range(NB):
                pool.indirect_dma_start(
                    out=h_all[:, 3 * (b // 2) + b % 2, :], out_offset=None, in_=ins["txt_w"],
                    in_offset=bass.IndirectOffsetOnAxis(ap=ids[:, b:b + 1], axis=0),
                ).then_inc(s_gath0 if b < 2 else s_gath, 16)
            pool.wait_ge(s_ld_ffn, 80)
            pool.wait_ge(s_pads, 16 * (SLOT_TILES // TILES))

            def finish_rows(c):
                pool.wait_ge(s_x2_ready, c + 1)
                wide = [128, 3, D]
                step(pool.tensor_tensor(xnw, x3w, gam[:].unsqueeze(1).to_broadcast(wide), ALU.mult))
                pool.tensor_tensor(xnw, xnw, bet[:].unsqueeze(1).to_broadcast(wide), ALU.add).then_inc(s_xn_ready, 1)
                pool.tensor_tensor(texts(h_all, c), texts(h_all, c), x2w[:, 0:2, :], ALU.add)
                pool.tensor_tensor(tile3(h_all, c, 2), tile3(h_all, c, 2), x2w[0:PROWS, 2, :],
                                   ALU.add).then_inc(s_h_res, 1)
                pool.wait_ge(s_xn_ready, c + 1)
                pool.tensor_copy(texts(xn_all, c), xnw[:, 0:2, :])
                pool.tensor_copy(tile3(xn_all, c, 2), xnw[0:PROWS, 2, :]).then_inc(s_xn_kept, 1)
                pool.wait_ge(s_xn_kept, c + 1)
                pool.wait_ge(s_xn_tr, c + 1)

            pool.wait_ge(s_ld_attn, 16 * 13)
            pool.memset(ident2b[:], 0.0).then_inc(s_ident2_clear, 1)
            pool.wait_ge(s_ident2_clear, 1)
            for k in range(2):
                pool.tensor_copy(ident2b[:, k, k * 128:(k + 1) * 128], identb[:])
            for k in range(2, TERMS):
                last = pool.tensor_scalar(kident[:, k - 2, :], identb[:], float(k), None, ALU.mult)
            last.then_inc(s_x_scaled, 1)
            pool.wait_ge(s_norm_part, 1)
            pool.partition_all_reduce(rows[:, 7:8], rows[:, 6:7], 128, RMAX).then_inc(s_norm_all, 1)
            with pool.Fori(0, PAIRS) as c:
                step.loop(c)
                finish_rows(c)
            for k in range(2):
                pool.wait_ge(s_slots_ready, k + 1)
                for t in range(TILES):
                    n = ROWS[t % 3]
                    pool.indirect_dma_start(
                        out=xg, out_offset=bass.IndirectOffsetOnAxis(ap=slots[k][0:n, t:t + 1], axis=0),
                        in_=xn_all[0:n, t, :], in_offset=None).then_inc(s_sent, 16)
            pool.wait_ge(s_eo_st0, 16 * SLOT_TILES // 2)
            pool.wait_ge(s_eo_st1, 16 * SLOT_TILES // 2)
            pool.wait_ge(s_down_mm, SLOT_TILES)
            for t in range(TILES):
                n = ROWS[t % 3]
                back = (s_back0, s_back1)[t // 3 % 2]
                if t >= 6 and t % 3 == 0:
                    pool.wait_ge(back, 96 * (t // 6))
                for k in range(2):
                    pool.indirect_dma_start(
                        out=G[k][0:n, t, :], out_offset=None, in_=eod,
                        in_offset=bass.IndirectOffsetOnAxis(ap=slots[k][0:n, t:t + 1], axis=0)).then_inc(back, 16)

        @block.tensor
        def _(pe):
            def acc(o, pairs):
                for n, (a, b) in enumerate(pairs):
                    last = pe.matmul(o, a, b, start=(n == 0), stop=(n == len(pairs) - 1))
                return last

            pe.wait_ge(s_ld_embed, 32)
            def embed(j):
                after(pe, s_emb_ev, j - 3)
                acc(ps[0:PROWS, j % 4, 0:D],
                    [(patches[:, c, j * PROWS:(j + 1) * PROWS], wtok[:, c, :]) for c in range(FC)]).then_inc(s_emb_mm, 1)

            embed(0)
            embed(1)
            pe.wait_ge(s_ld_attn, 16 * 13)
            acc(ps[:, 4, 0:128], [(p_uq[:, c, :], p_uk[:, c, :]) for c in range(2)]).then_inc(s_prep_mm, 1)
            acc(ps[:, 5, 0:D], [(p_uv[:, c, :], p_o[:, c, :]) for c in range(2)]).then_inc(s_prep_mm, 1)
            pe.wait_ge(s_prep_cp, 1)
            pe.matmul(ps[:, 6, :], p_g, p_dq, start=True, stop=True).then_inc(s_prep_mm, 1)
            embed(2)

            def turn_x(a):
                pe.wait_ge(s_x_ready, a + 1)
                for c in range(2):
                    for u, at in ((2, 0), (0, PROWS), (1, PROWS + 128)):
                        n = ROWS[u]
                        last = pe.transpose(ps[:, 6 + c, at:at + n], xw[0:n, u, c * 128:(c + 1) * 128],
                                            ident[0:n, 0:n])
                last.then_inc(s_x_tr, 1)

            def latents(a):
                pe.wait_ge(s_xT_cp, a + 1)
                acc(ps[:, 6, 0:TP], [(wdq[:, c, :], xT[:, c, :]) for c in range(2)])
                acc(ps[:, 7, 0:TP], [(wdkv[:, c, :], xT[:, c, :]) for c in range(2)]).then_inc(s_lat_mm, 1)

            def heads_t(w, src, half, bank, mm):
                for m in range(2):
                    g = 2 * half + m
                    last = pe.matmul(ps[:, bank + m, 0:TP], w[:, g * 128:(g + 1) * 128], src,
                                     start=True, stop=True)
                last.then_inc(mm, 1)

            def values(a):
                for b in range(2):
                    at = b * NQ
                    pe.matmul(ps[:, 4, b * D:(b + 1) * D], lat[:, 1, at + NPATCH:at + NQ], ve, start=True, stop=True)
                    last = pe.matmul(ps[0:NPATCH, 5, b * D:(b + 1) * D], lat[:, 1, at:at + NPATCH], ve,
                                     start=True, stop=True)
                last.then_inc(s_v_mm, 1)

            def score(n, p, b, half, gg):
                if gg == 0:
                    after(pe, s_shifted, n)
                    for i in range(4):
                        pe.matmul(ps[:, i, 0:2 * NQ + 2 * NPATCH], identb[:], maskb[:], start=True, stop=False,
                                  skip_group_check=True)
                at = b * NQ
                g = 2 * half + gg
                for i in range(4):
                    r = slice(32 * i, 32 * i + 32)
                    pe.matmul(ps[:, i, gg * NQ:(gg + 1) * NQ], qT[p][r, g, at + NPATCH:at + NQ],
                              kT[p][r, g, at:at + NQ], start=False, stop=True, skip_group_check=True)
                for i in range(4):
                    r = slice(32 * i, 32 * i + 32)
                    o = 2 * NQ + gg * NPATCH
                    last = pe.matmul(ps[0:NPATCH, i, o:o + NPATCH], qT[p][r, g, at:at + NPATCH],
                                     kT[p][r, g, at:at + NPATCH], start=False, stop=True, skip_group_check=True)
                if gg == 1:
                    last.then_inc(s_scores, 1)

            def turn_probs(gp, rp):
                for i in range(4):
                    pe.transpose(ps[:, 4 + gp, i * NTXT:(i + 1) * NTXT], Pt[rp][:, i, gp, NPATCH:NQ], ident[:])
                for i in range(4):
                    pe.transpose(ps[0:NPATCH, 6 + gp, i * NTXT:(i + 1) * NTXT], Pt[rp][:, i, gp, 0:NPATCH],
                                 ident[:])
                for i in range(4):
                    o = SPARE + NPATCH * (i % 2)
                    last = pe.transpose(ps[0:NPATCH, 2 * gp + i // 2, o:o + NPATCH], Pp[rp][:, i, gp, :],
                                        ident[0:NPATCH, 0:NPATCH])
                last.then_inc(s_p_tr, 1)

            def weigh_values(q, gp, p, b, g):
                pe.wait_ge(s_pt_txt, q + 1)
                pe.wait_ge(s_pt_patch, q + 1)
                bank = 4 + gp
                for i in range(4):
                    h = 4 * g + i
                    pe.matmul(ps[32 * i:32 * i + 32, bank, NPATCH:NQ], Vt[p][:, b, VW * h:VW * h + 32],
                              PTt[gp][:, i, :], start=True, stop=False, skip_group_check=True)
                for i in range(4):
                    h = 4 * g + i
                    last = pe.matmul(ps[32 * i:32 * i + 32, bank, 0:NQ], Vp[p][0:NPATCH, b, VW * h:VW * h + 32],
                                     PTp[gp][:, i, :], start=False, stop=True, skip_group_check=True)
                last.then_inc(s_pv, 1)

            def turn_y(p, tiles):
                for u, at, bank in tiles:
                    for g in range(4):
                        last = pe.transpose(ps[0:ROWS[u], bank, g * 128:(g + 1) * 128],
                                            yTs[p][:, g, at:at + ROWS[u]], ident[:])
                last.then_inc(s_y_tr, 1)

            def turn_xn(c):
                pe.wait_ge(s_xn_ready, c + 1)
                for k in range(2):
                    for u, at in ((2, 0), (0, PROWS), (1, PROWS + 128)):
                        n = ROWS[u]
                        last = pe.transpose(ps[:, 6 + k, at:at + n], xnw[0:n, u, k * 128:(k + 1) * 128],
                                            ident[0:n, 0:n])
                last.then_inc(s_xn_tr, 1)

            def abel_and_gate(c):
                for u, at, bank in ((0, PROWS, 6), (1, PROWS + 128, 7), (2, 0, 4)):
                    n = ROWS[u]
                    last = acc(ps[0:n, bank, 0:D + E], [(xnT[:, k, at:at + n], wag[:, k, :]) for k in range(2)])
                last.then_inc(s_ag_mm, 1)

            def product(bank, lhsT, rhs, start=True):
                for m in range(2):
                    for k in range(2):
                        last = pe.matmul(ps[:, bank, m * D:(m + 1) * D], lhsT[:, k, m * 128:(m + 1) * 128],
                                         rhs[:, k, :], start=(start and k == 0), stop=(k == 1),
                                         skip_group_check=not start)
                return last

            def turn(bank, src):
                for a in range(2):
                    for b in range(2):
                        last = pe.transpose(ps[:, bank, a * D + b * 128:a * D + (b + 1) * 128],
                                            src[:, b, a * 128:(a + 1) * 128], ident[:])
                return last

            def horner(k, groups, banks):
                d = TERMS - 1 - k
                for g, bank in zip(groups, banks):
                    if d:
                        pe.wait_ge(s_hr_ev, 3 * (d - 1) + g + 1)
                    if k > 1:
                        pe.matmul(ps[:, bank, :], kident[:, k - 2, :], ident2b[:, :, :].rearrange("p k n -> p (k n)"),
                                  start=True, stop=False, skip_group_check=True)
                    product(bank, XT[:, g], EX[:, g], k == 1).then_inc(s_hr_mm, 1)

            TEXTS_45 = ((0, PROWS, 4), (1, PROWS + 128, 5))
            PATCHES_4 = ((2, 0, 4),)

            def round_(j, k, par, first, last):
                n = 4 * j + k
                a = j + 1
                c = j - 1
                no_prev = first and k == 0
                q = 2 * n - 2
                prev_par = par if k else 1 - par
                pb, ph = (k - 1) % 2, ((k - 1) % 4) // 2
                rp = (k + 1) % 2
                if k % 2 == 0:
                    pe.wait_ge(s_q_cp, 2 * j + (1 + k // 2))
                    pe.wait_ge(s_k_cp, 2 * j + (1 + k // 2))
                score(n, par, k % 2, k // 2, 0)
                if k == 0:
                    if not first:
                        pe.wait_ge(s_yt, q)
                        pe.wait_ge(s_q_cp, 2 * j + 2)
                        pe.wait_ge(s_ag_ev, c + 1)
                    heads_t(ket, lat[:, 1, :], 1, 4, s_k_mm)
                if k == 1 and not first:
                    pe.wait_ge(s_yt, q)
                    pe.wait_ge(s_v_cp, j + 1)
                    turn_y(1 - par, TEXTS_45)
                if k == 3 and not last and not first:
                    pe.wait_ge(s_yt, q)
                    pe.wait_ge(s_k_cp, 2 * a + 1)
                    heads_t(wuq, lat[:, 0, :], 1, 4, s_q_mm)
                score(n, par, k % 2, k // 2, 1)
                if not no_prev:
                    pe.wait_ge(s_probs, n)
                    after(pe, s_yt, q)
                    if last and k:
                        pe.wait_ge(s_hr_ev, 2 * k - 1)
                    if k == 0:
                        pe.wait_ge(s_k_cp, 2 * j + 2)
                        pe.wait_ge(s_ag_ev, c + 1)
                    if k == 1:
                        pe.wait_ge(s_v_cp, j + 1)
                        if not last:
                            pe.wait_ge(s_xT_cp, a + 1)
                        if not first:
                            pe.wait_ge(s_y_ev, 2 * c + 1)
                    if k == 2:
                        if not last:
                            pe.wait_ge(s_lat_cp, a + 1)
                        if not first:
                            pe.wait_ge(s_y_ev, 2 * c + 2)
                    if k == 3 and not last:
                        pe.wait_ge(s_q_cp, 2 * a + (1 if first else 2))
                        pe.wait_ge(s_k_cp, 2 * a + 1)
                    turn_probs(0, rp)
                    turn_probs(1, rp)
                    weigh_values(q, 0, prev_par, pb, 2 * ph)
                    weigh_values(q + 1, 1, prev_par, pb, 2 * ph + 1)
                if k == 0:
                    if not last:
                        turn_x(a)
                    after(pe, s_yt, q + 2)
                    if first:
                        pe.wait_ge(s_k_cp, 2)
                    values(j)
                    if last:
                        pe.wait_ge(s_x_scaled, 2)
                        horner(5, (0,), (6,))
                if k == 1:
                    if not last:
                        pe.wait_ge(s_k_cp, 2 * j + 2)
                        latents(a)
                    if not first:
                        pe.wait_ge(s_yt, q + 1)
                        turn_y(1 - par, PATCHES_4)
                    if last:
                        horner(5, (1, 2), (7, 6))
                if k == 2 and last:
                    horner(4, (0, 1), (6, 7))
                if k == 2 and not last:
                    heads_t(wuq, lat[:, 0, :], 0, 6, s_q_mm)
                    pe.wait_ge(s_yt, q + 2)
                    heads_t(ket, lat[:, 1, :], 0, 4, s_k_mm)
                if k == 3:
                    if not first:
                        turn_xn(c)
                    pe.wait_ge(s_yt, q + 2)
                    if first:
                        heads_t(wuq, lat[:, 0, :], 1, 4, s_q_mm)
                    if last:
                        horner(4, (2,), (5,))
                    if not first:
                        pe.wait_ge(s_xnT_cp, c + 1)
                        abel_and_gate(c)

            pe.wait_ge(s_prep_cp, 3)
            turn_x(0)
            embed(3)
            latents(0)
            embed(4)
            pe.wait_ge(s_lat_cp, 1)
            for half in range(2):
                heads_t(wuq, lat[:, 0, :], half, 4 + 2 * half, s_q_mm)
            embed(5)
            pe.wait_ge(s_q_cp, 1)
            heads_t(ket, lat[:, 1, :], 0, 4, s_k_mm)
            embed(6)
            embed(7)
            pe.wait_ge(s_emb_ev, PAIRS)

            def pair(j, par, first, last):
                for k in range(4):
                    round_(j, k, par, first, last)

            pair_loop(pe, pair)

            n = 4 * PAIRS
            q = 2 * n - 2
            lp = (PAIRS - 1) % 2
            pe.wait_ge(s_probs, n)
            pe.wait_ge(s_yt, q)
            pe.wait_ge(s_ag_ev, PAIRS)
            pe.wait_ge(s_hr_ev, 6)
            for gp in range(2):
                turn_probs(gp, 1)
            for gp in range(2):
                weigh_values(q + gp, gp, lp, 1, 2 + gp)
            pe.wait_ge(s_yt, q + 2)
            turn_y(lp, TEXTS_45)
            turn_y(lp, ((2, 0, 6),))

            horner(3, range(3), range(3))
            horner(2, range(3), range(3))
            pe.wait_ge(s_y_ev, 2 * PAIRS)
            turn_xn(PAIRS - 1)
            pe.wait_ge(s_xnT_cp, PAIRS)
            abel_and_gate(PAIRS - 1)
            horner(1, range(3), range(3))
            pe.wait_ge(s_ag_ev, PAIRS + 1)
            pe.wait_ge(s_rt_m, 1)
            ms = msum[:, :, :].rearrange("p t e -> p (t e)")
            pe.matmul(ps[:, 6, 0:TILES * E], tri[:], ms, start=True, stop=True)
            pe.matmul(ps[:, 7, 0:TILES * E], ones[:], ms, start=True, stop=True).then_inc(s_rt_mm, 1)
            for g in range(3):
                pe.wait_ge(s_hr_ev, 3 * (TERMS - 2) + g + 1)
                turn(3 + g, EX[:, g]).then_inc(s_sqT_mm, 1)
            squarings = pe.value_load(expo[0:1, 1:2], min_val=1, max_val=126)
            with pe.Fori(0, squarings) as i:
                for g in range(3):
                    pe.wait_ge(s_sqT_cp, 3 * i + 3)
                    product(g, EXT[:, g], EX[:, g]).then_inc(s_sq_mm, 1)
                for g in range(3):
                    pe.wait_ge(s_sq_ev, 3 * i + g + 1)
                    turn(3 + g, EX[:, g]).then_inc(s_sqT_mm, 1)

            def in_tile(ldcount, t, p):
                pe.wait_ge((s_tok_ld0, s_tok_ld1)[p], ldcount)
                after(pe, s_tokT_cp, t)
                for c in range(2):
                    last = pe.transpose(ps[:, 0, c * 128:(c + 1) * 128], tok[p][:, c * 128:(c + 1) * 128], ident[:])
                last.then_inc(s_tok_tr, 1)

            def expert(t):
                return pe.value_load(exi[0:1, bass.ds(t, 1)], min_val=0, max_val=E - 1)

            def up(t, p, e):
                pe.wait_ge(s_tokT_cp, t + 1)
                if not (isinstance(t, int) and t < 2):
                    pe.wait_ge(s_up_ev, t - 1)
                for k in range(2):
                    w = w1[:, bass.ds(e, 1), k * HID:(k + 1) * HID].rearrange("p a n -> p (a n)")
                    last = pe.matmul(ps[:, 1 + p, :], tokT[p][:, k, :], w, start=(k == 0), stop=(k == 1))
                last.then_inc(s_up_mm, 1)

            def turn_hid(t, p):
                pe.wait_ge(s_gelu, t + 1)
                after(pe, s_hidT_cp, t)
                for c in range(4):
                    last = pe.transpose(ps[:, 3, c * 128:(c + 1) * 128], hid[p][:, c * 128:(c + 1) * 128], ident[:])
                last.then_inc(s_hid_tr, 1)

            def down(t, p, e, peeled):
                pe.wait_ge(s_hidT_cp, t + 1)
                if not peeled:
                    pe.wait_ge(s_eo_ready, t - 1)
                for k in range(4):
                    w = w2[:, bass.ds(e, 1), k * D:(k + 1) * D].rearrange("p a n -> p (a n)")
                    last = pe.matmul(ps[:, 4 + p, 0:D], hidT[p][:, k, :], w, start=(k == 0), stop=(k == 3))
                last.then_inc(s_down_mm, 1)

            e0, e1_ = expert(0), expert(1)
            in_tile(16, 0, 0)
            in_tile(16, 1, 1)
            pe.wait_ge(s_ld_exp, 16 * (2 * E + 2))
            up(0, 0, e0)
            pe.wait_ge(s_fin_ready, 1)
            product(6, EXT[:, 1], EX[:, 2]).then_inc(s_rmul, 1)
            turn_hid(0, 0)
            in_tile(32, 2, 0)
            up(1, 1, e1_)
            pe.wait_ge(s_rmul_ev, 1)
            product(7, EXT[:, 0], EX[:, 1]).then_inc(s_rmul, 1)
            e2_ = expert(2)
            down(0, 0, e0, True)
            turn_hid(1, 1)
            in_tile(32, 3, 1)
            up(2, 0, e2_)
            down(1, 1, e1_, True)
            with pe.Fori(0, SLOT_TILES // 2 - 2) as i:
                es = [expert(2 * i + (2 + p)) for p in range(3)]
                for p in range(2):
                    t = 2 * i + (2 + p)
                    in_tile(16 * i + 48, t + 2, p)
                    turn_hid(t, p)
                    up(t + 1, 1 - p, es[p + 1])
                    down(t, p, es[p], False)
            t = SLOT_TILES - 2
            ea, eb_ = expert(t), expert(t + 1)
            turn_hid(t, 0)
            up(t + 1, 1, eb_)
            down(t, 0, ea, False)
            turn_hid(t + 1, 1)
            down(t + 1, 1, eb_, False)

            def rotate(j, p, peeled):
                mb = 2 + 3 * p
                pe.wait_ge(s_mix, j + 1)
                if not peeled:
                    pe.wait_ge(s_mT_cp, j)
                for c in range(2):
                    for u, at in ((2, 0), (0, PROWS), (1, PROWS + 128)):
                        n = ROWS[u]
                        last = pe.transpose(ps[:, c, at:at + n], moe[p][0:n, u, c * 128:(c + 1) * 128],
                                            ident[0:n, 0:n])
                last.then_inc(s_m_tr, 1)
                pe.wait_ge(s_mT_cp, j + 1)
                if isinstance(j, int):
                    after(pe, s_mr_ev, j - 1)
                else:
                    pe.wait_ge(s_mr_ev, j - 1)
                for u, at in ((0, PROWS), (1, PROWS + 128), (2, 0)):
                    n = ROWS[u]
                    last = acc(ps[0:n, mb + u, 0:RG], [(moeT[p][:, k, at:at + n], R[:, k, :]) for k in range(2)])
                last.then_inc(s_mr_mm, 1)

            pe.wait_ge(s_r_wide, 1)
            rotate(0, 0, True)
            rotate(1, 1, False)
            with pe.Fori(0, PAIRS // 2 - 1) as i:
                for p in range(2):
                    rotate(2 * i + (2 + p), p, False)

        @block.scalar
        def _(act):
            step = Chain(act, s_act_step)
            act.preload_act_table_set("natural_log_exp_and_others")

            def copy(o, i_):
                return act.activation(o, i_, ACT.Copy)

            def norm_scale(var_ready, rs_ready, a, ch, dst, lo, hi):
                act.wait_ge(var_ready, a + 1)
                ch(act.activation(lnv[:, lo:hi], veps[:, lo:hi], ACT.Ln))
                act.activation(dst[:, lo:hi], lnv[:, lo:hi], ACT.Exp, scale=-0.5).then_inc(rs_ready, 1)

            def x_out(a):
                act.wait_ge(s_x_tr, a + 1)
                dst = xT.rearrange("p c (b n) -> p c b n", b=2)
                copy(dst[:, :, :, 0:NPATCH],
                     ps[:, 6:8, 0:PROWS].rearrange("p c (b n) -> p c b n", b=2))
                copy(dst[:, :, :, NPATCH:NQ],
                     ps[:, 6:8, PROWS:TP].rearrange("p c (b n) -> p c b n", b=2)).then_inc(s_xT_cp, 1)

            def lat_out(a):
                act.wait_ge(s_lat_mm, a + 1)
                copy(lat, ps[:, 6:8, 0:TP]).then_inc(s_lat_cp, 1)

            def q_out(a, p, half, bank):
                act.wait_ge(s_q_mm, 2 * a + half + 1)
                copy(qT[p][:, 2 * half:2 * half + 2, :], ps[:, bank:bank + 2, 0:TP]).then_inc(s_q_cp, 1)

            def k_out(a, p, half, bank):
                act.wait_ge(s_k_mm, 2 * a + half + 1)
                copy(kT[p][:, 2 * half:2 * half + 2, :], ps[:, bank:bank + 2, 0:TP]).then_inc(s_k_cp, 1)

            def v_out(a, p):
                act.wait_ge(s_v_mm, a + 1)
                copy(Vt[p][:, :, 0:HEADS * VW].rearrange("p b (h d) -> p b h d", d=VW)[:, :, :, 0:HD],
                     ps[:, 4, :].rearrange("p (b h d) -> p b h d", b=2, d=HD))
                copy(Vp[p][0:NPATCH, :, 0:HEADS * VW].rearrange("p b (h d) -> p b h d", d=VW)[:, :, :, 0:HD],
                     ps[0:NPATCH, 5, :].rearrange("p (b h d) -> p b h d", b=2, d=HD)).then_inc(s_v_cp, 1)

            def xn_out(c):
                act.wait_ge(s_xn_tr, c + 1)
                copy(xnT, ps[:, 6:8, 0:TP]).then_inc(s_xnT_cp, 1)

            def probs(n, rp):
                act.wait_ge(s_shifted, n + 1)
                act.activation(Pt[rp], Pt[rp], ACT.Exp, scale=0.25)
                act.activation(Pp[rp], Pp[rp], ACT.Exp, scale=0.25).then_inc(s_probs, 1)

            def pt_out(q, gp):
                act.wait_ge(s_p_tr, q + 1)
                copied = copy(PTt[gp], ps[:, 4 + gp, :].rearrange("p (i n) -> p i n", i=4))
                if gp:
                    copied = copy(PTp[gp][:, :, NPATCH:NQ], ps[0:NPATCH, 6 + gp, :].rearrange("p (i n) -> p i n", i=4))
                copied.then_inc(s_pt_txt, 1)

            def y_out(q, gp, p, b, g):
                act.wait_ge(s_pv, q + 1)
                copy(yTs[p][:, g, b * NPATCH:(b + 1) * NPATCH], ps[:, 4 + gp, 0:NPATCH])
                copy(yTs[p][:, g, PROWS + b * 128:PROWS + (b + 1) * 128],
                     ps[:, 4 + gp, NPATCH:NQ]).then_inc(s_yt, 1)

            def horner_out(k, groups, banks):
                for g, bank in zip(groups, banks):
                    act.wait_ge(s_hr_mm, 3 * (TERMS - 1 - k) + g + 1)
                    act.activation(EX[:, g], ps[:, bank, :].rearrange("p (k n) -> p k n", k=2), ACT.Copy,
                                   scale=1.0 / k).then_inc(s_hr_ev, 1)

            act.wait_ge(s_ones_set, 1)
            def embed_out(j):
                act.wait_ge(s_emb_mm, j + 1)
                copy(h_all[0:PROWS, 3 * j + 2, :], ps[0:PROWS, j % 4, 0:D]).then_inc(s_emb_ev, 1)

            embed_out(0)
            embed_out(1)
            norm_scale(s_ln1_var, s_ln1_rs, 0, step, rstd1, 0, 3)
            embed_out(2)
            x_out(0)
            embed_out(3)
            lat_out(0)
            embed_out(4)
            q_out(0, 0, 0, 4)
            q_out(0, 0, 1, 6)
            embed_out(5)
            k_out(0, 0, 0, 4)
            embed_out(6)
            embed_out(7)
            norm_scale(s_ln1_var, s_ln1_rs, 1, step, rstd1, 3, TILES)

            def round_(j, k, par, first, last):
                n, a, c, q = 4 * j + k, j + 1, j - 1, 8 * j + 2 * k - 2
                no_prev = first and k == 0
                prev_par = par if k else 1 - par
                pb, ph = (k - 1) % 2, ((k - 1) % 4) // 2
                if k == 0:
                    k_out(j, par, 1, 4)
                if k == 3 and not last and not first:
                    q_out(a, 1 - par, 1, 4)
                if not no_prev:
                    pt_out(q, 0)
                    pt_out(q + 1, 1)
                    y_out(q, 0, prev_par, pb, 2 * ph)
                    y_out(q + 1, 1, prev_par, pb, 2 * ph + 1)
                if k == 2 and not first:
                    norm_scale(s_ln2_var, s_ln2_rs, c, step, rstd, 0, 6)
                if k == 0:
                    if not last:
                        x_out(a)
                    v_out(j, par)
                    if last:
                        horner_out(5, (0,), (6,))
                if k == 1 and last:
                    horner_out(5, (1, 2), (7, 6))
                if k == 2 and last:
                    horner_out(4, (0, 1), (6, 7))
                if k == 1 and not last:
                    lat_out(a)
                if k == 2 and not last:
                    q_out(a, 1 - par, 0, 6)
                if k == 3:
                    if not first:
                        xn_out(c)
                    if first:
                        q_out(a, 1 - par, 1, 4)
                    if last:
                        horner_out(4, (2,), (5,))
                probs(n, k % 2)

            def pair(j, par, first, last):
                step.loop(2 if first else j + 1)
                for k in range(4):
                    round_(j, k, par, first, last)
                assert step.n == (0 if first else 1)

            pair_loop(act, pair)
            n = 4 * PAIRS
            q = 2 * n - 2
            for gp in range(2):
                pt_out(q + gp, gp)
            for gp in range(2):
                y_out(q + gp, gp, (PAIRS - 1) % 2, 1, 2 + gp)
            c = PAIRS - 1
            horner_out(3, (0, 1), (0, 1))
            norm_scale(s_ln2_var, s_ln2_rs, c, step, rstd, 0, 6)
            horner_out(3, (2,), (2,))
            horner_out(2, range(3), range(3))
            xn_out(c)
            horner_out(1, range(3), range(3))

            act.wait_ge(s_gap_ready, 1)
            act.activation(wt2[:], m2[:], ACT.Exp).then_inc(s_gates, 1)

            for g in range(3):
                act.wait_ge(s_sqT_mm, g + 1)
                copy(EXT[:, g], ps[:, 3 + g, :].rearrange("p (k n) -> p k n", k=2)).then_inc(s_sqT_cp, 1)
            squarings = act.value_load(expo[0:1, 1:2], min_val=1, max_val=126)
            with act.Fori(0, squarings) as i:
                for g in range(3):
                    act.wait_ge(s_sqT_mm, 3 * i + (g + 4))
                    copy(EXT[:, g], ps[:, 3 + g, :].rearrange("p (k n) -> p k n", k=2)).then_inc(s_sqT_cp, 1)

            act.wait_ge(s_ag_ev, PAIRS + 1)

            def abel(t):
                return act.activation(pre_all[:, bass.ds(t, 1), 0:D], pre_all[:, bass.ds(t, 1), 0:D], ACT.Gelu)

            def tokT_out(t, p, peeled):
                act.wait_ge(s_tok_tr, t + 1)
                if not peeled:
                    act.wait_ge(s_up_mm, t - 1)
                copy(tokT[p], ps[:, 0, 0:D].rearrange("p (c n) -> p c n", c=2)).then_inc(s_tokT_cp, 1)

            def gelu(t, p, peeled):
                act.wait_ge(s_up_ev, t + 1)
                if not peeled:
                    act.wait_ge(s_hid_tr, t - 1)
                act.activation(hid[p], pre[p], ACT.Gelu).then_inc(s_gelu, 1)

            def hidT_out(t, p, peeled):
                act.wait_ge(s_hid_tr, t + 1)
                if not peeled:
                    act.wait_ge(s_down_mm, t - 1)
                copy(hidT[p], ps[:, 3, :].rearrange("p (c n) -> p c n", c=4)).then_inc(s_hidT_cp, 1)

            tokT_out(0, 0, True)
            tokT_out(1, 1, True)
            gelu(0, 0, True)
            hidT_out(0, 0, True)
            tokT_out(2, 0, False)
            gelu(1, 1, True)
            hidT_out(1, 1, True)
            tokT_out(3, 1, False)
            gelu(2, 0, False)
            with act.Fori(0, SLOT_TILES // 2 - 2) as i:
                for p in range(2):
                    t = 2 * i + (2 + p)
                    hidT_out(t, p, False)
                    tokT_out(t + 2, p, False)
                    gelu(t + 1, 1 - p, False)
                abel(i)
            t = SLOT_TILES - 2
            hidT_out(t, 0, False)
            gelu(t + 1, 1, False)
            hidT_out(t + 1, 1, False)
            act.activation(pre_all[:, SLOT_TILES // 2 - 2:TILES, 0:D], pre_all[:, SLOT_TILES // 2 - 2:TILES, 0:D],
                           ACT.Gelu).then_inc(s_abel_done, 1)

            act.preload_act_table_set("natural_log_exp_and_others")
            def turned(j, p):
                act.wait_ge(s_m_tr, j + 1)
                copy(moeT[p], ps[:, 0:2, 0:TP]).then_inc(s_mT_cp, 1)

            def gate(j, p):
                act.wait_ge(s_z_ready, j + 1)
                act.activation(zg[:, 3 * p:3 * p + 3], zg[:, 3 * p:3 * p + 3], ACT.Exp, scale=-1.0).then_inc(s_z_exp, 1)

            def weighted(j, p):
                for u in range(3):
                    n = ROWS[u]
                    last = act.activation(moe[p][0:n, u, :], tile3(G[0], j, u), ACT.Copy,
                                          scale=wt1[0:n, bass.ds(3 * j + u, 1)])
                last.then_inc(s_weighted, 1)

            act.wait_ge(s_weights_ready, 1)
            act.wait_ge(s_back0, 96)
            weighted(0, 0)
            act.wait_ge(s_back1, 96)
            weighted(1, 1)
            turned(0, 0)
            with act.Fori(0, PAIRS // 2 - 1) as i:
                for p in range(2):
                    j = 2 * i + p
                    turned(j + 1, 1 - p)
                    gate(j, p)
                    act.wait_ge((s_back0, s_back1)[p], 96 * i + 192)
                    weighted(j + 2, p)
            turned(PAIRS - 1, 1)
            gate(PAIRS - 2, 0)
            gate(PAIRS - 1, 1)

        @block.vector
        def _(dve):
            step = Chain(dve, s_dve_step)
            for p in range(2):
                dve.memset(Vt[p], 1.0)
                dve.memset(Vp[p], 1.0)
            dve.memset(ones[:], 1.0)
            dve.memset(mv[:], 1.0)
            dve.memset(mv1[:], 1.0)
            dve.memset(ysum[:], 0.0)
            dve.memset(xw, 0.0)
            dve.memset(x3w, 0.0)
            dve.memset(xnw, 0.0).then_inc(s_ones_set, 1)
            dve.memset(pre_all[:], 0.0).then_inc(s_ag_ev, 1)
            dve.memset(x2w, 0.0).then_inc(s_h_res, 1)
            dve.wait_ge(s_prep_mm, 1)
            dve.tensor_copy(p_g, ps[:, 4, 0:128]).then_inc(s_prep_cp, 1)
            dve.wait_ge(s_prep_mm, 2)
            dve.tensor_copy(ve, ps[:, 5, 0:D]).then_inc(s_prep_cp, 1)
            dve.wait_ge(s_ones_set, 1)

            def statistics(src, out_, tiles, var, eps_var):
                for t0 in tiles:
                    for u in range(3):
                        last = dve.bn_stats(stats[0:ROWS[u], u, :], src(t0 + u))
                    step(last)
                    dve.memset(carry[:, 1:2], 0.0)
                    for u in range(3):
                        last = dve.bn_aggr(out_[0:ROWS[u], t0 + u, :], stats[0:ROWS[u], u, :])
                    step(last)
                return dve.tensor_scalar(eps_var, var, EPS, None, ALU.add)

            def refine(rs_ready, a, y, lo, hi):
                dve.wait_ge(rs_ready, a + 1)
                step(dve.scalar_tensor_tensor(out=nt1[:, lo:hi], in0=y[:, lo:hi], scalar=-0.5, in1=y[:, lo:hi],
                                              op0=ALU.mult, op1=ALU.mult))
                step(dve.tensor_tensor(nt2[:, lo:hi], nt1[:, lo:hi], veps[:, lo:hi], ALU.mult))
                step(dve.scalar_tensor_tensor(out=y[:, lo:hi], in0=nt2[:, lo:hi], scalar=1.5, in1=y[:, lo:hi],
                                              op0=ALU.add, op1=ALU.mult))

            def first_norm(a):
                for u in range(3):
                    n = ROWS[u]
                    t = bass.ds(3 * a + u, 1)
                    last = dve.tensor_scalar(xw[0:n, u, :], tile3(h_all, a, u),
                                             mv1[0:n, t, 0:1].rearrange("p a b -> p (a b)"), rstd1[0:n, t],
                                             ALU.subtract, ALU.mult)
                last.then_inc(s_x_ready, 1)

            def k_out(a, p, half):
                dve.wait_ge(s_k_mm, 2 * a + half + 1)
                dve.tensor_copy(kT[p][:, 2 * half:2 * half + 2, :], ps[:, 4:6, 0:TP]).then_inc(s_k_cp, 1)

            def shift(n, rp):
                dve.wait_ge(s_scores, n + 1)
                st = ps[:, 0:4, 0:2 * NQ].rearrange("p i (g n) -> p i g n", g=2)
                sp_ = ps[0:NPATCH, 0:4, 2 * NQ:2 * NQ + 2 * NPATCH].rearrange("p i (g n) -> p i g n", g=2)
                dve.tensor_reduce(mx[:], st, AX, ALU.max)
                step(dve.tensor_reduce(mxp[:], sp_, AX, ALU.max))
                dve.tensor_tensor(Pt[rp], st, mx[:].unsqueeze(3).to_broadcast([128, 4, 2, NQ]), ALU.subtract)
                dve.tensor_tensor(Pp[rp], sp_, mxp[:].unsqueeze(3).to_broadcast([NPATCH, 4, 2, NPATCH]),
                                  ALU.subtract).then_inc(s_shifted, 1)

            def pt_out(q, gp):
                dve.wait_ge(s_p_tr, q + 1)
                if gp == 0:
                    dve.tensor_copy(PTp[gp][:, :, NPATCH:NQ],
                                    ps[0:NPATCH, 6 + gp, :].rearrange("p (i n) -> p i n", i=4))
                dve.tensor_copy(PTp[gp].rearrange("p (b i) n -> p b i n", b=2)[:, :, :, 0:NPATCH],
                                ps[0:NPATCH, 2 * gp:2 * gp + 2, SPARE:SPARE + 2 * NPATCH].rearrange(
                                    "p b (i n) -> p b i n", i=2)).then_inc(s_pt_patch, 1)

            def y_over_sum(c, at, y, n, u0, u1):
                dve.wait_ge(s_y_tr, 2 * c + at + 1)
                w = u1 - u0
                step(dve.reciprocal(rec[0:n, u0:u1, :], y[:, :, :, HD]))
                o = ysum[0:n, u0:u1, :].rearrange("p u (h d) -> p u h d", d=HD)
                dve.tensor_tensor(o, y[:, :, :, 0:HD], rec[0:n, u0:u1, :].unsqueeze(3).to_broadcast([n, w, HEADS, HD]),
                                  ALU.mult).then_inc(s_y_ev, 1)

            def text_rows(c):
                y_over_sum(c, 0, ps[:, 4:6, :].rearrange("p u (h d) -> p u h d", d=32), 128, 0, 2)

            def patch_rows(c, bank):
                y_over_sum(c, 1, ps[0:PROWS, bank:bank + 1, :].rearrange("p u (h d) -> p u h d", d=32), PROWS, 2, 3)

            def add_attention(c):
                dve.wait_ge(s_y_ev, 2 * c + 2)
                dve.tensor_tensor(texts(h_all, c), texts(h_all, c), ysum[:, 0:2, :], ALU.add)
                step(dve.tensor_tensor(tile3(h_all, c, 2), tile3(h_all, c, 2), ysum[0:PROWS, 2, :], ALU.add))
                dve.memset(carry[:, 0:1], 0.0)
                step(statistics(lambda u: tile3(h_all, c, u), mv, (0,), mv[:, :, 1], veps[:, 0:3]))
                dve.scalar_tensor_tensor(out=veps[:, 3:6], in0=veps[:, 0:3], scalar=EPS, in1=mv[:, :, 1],
                                         op0=ALU.mult, op1=ALU.add).then_inc(s_ln2_var, 1)

            def both_norms(c):
                refine(s_ln2_rs, c, rstd, 0, 6)
                dve.wait_ge(s_h_res, c + 1)
                for u in range(3):
                    n = ROWS[u]
                    for x, r in ((x3w, 3 + u), (x2w, u)):
                        last = dve.tensor_scalar(x[0:n, u, :], tile3(h_all, c, u), mv[0:n, u, 0:1], rstd[0:n, r:r + 1],
                                                 ALU.subtract, ALU.mult)
                last.then_inc(s_x2_ready, 1)

            def ag_out(c):
                dve.wait_ge(s_ag_mm, c + 1)
                for u, bank in ((0, 6), (1, 7), (2, 4)):
                    n = ROWS[u]
                    last = dve.tensor_tensor(tile3(pre_all, c, u), ps[0:n, bank, 0:D + E], agb[0:n, :], ALU.add)
                last.then_inc(s_ag_ev, 1)

            first_rows = lambda t: h_all[0:ROWS[t % 3], t, :]
            dve.wait_ge(s_gath0, 32)
            dve.wait_ge(s_emb_ev, 1)
            statistics(first_rows, mv1, (0,), mv1[:, 0:3, 1], veps[:, 0:3]).then_inc(s_ln1_var, 1)
            dve.wait_ge(s_prep_mm, 3)
            dve.tensor_copy(ket, ps[:, 6, :]).then_inc(s_prep_cp, 1)
            refine(s_ln1_rs, 0, rstd1, 0, 3)
            first_norm(0)
            dve.wait_ge(s_gath, 16 * (NB - 2))
            for j in range(1, PAIRS):
                dve.wait_ge(s_emb_ev, j + 1)
                last = statistics(first_rows, mv1, (3 * j,), mv1[:, 3 * j:3 * j + 3, 1], veps[:, 3 * j:3 * j + 3])
                if j < PAIRS - 1:
                    step(last)
                else:
                    last.then_inc(s_ln1_var, 1)
            refine(s_ln1_rs, 1, rstd1, 3, TILES)

            def generators_norm():
                dve.wait_ge(s_ld_gens, 32)
                step(dve.tensor_reduce(rows[:, 0:6].rearrange("p (g k) -> p g k", g=3), X, AX, ALU.add,
                                       apply_absolute_value=True))
                dve.tensor_reduce(rows[:, 6:7], rows[:, 0:6], AX, ALU.max).then_inc(s_norm_part, 1)

            fl = lambda t: t.rearrange("p g k n -> p (g k n)")

            def generators_scale():
                dve.wait_ge(s_norm_all, 1)
                step(dve.tensor_scalar(expo[:, 0:1], rows[:, 7:8].bitcast(I32), 23, None, ALU.logical_shift_right))
                step(dve.tensor_scalar(expo[:, 1:2], expo[:, 0:1], -124, 1, ALU.add, ALU.max))
                step(dve.tensor_scalar(expo[:, 2:3], expo[:, 1:2], -1, 127, ALU.mult, ALU.add))
                step(dve.tensor_scalar(rows[:, 6:7].bitcast(I32), expo[:, 2:3], 23, None, ALU.logical_shift_left))
                step(dve.tensor_scalar(fl(XT), fl(XT), rows[:, 6:7], None, ALU.mult))

            def first_term():
                step(dve.tensor_scalar(fl(X), fl(X), rows[:, 6:7], None, ALU.mult))
                step(dve.tensor_scalar(fl(EX), fl(X), 1.0 / TERMS, None, ALU.mult))
                for k in range(2):
                    cols = slice(k * 128, (k + 1) * 128)
                    for g in range(3):
                        last = dve.tensor_tensor(EX[:, g, k, cols], EX[:, g, k, cols], ident[:], ALU.add)
                last.then_inc(s_x_scaled, 1)

            def round_(j, k, par, first, last):
                n, a, c, q = 4 * j + k, j + 1, j - 1, 8 * j + 2 * k - 2
                no_prev = first and k == 0
                if k == 0 and not last:
                    dve.wait_ge(s_x_tr, a)
                    first_norm(a)
                if k == 1 and not first:
                    text_rows(c)
                if not no_prev:
                    pt_out(q, 0)
                    pt_out(q + 1, 1)
                shift(n, k % 2)
                if k == 1 and not first:
                    patch_rows(c, 4)
                    add_attention(c)
                if k == 2:
                    if not last:
                        k_out(a, 1 - par, 0)
                    if not first:
                        both_norms(c)
                if k == 3 and not first:
                    ag_out(c)
                if first:
                    if k == 1:
                        generators_norm()
                    if k == 2:
                        generators_scale()
                    if k == 3:
                        first_term()

            C_STEPS = 2 + 1 + 3 + 3
            before = [step.n]

            def pair(j, par, first, last):
                step.loop(before[0] if first else (C_STEPS + 4) * j + (before[0] - C_STEPS - 4))
                for k in range(4):
                    round_(j, k, par, first, last)
                if first:
                    before[0] += step.n
                else:
                    assert step.n == C_STEPS + 4, step.n

            pair_loop(dve, pair)
            n = 4 * PAIRS
            q = 2 * n - 2
            for gp in range(2):
                pt_out(q + gp, gp)
            c = PAIRS - 1
            text_rows(c)
            patch_rows(c, 6)
            add_attention(c)
            both_norms(c)
            ag_out(c)
            dve.wait_ge(s_ag_ev, PAIRS + 1)

            dve.wait_ge(s_ld_route, 64)
            dve.wait_ge(s_ag_ev, PAIRS + 1)
            logits = pre_all[:, :, D:D + E]
            def bt(x):
                return x[:].unsqueeze(2).to_broadcast(TE)
            def be(x):
                return x[:].unsqueeze(1).to_broadcast(TE)

            def first_best(src, m, e, oh):
                step(dve.tensor_reduce(m[:], src, AX, ALU.max))
                step(dve.tensor_tensor(r2, src, bt(m), ALU.is_equal))
                step(dve.tensor_tensor(r2, r2, be(em8), ALU.mult))
                step(dve.tensor_reduce(e[:], r2, AX, ALU.min))
                step(dve.tensor_tensor(oh[:], bt(e), be(em8), ALU.is_equal))

            first_best(logits, m1, e1, oh1)
            step(dve.scalar_tensor_tensor(out=r1, in0=oh1[:], scalar=-3.0e38, in1=logits,
                                          op0=ALU.mult, op1=ALU.add))
            first_best(r1, m2, e2, oh2)
            step(dve.tensor_tensor(msum[:], oh1[:], oh2[:], ALU.add))
            dve.tensor_tensor(msum[:], msum[:], bt(valid), ALU.mult).then_inc(s_rt_m, 1)
            dve.tensor_tensor(m2[:], m2[:], m1[:], ALU.subtract).then_inc(s_gap_ready, 1)
            dve.wait_ge(s_rt_mm, 1)
            dve.wait_ge(s_rt_m, 1)
            ps7 = ps[:, 7, 0:TILES * E].rearrange("p (t e) -> p t e", e=E)
            ps6 = ps[:, 6, 0:TILES * E].rearrange("p (t e) -> p t e", e=E)
            step(dve.tensor_copy(r1, ps7))
            src, dst = r1, r2
            sh = 1
            while sh < TILES:
                dve.tensor_copy(dst[:, 0:sh, :], src[:, 0:sh, :])
                step(dve.tensor_tensor(dst[:, sh:, :], src[:, sh:, :], src[:, 0:TILES - sh, :], ALU.add))
                src, dst = dst, src
                sh *= 2
            step(dve.tensor_copy(cnti[:], src[:, TILES - 1, :]))
            step(dve.tensor_scalar(cnti[:], cnti[:], 127, None, ALU.add))
            step(dve.tensor_scalar(cnti[:], cnti[:], 7, 7, ALU.arith_shift_right, ALU.logical_shift_left))
            step(dve.tensor_copy(cnt[:], cnti[:]))
            step(dve.tensor_tensor_scan(endb[:], ones[:, 0:E], cnt[:], 0.0, ALU.mult, ALU.add))
            step(dve.tensor_tensor(base[:], endb[:], cnt[:], ALU.subtract))
            step(dve.tensor_tensor(src[:], src[:], ps7, ALU.subtract))
            step(dve.tensor_tensor(src[:], src[:], ps6, ALU.add))
            step(dve.tensor_tensor(src[:], src[:], be(base), ALU.add))
            for k, oh in ((0, oh1), (1, oh2)):
                step(dve.tensor_tensor(dst[:], src[:], oh[:], ALU.mult))
                step(dve.tensor_reduce((e1, e2)[k][:], dst[:], AX, ALU.add))
                dve.tensor_copy(slots[k][:], (e1, e2)[k][:]).then_inc(s_slots_ready, 1)
            CE = [128, SLOT_TILES, E - 1]
            step(dve.tensor_tensor(cmp, slot0[:].unsqueeze(2).to_broadcast(CE),
                                   endb[:, 0:E - 1].unsqueeze(1).to_broadcast(CE), ALU.is_ge))
            step(dve.tensor_reduce(exf[:], cmp, AX, ALU.add))
            dve.tensor_copy(exi[:], exf[:]).then_inc(s_experts_ready, 1)
            squarings = dve.value_load(expo[0:1, 1:2], min_val=1, max_val=126)
            dve.wait_ge(s_hr_ev, 3 * (TERMS - 1))
            with dve.Fori(0, squarings) as i:
                for g in range(3):
                    dve.wait_ge(s_sq_mm, 3 * i + g + 1)
                    dve.wait_ge(s_sqT_mm, 3 * i + 3)
                    dve.scalar_tensor_tensor(out=EX[:, g], in0=EX[:, g], scalar=2.0,
                                             in1=ps[:, g, :].rearrange("p (k n) -> p k n", k=2),
                                             op0=ALU.mult, op1=ALU.add).then_inc(s_sq_ev, 1)
                dve.wait_ge(s_sq_ev, 3 * i + 3)
            dve.wait_ge(s_sqT_cp, 3 * squarings + 3)
            for m in (EX[:, 2], EXT[:, 1], EXT[:, 0]):
                for k in range(2):
                    cols = slice(k * 128, (k + 1) * 128)
                    last = dve.tensor_tensor(m[:, k, cols], m[:, k, cols], ident[:], ALU.add)
            last.then_inc(s_fin_ready, 1)

            def up_out(t, p, peeled):
                e = dve.value_load(exi[0:1, bass.ds(t, 1)], min_val=0, max_val=E - 1)
                dve.wait_ge(s_up_mm, t + 1)
                if not peeled:
                    dve.wait_ge(s_gelu, t - 1)
                dve.tensor_tensor(pre[p], ps[:, 1 + p, :], eb1[:, bass.ds(e, 1), :].rearrange("p a n -> p (a n)"),
                                  ALU.add).then_inc(s_up_ev, 1)

            def down_out(t, p, stored):
                e = dve.value_load(exi[0:1, bass.ds(t, 1)], min_val=0, max_val=E - 1)
                dve.wait_ge(s_down_mm, t + 1)
                if stored is not None:
                    dve.wait_ge((s_eo_st0, s_eo_st1)[p], stored)
                dve.tensor_tensor(eo[p], ps[:, 4 + p, 0:D], eb2[:, bass.ds(e, 1), :].rearrange("p a n -> p (a n)"),
                                  ALU.add).then_inc(s_eo_ready, 1)

            dve.wait_ge(s_ld_exp, 16 * (2 * E + 2))
            up_out(0, 0, True)
            dve.wait_ge(s_rmul, 1)
            dve.tensor_copy(EX[:, 1], ps[:, 6, :].rearrange("p (k n) -> p k n", k=2)).then_inc(s_rmul_ev, 1)
            up_out(1, 1, True)
            dve.wait_ge(s_rmul, 2)
            dve.tensor_copy(R[:, :, 0:D], ps[:, 7, :].rearrange("p (k n) -> p k n", k=2)).then_inc(s_fin_ready, 1)
            down_out(0, 0, None)
            up_out(2, 0, False)
            down_out(1, 1, None)
            with dve.Fori(0, SLOT_TILES // 2 - 2) as i:
                for p in range(2):
                    t = 2 * i + (2 + p)
                    up_out(t + 1, 1 - p, False)
                    down_out(t, p, 16 * i + 16)
            t = SLOT_TILES - 2
            up_out(t + 1, 1, False)
            down_out(t, 0, 16 * (t // 2))
            down_out(t + 1, 1, 16 * (t // 2))

            sel = lambda x, j, u: x[0:ROWS[u], bass.ds(3 * j + u, 1)]

            def mix(j, p):
                dve.wait_ge(s_weighted, j + 1)
                for u in range(3):
                    n = ROWS[u]
                    last = dve.scalar_tensor_tensor(out=moe[p][0:n, u, :], in0=tile3(G[1], j, u), scalar=sel(wt2, j, u),
                                                    in1=moe[p][0:n, u, :], op0=ALU.mult, op1=ALU.add)
                last.then_inc(s_mix, 1)

            def gate(j, p):
                mb = 2 + 3 * p
                z3 = zg[:, 3 * p:3 * p + 3]
                t3 = bass.ds(3 * j, 2)
                dve.wait_ge(s_mr_mm, j + 1)
                dve.tensor_tensor(zg[:, 3 * p:3 * p + 2], ps[:, mb:mb + 2, D], zab[:, t3], ALU.add)
                dve.tensor_tensor(zg[0:PROWS, 3 * p + 2:3 * p + 3], ps[0:PROWS, mb + 2, D:D + 1],
                                  zab[0:PROWS, bass.ds(3 * j + 2, 1)], ALU.add).then_inc(s_z_ready, 1)
                ab = pre_all[:, t3, 0:D]
                ab2 = pre_all[0:PROWS, bass.ds(3 * j + 2, 1), 0:D].rearrange("p a d -> p (a d)")
                dve.tensor_tensor(mo[p][:, 0:2, :], ps[:, mb:mb + 2, 0:D], ab, ALU.subtract)
                dve.tensor_tensor(mo[p][0:PROWS, 2, :], ps[0:PROWS, mb + 2, 0:D], ab2, ALU.subtract).then_inc(s_mr_ev, 1)
                dve.tensor_tensor(res[p][:, 0:2, :], texts(h_all, j), ab, ALU.add)
                step(dve.tensor_tensor(res[p][0:PROWS, 2, :], tile3(h_all, j, 2), ab2, ALU.add))

            def finish(j, p):
                z3 = zg[:, 3 * p:3 * p + 3]
                dve.wait_ge(s_z_exp, j + 1)
                step(dve.tensor_scalar(z3, z3, 1.0, None, ALU.add))
                step(dve.reciprocal(z3, z3))
                dve.wait_ge(s_mr_ev, j + 1)
                for u in range(3):
                    n = ROWS[u]
                    last = dve.scalar_tensor_tensor(out=res[p][0:n, u, :], in0=mo[p][0:n, u, :],
                                                    scalar=zg[0:n, 3 * p + u:3 * p + u + 1], in1=res[p][0:n, u, :],
                                                    op0=ALU.mult, op1=ALU.add)
                last.then_inc(s_res_ready, 1)

            dve.wait_ge(s_gates, 1)
            step(dve.tensor_scalar(m1[:], wt2[:], 1.0, None, ALU.add))
            step(dve.reciprocal(wt1[:], m1[:]))
            dve.tensor_tensor(wt2[:], wt2[:], wt1[:], ALU.mult).then_inc(s_weights_ready, 1)
            dve.wait_ge(s_weights_ready, 1)

            MIX_STEPS, OUT_STEPS = 0, 3
            dve.wait_ge(s_fin_ready, 2)
            for k in range(2):
                step(dve.tensor_tensor_reduce(ysum[:, 0, :], R[:, k, 0:D], gcw[:, D:2 * D], 1.0, 0.0, ALU.mult, ALU.add,
                                              zmo[:, k:k + 1]))
            dve.tensor_copy(R[:, :, D], zmo[:, 0:2]).then_inc(s_r_wide, 1)
            dve.wait_ge(s_abel_done, 1)
            for t in range(TILES):
                last = dve.tensor_tensor_reduce(ysum[:, t % 3, :], pre_all[:, t, 0:D], gcw[:, 0:D], 1.0, 0.0, ALU.mult,
                                                ALU.add, zab[:, t:t + 1])
                if t % 3 == 2:
                    step(last)
            step(dve.tensor_scalar(zab[:], zab[:], gcb[:, 0:1], None, ALU.add))
            dve.memset(zg[:], 0.0)
            dve.wait_ge(s_back0, 96)
            mixbase = step.base + step.n
            step.loop(mixbase)
            mix(0, 0)
            for j in range(2):
                dve.wait_ge(s_back1 if j == 0 else s_back0, 96 if j == 0 else 192)
                if j == 1:
                    dve.wait_ge(s_m_tr, 1)
                mix(j + 1, 1 - j)
                gate(j, j)
                finish(j, j)
            with dve.Fori(0, PAIRS // 2 - 2) as i:
                step.loop((MIX_STEPS + OUT_STEPS) * 2 * i + (mixbase + 3 * MIX_STEPS + 2 * OUT_STEPS))
                for p in range(2):
                    j = 2 * i + (2 + p)
                    dve.wait_ge((s_back1, s_back0)[p], 96 * i + 96 * (2 + p))
                    dve.wait_ge(s_m_tr, j)
                    mix(j + 1, 1 - p)
                    dve.wait_ge((s_out_st0, s_out_st1)[p], 64 * i + 64)
                    gate(j, p)
                    finish(j, p)
            step.loop(mixbase + (PAIRS - 1) * MIX_STEPS + (PAIRS - 2) * OUT_STEPS)
            j = PAIRS - 2
            dve.wait_ge(s_back1, 96 * PAIRS // 2)
            dve.wait_ge(s_m_tr, j)
            mix(j + 1, 1)
            for p in range(2):
                dve.wait_ge((s_out_st0, s_out_st1)[p], 64 * (PAIRS // 2 - 1))
                gate(j + p, p)
                finish(j + p, p)


def kernel(**inputs):
    import numpy as np
    import ml_dtypes
    import concourse.bacc as bacc
    from concourse.bass_utils import run_bass_kernel_spmd as run

    f = {k: np.asarray(v) for k, v in inputs.items()}
    c = np.ascontiguousarray

    def head_columns(w):
        o = np.zeros((w.shape[0], HEADS, 32), w.dtype)
        o[:, :, 0:HD] = w.reshape(w.shape[0], HEADS, HD)
        return o.reshape(w.shape[0], HEADS * 32)

    pat = f["x"].reshape(NB, 3, 6, 16, 6, 16).transpose(0, 1, 3, 5, 2, 4).reshape(NB, NPATCH, 768)
    pat = pat.transpose(2, 0, 1).reshape(768, NB * NPATCH)
    order = np.arange(128)
    mask = np.zeros((128, 2 * NQ + 2 * NPATCH), np.float32)
    low = np.float32(-1e30)
    later = order[None, :] > order[:, None]
    for g in range(2):
        mask[:, g * NQ + NPATCH:(g + 1) * NQ][later] = low
        mask[0:NPATCH, 2 * NQ + g * NPATCH:2 * NQ + (g + 1) * NPATCH][later[0:NPATCH, 0:NPATCH]] = low
    arrays = {
        "patches": c(pat), "ids": c(f["x_txt"].T), "wtok": f["L0_tok_W"], "txt_w": f["L0_txt_w"],
        "uq": f["L0_attn_W_uq"], "uk": f["L0_attn_W_uk"], "uv": f["L0_attn_W_uv"], "o_t": c(f["L0_attn_W_o"].T),
        "dq_t": c(f["L0_attn_W_dq"].T), "dkv_t": c(f["L0_attn_W_dkv"].T),
        "dq_pad": head_columns(f["L0_attn_W_dq"]), "uq_pad": head_columns(f["L0_attn_W_uq"].T),
        "ag": np.concatenate([f["L0_ffn_abel_w"], f["L0_ffn_moe_gate_w"]], axis=1),
        "ag_b": np.concatenate([f["L0_ffn_abel_b"], f["L0_ffn_moe_gate_b"]]),
        "gamma": f["L0_ffn_ln_gamma"], "beta": f["L0_ffn_ln_beta"],
        "gc_w": c(f["L0_ffn_gc_w"].reshape(-1)), "gc_b": f["L0_ffn_gc_b"],
        "ew1": f["L0_ffn_ew1"], "ew2": f["L0_ffn_ew2"], "eb1": f["L0_ffn_eb1"], "eb2": f["L0_ffn_eb2"],
        "gens": f["L0_ffn_gens"], "gens_t": c(f["L0_ffn_gens"].transpose(0, 2, 1)),
        "ident": np.eye(128, dtype=np.float32), "identb": np.eye(128).astype(ml_dtypes.bfloat16),
        "maskb": mask.astype(ml_dtypes.bfloat16),
        "valid": np.stack([(order < ROWS[t % 3]) for t in range(TILES)], 1).astype(np.float32),
        "tri": (order[:, None] < order[None, :]).astype(np.float32),
        "em8": np.tile(np.arange(E, dtype=np.float32) - 8, (128, 1)),
        "slot0": np.tile(128 * np.arange(SLOT_TILES, dtype=np.float32), (128, 1)),
    }
    nc = bacc.Bacc("TRN2", target_bir_lowering=False, num_devices=1)
    ins = {k: nc.dram_tensor("in_" + k, a.shape, mybir.dt.from_np(a.dtype), kind="ExternalInput").ap()
           for k, a in arrays.items()}
    out = nc.dram_tensor("out", (NB, NQ, D), F32, kind="ExternalOutput").ap()
    early_fusion_program(nc, ins, out)
    r = run(nc, [{"in_" + k: a for k, a in arrays.items()}], core_ids=[0])
    return r.results[0]["out"]
```
